# Optimizing a Trainium2 kernel written in Bass

```python
import numpy as np
import jax
import jax.numpy as jnp

def _softmax(x, axis=-1):
    return jax.nn.softmax(x, axis=axis)

def _gelu(x):
    return jax.nn.gelu(x, approximate=True)

def _silu(x):
    return jax.nn.silu(x)

def _sigmoid(x):
    return jax.nn.sigmoid(x)

def _layernorm(x, axis=-1, eps=1e-05):
    m = jnp.mean(x, axis=axis, keepdims=True)
    v = jnp.var(x, axis=axis, keepdims=True)
    return (x - m) / jnp.sqrt(v + eps)

def _scatter_add(tgt, idx, src, axis=0):
    return tgt.at[idx].add(src)

def _segment_sum(src, seg, n):
    return jax.ops.segment_sum(src, seg, n)
kernel_name = 'mk_adaln_d2_jaxref_r4_17a8da'

def setup_inputs(seed: int=0):
    np.random.seed(seed)
    _w = jnp.asarray

    def _L0_attn_setup():
        import jax, jax.numpy as jnp
        import numpy as np
        import math
        B, T, D = (2, 1024, 256)
        H = 16
        HEAD_DIM = D // H
        CHUNK = 64

        def chunked_attention(q, k, v, chunk_size, scale):
            Bq, Hq, Tq, hd = q.shape
            S = k.shape[2]
            nc = Tq // chunk_size
            q_chunks = q.reshape(Bq, Hq, nc, chunk_size, hd).transpose(2, 0, 1, 3, 4)
            starts = jnp.arange(nc, dtype=jnp.int32) * chunk_size
            k_pos = jnp.arange(S)

            def body(carry, xs):
                qc, start = xs
                scores = jnp.einsum('bhqd,bhkd->bhqk', qc, k) * scale
                q_pos = start + jnp.arange(chunk_size)
                causal_mask = k_pos[None, :] > q_pos[:, None]
                scores = jnp.where(causal_mask[None, None], -jnp.inf, scores)
                m = jnp.max(scores, axis=-1, keepdims=True)
                m = jnp.where(jnp.isinf(m), jnp.zeros_like(m), m)
                p = jax.nn.softmax(scores - m, axis=-1)
                oc = jnp.einsum('bhqk,bhkd->bhqd', p, v)
                return (carry, oc)
            _, outs = jax.lax.scan(body, None, (q_chunks, starts))
            return outs.transpose(1, 2, 0, 3, 4).reshape(Bq, Hq, Tq, hd)
        key = jax.random.key(seed)
        ks = jax.random.split(key, 9)
        s = 1.0 / math.sqrt(D)
        return {'x': jax.random.normal(ks[0], (B, T, D), dtype=jnp.float32), 'Wq': jax.random.normal(ks[1], (D, D), dtype=jnp.float32) * s, 'bq': jax.random.normal(ks[2], (D,), dtype=jnp.float32) * 0.01, 'Wk': jax.random.normal(ks[3], (D, D), dtype=jnp.float32) * s, 'bk': jax.random.normal(ks[4], (D,), dtype=jnp.float32) * 0.01, 'Wv': jax.random.normal(ks[5], (D, D), dtype=jnp.float32) * s, 'bv': jax.random.normal(ks[6], (D,), dtype=jnp.float32) * 0.01, 'Wo': jax.random.normal(ks[7], (D, D), dtype=jnp.float32) * s, 'bo': jax.random.normal(ks[8], (D,), dtype=jnp.float32) * 0.01}
    _L0_attn_in = _L0_attn_setup()

    def _L0_ffn_setup():
        import jax, jax.numpy as jnp
        import numpy as np
        B, N, D = (4, 2048, 256)
        HEADS, DH = (8, 64)
        HID = HEADS * DH
        WIN = 128
        NQ, NKV = (256, 512)
        EPS, N_ITERS, FETCH_K = (1.0, 50, 9.0 / 8.0)
        SCALE = DH ** (-0.5)

        def rmsnorm(x, gamma):
            norm = jnp.maximum(jnp.linalg.norm(x, axis=-1, keepdims=True), 1e-12)
            return x / norm * x.shape[-1] ** 0.5 * gamma

        def coor_descent(s, k):
            logk = jnp.log(jnp.asarray(k, s.dtype))

            def body(_, ab):
                a, b = ab
                a = EPS * (logk - jax.nn.logsumexp((s + b) / EPS, axis=-1, keepdims=True))
                b = -jax.nn.relu(s + a)
                return (a, b)
            a, b = jax.lax.fori_loop(0, N_ITERS, body, (jnp.zeros_like(s[..., :1]), -s))
            return jnp.exp((s + a + b) / EPS)

        def route(x, routing_token, num_tokens):
            s = jnp.einsum('bnd,d->bn', x, routing_token)
            k = min(num_tokens * FETCH_K, x.shape[1])
            scores = coor_descent(s, k)
            sel_scores, sel_idx = jax.lax.top_k(scores, num_tokens)
            sel_scores = sel_scores + jax.lax.stop_gradient(1.0 - sel_scores)
            return (sel_scores, sel_idx)

        def light_local_attn(x, gamma, wq, wkv, wo):
            b, n, d = x.shape
            xn = rmsnorm(x, gamma)
            q = xn @ wq
            k, v = jnp.split(xn @ wkv, 2, axis=-1)

            def win(t):
                return t.reshape(b, n // WIN, WIN, HEADS, DH).transpose(0, 1, 3, 2, 4)
            q, k, v = (win(q) * SCALE, win(k), win(v))
            attn = jax.nn.softmax(jnp.einsum('bwhid,bwhjd->bwhij', q, k), axis=-1)
            out = jnp.einsum('bwhij,bwhjd->bwhid', attn, v)
            out = out.transpose(0, 1, 3, 2, 4).reshape(b, n, HID)
            return out @ wo

        def heavy_attn(xq, context, scores_kv, gamma, wq, wkv_t, wo):
            b, nq, d = xq.shape
            nkv = context.shape[1]
            xqn = rmsnorm(xq, gamma)
            ctx = rmsnorm(context, gamma)[:, None]
            q = (xqn @ wq).reshape(b, nq, HEADS, DH).transpose(0, 2, 1, 3) * SCALE
            kvw = wkv_t.reshape(1, HEADS, 2 * DH, d)
            kv = jnp.einsum('rhdi,brni->brhnd', kvw, ctx)
            k, v = jnp.split(kv, 2, axis=-1)
            v = v * scores_kv[:, None, None, :, None]
            k = k.reshape(b, HEADS, nkv, DH)
            v = v.reshape(b, HEADS, nkv, DH)
            attn = jax.nn.softmax(jnp.einsum('bhid,bhjd->bhij', q, k), axis=-1)
            out = jnp.einsum('bhij,bhjd->bhid', attn, v)
            out = out.transpose(0, 2, 1, 3).reshape(b, nq, HID)
            return out @ wo
        key = jax.random.key(seed)
        ks = jax.random.split(key, 10)
        lin = lambda k, shape, fan: jax.random.normal(k, shape, jnp.float32) * fan ** (-0.5)
        return dict(x=jax.random.normal(ks[0], (B, N, D), jnp.float32), gamma_light=jnp.ones((D,), jnp.float32), wq_light=lin(ks[1], (D, HID), D), wkv_light=lin(ks[2], (D, 2 * HID), D), wo_light=lin(ks[3], (HID, D), HID), q_routing_token=jax.random.normal(ks[4], (D,), jnp.float32), kv_routing_token=jax.random.normal(ks[5], (D,), jnp.float32), gamma_heavy=jnp.ones((D,), jnp.float32), wq_heavy=lin(ks[6], (D, HID), D), wkv_heavy=lin(ks[7], (2 * HID, D), D), wo_heavy=lin(ks[8], (HID, D), HID))
    _L0_ffn_in = _L0_ffn_setup()
    _L0_c = _w((lambda *s: np.random.randn(*s).astype(np.float32) * 0.05)(4, 256))
    _L0_wmod = _w((lambda *s: np.random.randn(*s).astype(np.float32) * 0.05)(256, 6 * 256) * 256 ** (-0.5))

    def _L1_attn_setup():
        import jax, jax.numpy as jnp
        import numpy as np
        from jax import lax
        B, S, H = (8, 1024, 256)
        key = jax.random.key(seed)
        ks = jax.random.split(key, 9)
        x = jax.random.normal(ks[0], (B, S, H), dtype=jnp.float32)
        time_decay = jax.random.normal(ks[1], (H,), dtype=jnp.float32) * 0.01
        time_mix_k = jnp.ones((H,), dtype=jnp.float32) * 0.5
        time_mix_v = jnp.ones((H,), dtype=jnp.float32) * 0.5
        time_mix_r = jnp.ones((H,), dtype=jnp.float32) * 0.5
        sc = 1.0 / np.sqrt(H)
        Wk = jax.random.uniform(ks[2], (H, H), jnp.float32, -sc, sc)
        Wv = jax.random.uniform(ks[3], (H, H), jnp.float32, -sc, sc)
        Wr = jax.random.uniform(ks[4], (H, H), jnp.float32, -sc, sc)
        Wo = jax.random.uniform(ks[5], (H, H), jnp.float32, -sc, sc)
        return {'x': x, 'time_decay': time_decay, 'time_mix_k': time_mix_k, 'time_mix_v': time_mix_v, 'time_mix_r': time_mix_r, 'Wk': Wk, 'Wv': Wv, 'Wr': Wr, 'Wo': Wo}
    _L1_attn_in = _L1_attn_setup()

    def _L1_ffn_setup():
        import jax, jax.numpy as jnp
        import numpy as np
        DIM = 256
        DEPTH = 2
        HEADS = 8
        DIM_HEAD = 64
        WINDOW = 128
        INNER = HEADS * DIM_HEAD
        HID = int(DIM * 4 * 2 / 3)
        B, N = (2, 2048)
        QK_SCALE = 8.0

        def shift_token(t):
            t1, t2 = jnp.split(t, 2, axis=-1)
            t2 = jnp.pad(t2, ((0, 0), (1, 0), (0, 0)))[:, :-1]
            return jnp.concatenate([t1, t2], axis=-1)

        def l2norm(t):
            return t / jnp.clip(jnp.linalg.norm(t, axis=-1, keepdims=True), 1e-12)

        def rotate_half(x):
            x1, x2 = jnp.split(x, 2, axis=-1)
            return jnp.concatenate([-x2, x1], axis=-1)

        def rotary_xpos(q, k):
            n = q.shape[-2]
            half_idx = jnp.arange(0, DIM_HEAD, 2, dtype=jnp.float32)
            inv_freq = 1.0 / 10000.0 ** (half_idx / DIM_HEAD)
            t = jnp.arange(n, dtype=jnp.float32)
            freqs = t[:, None] * inv_freq[None, :]
            freqs = jnp.concatenate([freqs, freqs], axis=-1)
            base = (half_idx + 0.4 * DIM_HEAD) / (1.4 * DIM_HEAD)
            power = (t - n // 2) / float(WINDOW // 2)
            scale = base[None, :] ** power[:, None]
            scale = jnp.concatenate([scale, scale], axis=-1)
            cos, sin = (jnp.cos(freqs), jnp.sin(freqs))
            q = q * cos * scale + rotate_half(q) * sin * scale
            k = k * cos / scale + rotate_half(k) * sin / scale
            return (q, k)

        def local_attention(q, k, v):
            b, h, n, d = q.shape
            w = n // WINDOW
            bq = q.reshape(b, h, w, WINDOW, d) * QK_SCALE
            bk = k.reshape(b, h, w, WINDOW, d)
            bv = v.reshape(b, h, w, WINDOW, d)

            def look_around(t):
                p = jnp.pad(t, ((0, 0), (0, 0), (1, 0), (0, 0), (0, 0)))
                return jnp.concatenate([p[:, :, :w], p[:, :, 1:]], axis=3)
            bk, bv = (look_around(bk), look_around(bv))
            bt = jnp.arange(n).reshape(w, WINDOW)
            btp = jnp.pad(bt, ((1, 0), (0, 0)), constant_values=-1)
            btk = jnp.concatenate([btp[:w], btp[1:]], axis=1)
            sim = jnp.einsum('bhwid,bhwjd->bhwij', bq, bk)
            i = bt[:, :, None]
            j = btk[:, None, :]
            mask = (i < j) | (i > j + WINDOW) | (j == -1)
            sim = jnp.where(mask, -jnp.finfo(sim.dtype).max, sim)
            attn = jax.nn.softmax(sim, axis=-1)
            out = jnp.einsum('bhwij,bhwjd->bhwid', attn, bv)
            return out.reshape(b, h, n, d)

        def _layer(x, wqkv, qs, ksc, wo, lg, lb, w1, b1, w2, b2):
            b, n, _ = x.shape
            h = shift_token(x)
            qkv = h @ wqkv
            q, k, v = jnp.split(qkv, 3, axis=-1)
            to_heads = lambda t: t.reshape(b, n, HEADS, DIM_HEAD).transpose(0, 2, 1, 3)
            q, k, v = (to_heads(q), to_heads(k), to_heads(v))
            q = l2norm(q) * qs
            k = l2norm(k) * ksc
            q, k = rotary_xpos(q, k)
            o = local_attention(q, k, v)
            o = o.transpose(0, 2, 1, 3).reshape(b, n, INNER)
            x = x + o @ wo
            h = shift_token(x)
            mu = h.mean(-1, keepdims=True)
            var = h.var(-1, keepdims=True)
            h = (h - mu) / jnp.sqrt(var + 1e-05) * lg + lb
            h = h @ w1 + b1
            a, g = jnp.split(h, 2, axis=-1)
            h = a * jax.nn.gelu(g, approximate=False)
            x = x + h @ w2 + b2
            return x
        key = jax.random.key(seed)
        ks = jax.random.split(key, 6)
        return {'x': jax.random.normal(ks[0], (B, N, DIM), jnp.float32), 'wqkv': jax.random.normal(ks[1], (DEPTH, DIM, 3 * INNER), jnp.float32) * 0.02, 'q_scale': jnp.ones((DEPTH, DIM_HEAD), jnp.float32), 'k_scale': jnp.ones((DEPTH, DIM_HEAD), jnp.float32), 'wo': jax.random.normal(ks[2], (DEPTH, INNER, DIM), jnp.float32) * 0.02, 'ln_g': jnp.ones((DEPTH, DIM), jnp.float32), 'ln_b': jnp.zeros((DEPTH, DIM), jnp.float32), 'w1': jax.random.normal(ks[3], (DEPTH, DIM, 2 * HID), jnp.float32) * 0.02, 'b1': jnp.zeros((DEPTH, 2 * HID), jnp.float32), 'w2': jax.random.normal(ks[4], (DEPTH, HID, DIM), jnp.float32) * 0.02, 'b2': jnp.zeros((DEPTH, DIM), jnp.float32)}
    _L1_ffn_in = _L1_ffn_setup()
    _L1_c = _w((lambda *s: np.random.randn(*s).astype(np.float32) * 0.05)(4, 256))
    _L1_wmod = _w((lambda *s: np.random.randn(*s).astype(np.float32) * 0.05)(256, 6 * 256) * 256 ** (-0.5))
    _d = {'L0_attn_x': _L0_attn_in['x'], 'L0_attn_Wq': _L0_attn_in['Wq'], 'L0_attn_bq': _L0_attn_in['bq'], 'L0_attn_Wk': _L0_attn_in['Wk'], 'L0_attn_bk': _L0_attn_in['bk'], 'L0_attn_Wv': _L0_attn_in['Wv'], 'L0_attn_bv': _L0_attn_in['bv'], 'L0_attn_Wo': _L0_attn_in['Wo'], 'L0_attn_bo': _L0_attn_in['bo'], 'L0_ffn_gamma_light': _L0_ffn_in['gamma_light'], 'L0_ffn_wq_light': _L0_ffn_in['wq_light'], 'L0_ffn_wkv_light': _L0_ffn_in['wkv_light'], 'L0_ffn_wo_light': _L0_ffn_in['wo_light'], 'L0_ffn_q_routing_token': _L0_ffn_in['q_routing_token'], 'L0_ffn_kv_routing_token': _L0_ffn_in['kv_routing_token'], 'L0_ffn_gamma_heavy': _L0_ffn_in['gamma_heavy'], 'L0_ffn_wq_heavy': _L0_ffn_in['wq_heavy'], 'L0_ffn_wkv_heavy': _L0_ffn_in['wkv_heavy'], 'L0_ffn_wo_heavy': _L0_ffn_in['wo_heavy'], 'L0_c': _L0_c, 'L0_wmod': _L0_wmod, 'L1_attn_time_decay': _L1_attn_in['time_decay'], 'L1_attn_time_mix_k': _L1_attn_in['time_mix_k'], 'L1_attn_time_mix_v': _L1_attn_in['time_mix_v'], 'L1_attn_time_mix_r': _L1_attn_in['time_mix_r'], 'L1_attn_Wk': _L1_attn_in['Wk'], 'L1_attn_Wv': _L1_attn_in['Wv'], 'L1_attn_Wr': _L1_attn_in['Wr'], 'L1_attn_Wo': _L1_attn_in['Wo'], 'L1_ffn_wqkv': _L1_ffn_in['wqkv'], 'L1_ffn_q_scale': _L1_ffn_in['q_scale'], 'L1_ffn_k_scale': _L1_ffn_in['k_scale'], 'L1_ffn_wo': _L1_ffn_in['wo'], 'L1_ffn_ln_g': _L1_ffn_in['ln_g'], 'L1_ffn_ln_b': _L1_ffn_in['ln_b'], 'L1_ffn_w1': _L1_ffn_in['w1'], 'L1_ffn_b1': _L1_ffn_in['b1'], 'L1_ffn_w2': _L1_ffn_in['w2'], 'L1_ffn_b2': _L1_ffn_in['b2'], 'L1_c': _L1_c, 'L1_wmod': _L1_wmod}
    _x0 = _d['L0_attn_x']
    _d['L0_attn_x'] = jax.random.normal(jax.random.fold_in(jax.random.key(seed), 1), (4, 1024, 256), dtype=_x0.dtype)
    del _x0
    return _d

def reference(L0_attn_x, L0_attn_Wq, L0_attn_bq, L0_attn_Wk, L0_attn_bk, L0_attn_Wv, L0_attn_bv, L0_attn_Wo, L0_attn_bo, L0_ffn_gamma_light, L0_ffn_wq_light, L0_ffn_wkv_light, L0_ffn_wo_light, L0_ffn_q_routing_token, L0_ffn_kv_routing_token, L0_ffn_gamma_heavy, L0_ffn_wq_heavy, L0_ffn_wkv_heavy, L0_ffn_wo_heavy, L0_c, L0_wmod, L1_attn_time_decay, L1_attn_time_mix_k, L1_attn_time_mix_v, L1_attn_time_mix_r, L1_attn_Wk, L1_attn_Wv, L1_attn_Wr, L1_attn_Wo, L1_ffn_wqkv, L1_ffn_q_scale, L1_ffn_k_scale, L1_ffn_wo, L1_ffn_ln_g, L1_ffn_ln_b, L1_ffn_w1, L1_ffn_b1, L1_ffn_w2, L1_ffn_b2, L1_c, L1_wmod):

    def _L0_attn_ref(x, Wq, bq, Wk, bk, Wv, bv, Wo, bo):
        import jax, jax.numpy as jnp
        import numpy as np
        import math
        B, T, D = (2, 1024, 256)
        H = 16
        HEAD_DIM = D // H
        CHUNK = 64

        def chunked_attention(q, k, v, chunk_size, scale):
            Bq, Hq, Tq, hd = q.shape
            S = k.shape[2]
            nc = Tq // chunk_size
            q_chunks = q.reshape(Bq, Hq, nc, chunk_size, hd).transpose(2, 0, 1, 3, 4)
            starts = jnp.arange(nc, dtype=jnp.int32) * chunk_size
            k_pos = jnp.arange(S)

            def body(carry, xs):
                qc, start = xs
                scores = jnp.einsum('bhqd,bhkd->bhqk', qc, k) * scale
                q_pos = start + jnp.arange(chunk_size)
                causal_mask = k_pos[None, :] > q_pos[:, None]
                scores = jnp.where(causal_mask[None, None], -jnp.inf, scores)
                m = jnp.max(scores, axis=-1, keepdims=True)
                m = jnp.where(jnp.isinf(m), jnp.zeros_like(m), m)
                p = jax.nn.softmax(scores - m, axis=-1)
                oc = jnp.einsum('bhqk,bhkd->bhqd', p, v)
                return (carry, oc)
            _, outs = jax.lax.scan(body, None, (q_chunks, starts))
            return outs.transpose(1, 2, 0, 3, 4).reshape(Bq, Hq, Tq, hd)
        Bx, Tx, Dx = x.shape
        scale = 1.0 / math.sqrt(HEAD_DIM)

        def proj(W, b):
            y = x @ W.T + b
            return y.reshape(Bx, Tx, H, HEAD_DIM).transpose(0, 2, 1, 3)
        q = proj(Wq, bq)
        k = proj(Wk, bk)
        v = proj(Wv, bv)
        out = chunked_attention(q, k, v, CHUNK, scale)
        out = out.transpose(0, 2, 1, 3).reshape(Bx, Tx, Dx)
        return out @ Wo.T + bo

    def _L0_ffn_ref(x, gamma_light, wq_light, wkv_light, wo_light, q_routing_token, kv_routing_token, gamma_heavy, wq_heavy, wkv_heavy, wo_heavy):
        import jax, jax.numpy as jnp
        import numpy as np
        B, N, D = (4, 2048, 256)
        HEADS, DH = (8, 64)
        HID = HEADS * DH
        WIN = 128
        NQ, NKV = (256, 512)
        EPS, N_ITERS, FETCH_K = (1.0, 50, 9.0 / 8.0)
        SCALE = DH ** (-0.5)

        def rmsnorm(x, gamma):
            norm = jnp.maximum(jnp.linalg.norm(x, axis=-1, keepdims=True), 1e-12)
            return x / norm * x.shape[-1] ** 0.5 * gamma

        def coor_descent(s, k):
            logk = jnp.log(jnp.asarray(k, s.dtype))

            def body(_, ab):
                a, b = ab
                a = EPS * (logk - jax.nn.logsumexp((s + b) / EPS, axis=-1, keepdims=True))
                b = -jax.nn.relu(s + a)
                return (a, b)
            a, b = jax.lax.fori_loop(0, N_ITERS, body, (jnp.zeros_like(s[..., :1]), -s))
            return jnp.exp((s + a + b) / EPS)

        def route(x, routing_token, num_tokens):
            s = jnp.einsum('bnd,d->bn', x, routing_token)
            k = min(num_tokens * FETCH_K, x.shape[1])
            scores = coor_descent(s, k)
            sel_scores, sel_idx = jax.lax.top_k(scores, num_tokens)
            sel_scores = sel_scores + jax.lax.stop_gradient(1.0 - sel_scores)
            return (sel_scores, sel_idx)

        def light_local_attn(x, gamma, wq, wkv, wo):
            b, n, d = x.shape
            xn = rmsnorm(x, gamma)
            q = xn @ wq
            k, v = jnp.split(xn @ wkv, 2, axis=-1)

            def win(t):
                return t.reshape(b, n // WIN, WIN, HEADS, DH).transpose(0, 1, 3, 2, 4)
            q, k, v = (win(q) * SCALE, win(k), win(v))
            attn = jax.nn.softmax(jnp.einsum('bwhid,bwhjd->bwhij', q, k), axis=-1)
            out = jnp.einsum('bwhij,bwhjd->bwhid', attn, v)
            out = out.transpose(0, 1, 3, 2, 4).reshape(b, n, HID)
            return out @ wo

        def heavy_attn(xq, context, scores_kv, gamma, wq, wkv_t, wo):
            b, nq, d = xq.shape
            nkv = context.shape[1]
            xqn = rmsnorm(xq, gamma)
            ctx = rmsnorm(context, gamma)[:, None]
            q = (xqn @ wq).reshape(b, nq, HEADS, DH).transpose(0, 2, 1, 3) * SCALE
            kvw = wkv_t.reshape(1, HEADS, 2 * DH, d)
            kv = jnp.einsum('rhdi,brni->brhnd', kvw, ctx)
            k, v = jnp.split(kv, 2, axis=-1)
            v = v * scores_kv[:, None, None, :, None]
            k = k.reshape(b, HEADS, nkv, DH)
            v = v.reshape(b, HEADS, nkv, DH)
            attn = jax.nn.softmax(jnp.einsum('bhid,bhjd->bhij', q, k), axis=-1)
            out = jnp.einsum('bhij,bhjd->bhid', attn, v)
            out = out.transpose(0, 2, 1, 3).reshape(b, nq, HID)
            return out @ wo
        b = x.shape[0]
        light_out = light_local_attn(x, gamma_light, wq_light, wkv_light, wo_light)
        scores_q, idx_q = route(x, q_routing_token, NQ)
        scores_kv, idx_kv = route(x, kv_routing_token, NKV)
        routed_q = jnp.take_along_axis(x, idx_q[..., None], axis=1)
        routed_kv = jnp.take_along_axis(x, idx_kv[..., None], axis=1)
        routed_out = heavy_attn(routed_q, routed_kv, scores_kv, gamma_heavy, wq_heavy, wkv_heavy, wo_heavy)
        routed_out = routed_out * scores_q[..., None]
        heavy_out = jnp.zeros_like(x).at[jnp.arange(b)[:, None], idx_q].set(routed_out)
        return light_out + heavy_out

    def _L1_attn_ref(x, time_decay, time_mix_k, time_mix_v, time_mix_r, Wk, Wv, Wr, Wo):
        import jax, jax.numpy as jnp
        import numpy as np
        from jax import lax
        B, S, H = (8, 1024, 256)
        d = jnp.exp(-jnp.exp(time_decay))
        b, s, h = x.shape

        def step(state, xt):
            new_state = xt + state * d
            return (new_state, state)
        init = jnp.zeros((b, h), dtype=x.dtype)
        _, prev = lax.scan(step, init, jnp.swapaxes(x, 0, 1))
        prev = jnp.swapaxes(prev, 0, 1)
        k_in = x * time_mix_k + prev * (1.0 - time_mix_k)
        v_in = x * time_mix_v + prev * (1.0 - time_mix_v)
        r_in = x * time_mix_r + prev * (1.0 - time_mix_r)
        _k = jnp.einsum('bsh,oh->bso', k_in, Wk)
        v = jnp.einsum('bsh,oh->bso', v_in, Wv)
        r = jax.nn.sigmoid(jnp.einsum('bsh,oh->bso', r_in, Wr))
        out = r * jnp.einsum('bsh,oh->bso', v, Wo)
        return out

    def _L1_ffn_ref(x, wqkv, q_scale, k_scale, wo, ln_g, ln_b, w1, b1, w2, b2):
        import jax, jax.numpy as jnp
        import numpy as np
        DIM = 256
        DEPTH = 2
        HEADS = 8
        DIM_HEAD = 64
        WINDOW = 128
        INNER = HEADS * DIM_HEAD
        HID = int(DIM * 4 * 2 / 3)
        B, N = (2, 2048)
        QK_SCALE = 8.0

        def shift_token(t):
            t1, t2 = jnp.split(t, 2, axis=-1)
            t2 = jnp.pad(t2, ((0, 0), (1, 0), (0, 0)))[:, :-1]
            return jnp.concatenate([t1, t2], axis=-1)

        def l2norm(t):
            return t / jnp.clip(jnp.linalg.norm(t, axis=-1, keepdims=True), 1e-12)

        def rotate_half(x):
            x1, x2 = jnp.split(x, 2, axis=-1)
            return jnp.concatenate([-x2, x1], axis=-1)

        def rotary_xpos(q, k):
            n = q.shape[-2]
            half_idx = jnp.arange(0, DIM_HEAD, 2, dtype=jnp.float32)
            inv_freq = 1.0 / 10000.0 ** (half_idx / DIM_HEAD)
            t = jnp.arange(n, dtype=jnp.float32)
            freqs = t[:, None] * inv_freq[None, :]
            freqs = jnp.concatenate([freqs, freqs], axis=-1)
            base = (half_idx + 0.4 * DIM_HEAD) / (1.4 * DIM_HEAD)
            power = (t - n // 2) / float(WINDOW // 2)
            scale = base[None, :] ** power[:, None]
            scale = jnp.concatenate([scale, scale], axis=-1)
            cos, sin = (jnp.cos(freqs), jnp.sin(freqs))
            q = q * cos * scale + rotate_half(q) * sin * scale
            k = k * cos / scale + rotate_half(k) * sin / scale
            return (q, k)

        def local_attention(q, k, v):
            b, h, n, d = q.shape
            w = n // WINDOW
            bq = q.reshape(b, h, w, WINDOW, d) * QK_SCALE
            bk = k.reshape(b, h, w, WINDOW, d)
            bv = v.reshape(b, h, w, WINDOW, d)

            def look_around(t):
                p = jnp.pad(t, ((0, 0), (0, 0), (1, 0), (0, 0), (0, 0)))
                return jnp.concatenate([p[:, :, :w], p[:, :, 1:]], axis=3)
            bk, bv = (look_around(bk), look_around(bv))
            bt = jnp.arange(n).reshape(w, WINDOW)
            btp = jnp.pad(bt, ((1, 0), (0, 0)), constant_values=-1)
            btk = jnp.concatenate([btp[:w], btp[1:]], axis=1)
            sim = jnp.einsum('bhwid,bhwjd->bhwij', bq, bk)
            i = bt[:, :, None]
            j = btk[:, None, :]
            mask = (i < j) | (i > j + WINDOW) | (j == -1)
            sim = jnp.where(mask, -jnp.finfo(sim.dtype).max, sim)
            attn = jax.nn.softmax(sim, axis=-1)
            out = jnp.einsum('bhwij,bhwjd->bhwid', attn, bv)
            return out.reshape(b, h, n, d)

        def _layer(x, wqkv, qs, ksc, wo, lg, lb, w1, b1, w2, b2):
            b, n, _ = x.shape
            h = shift_token(x)
            qkv = h @ wqkv
            q, k, v = jnp.split(qkv, 3, axis=-1)
            to_heads = lambda t: t.reshape(b, n, HEADS, DIM_HEAD).transpose(0, 2, 1, 3)
            q, k, v = (to_heads(q), to_heads(k), to_heads(v))
            q = l2norm(q) * qs
            k = l2norm(k) * ksc
            q, k = rotary_xpos(q, k)
            o = local_attention(q, k, v)
            o = o.transpose(0, 2, 1, 3).reshape(b, n, INNER)
            x = x + o @ wo
            h = shift_token(x)
            mu = h.mean(-1, keepdims=True)
            var = h.var(-1, keepdims=True)
            h = (h - mu) / jnp.sqrt(var + 1e-05) * lg + lb
            h = h @ w1 + b1
            a, g = jnp.split(h, 2, axis=-1)
            h = a * jax.nn.gelu(g, approximate=False)
            x = x + h @ w2 + b2
            return x
        for l in range(DEPTH):
            x = _layer(x, wqkv[l], q_scale[l], k_scale[l], wo[l], ln_g[l], ln_b[l], w1[l], b1[l], w2[l], b2[l])
        return x
    x = L0_attn_x
    mod = (_silu(L0_c) @ L0_wmod).reshape(L0_c.shape[0], 6, 1, -1)
    sa, ca, ga, sb, cb, gb = (mod[:, 0], mod[:, 1], mod[:, 2], mod[:, 3], mod[:, 4], mod[:, 5])
    ga = (2 * (ga >= 0) - 1) * jnp.maximum(jnp.abs(ga), 0.25)
    gb = (2 * (gb >= 0) - 1) * jnp.maximum(jnp.abs(gb), 0.25)
    h = _layernorm(x, axis=-1) * (1 + ca) + sa
    x = x + ga * _L0_attn_ref(h, L0_attn_Wq, L0_attn_bq, L0_attn_Wk, L0_attn_bk, L0_attn_Wv, L0_attn_bv, L0_attn_Wo, L0_attn_bo)
    h = _layernorm(x, axis=-1) * (1 + cb) + sb
    x = x + gb * _L0_ffn_ref(h, L0_ffn_gamma_light, L0_ffn_wq_light, L0_ffn_wkv_light, L0_ffn_wo_light, L0_ffn_q_routing_token, L0_ffn_kv_routing_token, L0_ffn_gamma_heavy, L0_ffn_wq_heavy, L0_ffn_wkv_heavy, L0_ffn_wo_heavy)
    mod = (_silu(L1_c) @ L1_wmod).reshape(L1_c.shape[0], 6, 1, -1)
    sa, ca, ga, sb, cb, gb = (mod[:, 0], mod[:, 1], mod[:, 2], mod[:, 3], mod[:, 4], mod[:, 5])
    ga = (2 * (ga >= 0) - 1) * jnp.maximum(jnp.abs(ga), 0.25)
    gb = (2 * (gb >= 0) - 1) * jnp.maximum(jnp.abs(gb), 0.25)
    h = _layernorm(x, axis=-1) * (1 + ca) + sa
    x = x + ga * _L1_attn_ref(h, L1_attn_time_decay, L1_attn_time_mix_k, L1_attn_time_mix_v, L1_attn_time_mix_r, L1_attn_Wk, L1_attn_Wv, L1_attn_Wr, L1_attn_Wo)
    h = _layernorm(x, axis=-1) * (1 + cb) + sb
    x = x + gb * _L1_ffn_ref(h, L1_ffn_wqkv, L1_ffn_q_scale, L1_ffn_k_scale, L1_ffn_wo, L1_ffn_ln_g, L1_ffn_ln_b, L1_ffn_w1, L1_ffn_b1, L1_ffn_w2, L1_ffn_b2)
    return x

_drawn_inputs = setup_inputs


def setup_inputs(seed=0):
    import zlib

    import numpy as np

    out = dict(_drawn_inputs(seed))
    spreads = {'L0_ffn_gamma_light': (1.0, 0.6),
     'L0_ffn_gamma_heavy': (1.0, 0.6),
     'L1_attn_time_mix_k': (0.5, 0.2),
     'L1_attn_time_mix_v': (0.5, 0.6),
     'L1_attn_time_mix_r': (0.5, 0.6),
     'L1_ffn_q_scale': (1.0, 0.6),
     'L1_ffn_k_scale': (1.0, 0.6),
     'L1_ffn_ln_g': (1.0, 0.6),
     'L1_ffn_ln_b': (0.0, 0.8),
     'L1_ffn_b1': (0.0, 0.8),
     'L1_ffn_b2': (0.0, 0.451)}
    factors = {'L0_attn_bq': 8.0,
     'L0_attn_bk': 64.0,
     'L0_attn_bv': 8.0,
     'L0_attn_bo': 8.0,
     'L0_ffn_q_routing_token': 4.486,
     'L0_ffn_kv_routing_token': 5.878,
     'L0_ffn_wq_heavy': 4.434,
     'L0_ffn_wkv_heavy': 3.761,
     'L0_ffn_wo_heavy': 3.786,
     'L1_attn_time_decay': 64.0,
     'L1_attn_Wr': 8.0,
     'L1_ffn_wqkv': 6.661,
     'L1_ffn_wo': 6.805,
     'L1_ffn_w1': 4.774,
     'L1_ffn_w2': 4.739}
    for name, (base, spread) in spreads.items():
        noise = np.random.default_rng([zlib.crc32(name.encode()), seed]).standard_normal(out[name].shape)
        drawn = base * np.exp(spread * noise) if base else spread * noise
        out[name] = jnp.asarray(drawn.astype(out[name].dtype))
    for name, factor in factors.items():
        out[name] = (out[name] * factor).astype(out[name].dtype)
    return out
```

```python
from contextlib import ExitStack

import numpy as np
import concourse.bass as bass
from concourse import mybir

F32 = mybir.dt.float32
BF16 = mybir.dt.bfloat16
I32 = mybir.dt.int32
ACT = mybir.ActivationFunctionType
ALU = mybir.AluOpType
AX_X = mybir.AxisListType.X

P = 128
B, T, D = 4, 1024, 256
DK = D // P
TP = T + 1
NB = 512
NBLK = T // NB
WIN = 128
NW = T // WIN
A_H, A_HD = 16, 16
A_G = 4
HEADS, DH = 8, 64
HID = HEADS * DH
HM = HID // P
NQ, NKV, FETCH = 256, 512, 9.0 / 8.0
N_ITERS = 50
FFN = int(D * 4 * 2 / 3)
FM = -(-FFN // P)
NEG = -1e30
LN_EXP = "natural_log_exp_and_others"
LN_EPS = 1e-5
NORM2_MIN = 1e-24
LN2 = float(np.log(2.0))
LN_SHIFT = 20


ONE = 1


def upto(i, per, k):
    return i * per + k


class Chain:

    def __init__(self, eng, sem, i, per):
        self.eng, self.sem, self.i, self.per, self.n = eng, sem, i, per, 0

    def __call__(self, ins):
        ins.then_inc(self.sem, 1)
        self.n += 1
        self.eng.wait_ge(self.sem, ONE + upto(self.i, self.per, self.n))

    def close(self):
        assert self.n == self.per, (self.n, self.per)


class Scope:

    def __init__(self, nc, ctx, tag):
        self.nc, self.ctx, self.tag, self.sems = nc, ctx, tag, []

    def sb(self, name, shape, dt=F32):
        return self.ctx.enter_context(self.nc.sbuf_tensor(f"{self.tag}_{name}", shape, dt))

    def ps(self, name, shape=(P, 512), dt=F32):
        return self.ctx.enter_context(self.nc.psum_tensor(f"{self.tag}_{name}", list(shape), dt))

    def sem(self, name):
        if not self.sems:
            self.ctx.callback(self.clear)
        self.sems.append(self.nc.alloc_semaphore(f"{self.tag}_{name}"))
        self.nc.sync.sem_inc(self.sems[-1], ONE)
        return self.sems[-1]

    def clear(self):
        self.nc.clear_and_free_semaphores(self.sems)
        self.nc.all_engine_barrier()


def col(b, off, n):
    return bass.ds(b * TP + 1 + off, n)


def modulation_stage(nc, g, d):
    with ExitStack() as ctx:
        s = Scope(nc, ctx, "mod")
        c = s.sb("c", [P, 2, DK, B])
        e = s.sb("e", [P, 2, DK, B])
        w = s.sb("w", [P, 2, DK, 6 * D])
        ng = s.sb("ng", [P, 2, B, 12])
        sg = s.sb("sg", [P, 2, B, 12])
        pm = s.ps("pm", [P, 2, 12, B])
        s_load, s_exp, s_c, s_mm, s_v, s_zero = (s.sem(x) for x in ("load", "exp", "c", "mm", "v", "zero"))
        MOD = g["MOD"]
        with nc.Block() as block:
            @block.sync
            def _(sp):
                for l in range(2):
                    sp.dma_start(c[:, l], d["cT"][l].rearrange("(k p) b -> p k b", p=P)).then_inc(s_load, 16)
                    sp.dma_start(w[:, l], d["wmod"][l].rearrange("(k p) n -> p k n", p=P)).then_inc(s_load, 16)
                sp.dma_start(g["X"][:, :, :], d["xT"].rearrange("(k p) n -> p k n", p=P)).then_inc(s_load, 16)
                for name in ("ones", "ident", "blk64", "rot64"):
                    sp.dma_start(g[name][:, :], d[name]).then_inc(s_load, 16)
                sp.wait_ge(s_load, ONE + 16 * 9)

            @block.gpsimd
            def _(pool):
                pool.memset(g["bias"][:, 0:1], LN_EPS).then_inc(s_zero, 1)
                for n, v in enumerate((1.0, 8.0, 16.0)):
                    pool.memset(g["bias"][:, n + 1:n + 2], float(np.log(v)) + 0.5 * LN_SHIFT * LN2).then_inc(s_zero, 1)
                pool.wait_ge(s_zero, ONE + 4)

            @block.scalar
            def _(act):
                act.wait_ge(s_load, ONE + 16 * 9)
                act.activation(e[:, :, :, :], c[:, :, :, :], ACT.Exp, scale=-1.0).then_inc(s_exp, 1)

            @block.tensor
            def _(pe):
                pe.wait_ge(s_c, ONE + 3)
                for l in range(2):
                    for m in range(12):
                        for k in range(DK):
                            ins = pe.matmul(pm[:, l, m, :], w[:, l, k, m * P:(m + 1) * P], c[:, l, k, :],
                                            start=(k == 0), stop=(k == DK - 1))
                ins.then_inc(s_mm, 1)

            @block.vector
            def _(dve):
                link = Chain(dve, s_v, 0, 8)
                dve.wait_ge(s_exp, ONE + 1)
                dve.tensor_scalar(e[:, :, :, :], e[:, :, :, :], 1.0, None, ALU.add).then_inc(s_c, 1)
                dve.wait_ge(s_c, ONE + 1)
                dve.reciprocal(e[:, :, :, :], e[:, :, :, :]).then_inc(s_c, 1)
                dve.wait_ge(s_c, ONE + 2)
                dve.tensor_tensor(c[:, :, :, :], c[:, :, :, :], e[:, :, :, :], ALU.mult).then_inc(s_c, 1)
                dve.wait_ge(s_mm, ONE + 1)
                for l in range(2):
                    link(dve.tensor_copy(MOD[:, l, :, :], pm[:, l].rearrange("p m b -> p b m")))
                v = MOD[:, :, :, :].rearrange("p l b (s k) -> p (l b) s k", k=DK)
                sc = v[:, :, 1:5:3, :]
                link(dve.tensor_scalar(sc, sc, 1.0, None, ALU.add))
                gt = v[:, :, 2:6:3, :]
                n_ = ng[:, :, :, 0:4].rearrange("p l b (s k) -> p (l b) s k", k=DK)
                s_ = sg[:, :, :, 0:4].rearrange("p l b (s k) -> p (l b) s k", k=DK)
                link(dve.tensor_scalar(n_, gt, -1.0, None, ALU.mult))
                link(dve.tensor_tensor(n_, n_, gt, ALU.max))
                link(dve.tensor_scalar(n_, n_, 0.25, 2.0, ALU.max, ALU.mult))
                link(dve.tensor_scalar(s_, gt, 0.0, -0.5, ALU.is_ge, ALU.add))
                link(dve.tensor_tensor(gt, s_, n_, ALU.mult))
                link.close()


def norm_stage(nc, g, d, tag, layer, which, route=False):
    with ExitStack() as ctx:
        s = Scope(nc, ctx, tag)
        xc, sq, h, hs = (s.sb(n, [P, DK, NB]) for n in ("xc", "sq", "h", "hs"))
        lv, rs, l2, r2 = (s.sb(n, [P, NB]) for n in ("lv", "rs", "l2", "r2"))
        p_mean, p_var, p_nn = s.ps("p_mean"), s.ps("p_var"), s.ps("p_nn")
        s_mean, s_xc, s_sq, s_var, s_rs, s_v, s_a, s_h = (
            s.sem(x) for x in ("mean", "xc", "sq", "var", "rs", "v", "a", "h"))
        s_h2, s_nn, s_n2, s_r2, s_rt, s_st, s_out, s_load, s_y = (
            s.sem(x) for x in ("h2", "nn", "n2", "r2_", "rt", "st", "out", "load", "y"))
        MOD, X, Y = g["MOD"], g["X"], g["Y"]
        if route:
            p_rt = s.ps("p_rt", (2, NB))
            rtok = s.sb("rtok", [P, DK, 2])
            srow = s.sb("srow", [2, NB])

        def blocks(eng):
            with eng.Fori(0, B) as b:
                with eng.Fori(0, NBLK) as c:
                    yield b, c

        with nc.Block() as block:
            @block.sync
            def _(sp):
                if route:
                    sp.dma_start(rtok[:, :, :], d["rtok"].rearrange("(k p) r -> p k r", p=P)).then_inc(s_load, 16)
                    for b, c in blocks(sp):
                        i = b * NBLK + c
                        sp.wait_ge(s_st, ONE + i + 1)
                        sp.dma_start(g["s_dram"][bass.ds(2 * b, 2), bass.ds(c * NB, NB)], srow[:, :]).then_inc(s_out, 16)
                    sp.wait_ge(s_out, ONE + 16 * B * NBLK)

            @block.tensor
            def _(pe):
                if route:
                    pe.wait_ge(s_load, ONE + 16)
                for b, c in blocks(pe):
                    i = b * NBLK + c
                    pe.wait_ge(s_xc, ONE + 2 * i)
                    for k in range(DK):
                        ins = pe.matmul(p_mean[:, :], g["ones"][:, :], X[:, k, bass.ds(b * T + c * NB, NB)],
                                        start=(k == 0), stop=(k == DK - 1))
                    ins.then_inc(s_mean, 1)
                    pe.wait_ge(s_sq, ONE + upto(i, 1, 1))
                    for k in range(DK):
                        ins = pe.matmul(p_var[:, :], g["ones"][:, :], sq[:, k, :], start=(k == 0), stop=(k == DK - 1))
                    ins.then_inc(s_var, 1)
                    if route:
                        pe.wait_ge(s_h, ONE + upto(i, 1, 1))
                        pe.wait_ge(s_st, ONE + i)
                        for k in range(DK):
                            ins = pe.matmul(p_rt[:, :], rtok[:, k, :], h[:, k, :], start=(k == 0), stop=(k == DK - 1))
                        ins.then_inc(s_rt, 1)
                        pe.wait_ge(s_h2, ONE + upto(i, 1, 1))
                        for k in range(DK):
                            ins = pe.matmul(p_nn[:, :], g["ones"][:, :], hs[:, k, :], start=(k == 0), stop=(k == DK - 1))
                        ins.then_inc(s_nn, 1)

            @block.scalar
            def _(act):
                act.preload_act_table_set(LN_EXP)
                for b, c in blocks(act):
                    i = b * NBLK + c
                    act.wait_ge(s_xc, ONE + upto(i, 2, 2))
                    act.wait_ge(s_var, ONE + i)
                    act.activation(sq[:, :, :], xc[:, :, :], ACT.Square).then_inc(s_sq, 1)
                    act.wait_ge(s_var, ONE + upto(i, 1, 1))
                    act.activation(lv[:, :], p_var[:, :], ACT.Ln, bias=g["bias"][:, 0:1]).then_inc(s_a, 1)
                    act.wait_ge(s_a, ONE + upto(i, 1, 1))
                    act.activation(rs[:, :], lv[:, :], ACT.Exp, scale=-0.5).then_inc(s_rs, 1)
                    if route:
                        act.wait_ge(s_h, ONE + upto(i, 1, 1))
                        act.activation(hs[:, :, :], h[:, :, :], ACT.Square).then_inc(s_h2, 1)
                        act.wait_ge(s_n2, ONE + upto(i, 1, 1))
                        act.activation(l2[:, :], r2[:, :], ACT.Ln, scale=float(2 ** LN_SHIFT)).then_inc(s_r2, 1)
                        act.wait_ge(s_r2, ONE + upto(i, 2, 1))
                        act.activation(r2[:, :], l2[:, :], ACT.Exp, scale=-0.5, bias=g["bias"][:, 1:2]).then_inc(s_r2, 1)

            @block.vector
            def _(dve):
                for b, c in blocks(dve):
                    i = b * NBLK + c
                    link = Chain(dve, s_v, i, 2)
                    dve.wait_ge(s_h, ONE + i)
                    dve.wait_ge(s_mean, ONE + upto(i, 1, 1))
                    for k in range(DK):
                        dve.tensor_tensor(xc[:, k, :], X[:, k, bass.ds(b * T + c * NB, NB)], p_mean[:, :],
                                          ALU.subtract).then_inc(s_xc, 1)
                    dve.wait_ge(s_rs, ONE + upto(i, 1, 1))
                    for k in range(DK):
                        ins = dve.tensor_tensor(xc[:, k, :], xc[:, k, :], rs[:, :], ALU.mult)
                        link(ins)
                    for k in range(DK):
                        if route:
                            out = h[:, k, :]
                        else:
                            out = Y[:, k, col(b, c * NB, NB)]
                        ins = dve.tensor_scalar(out, xc[:, k, :], MOD[:, layer, bass.ds(b, 1), which * 6 + 2 + k],
                                                MOD[:, layer, bass.ds(b, 1), which * 6 + k], ALU.mult, ALU.add)
                    ins.then_inc(s_h, 1)
                    if route:
                        dve.wait_ge(s_rt, ONE + upto(i, 1, 1))
                        dve.wait_ge(s_out, ONE + 16 * i)
                        dve.tensor_copy(srow[:, :], p_rt[:, :]).then_inc(s_st, 1)
                        dve.wait_ge(s_nn, ONE + upto(i, 1, 1))
                        dve.tensor_scalar(r2[:, :], p_nn[:, :], NORM2_MIN / D, None, ALU.max).then_inc(s_n2, 1)
                        dve.wait_ge(s_r2, ONE + upto(i, 2, 2))
                        for k in range(DK):
                            ins = dve.tensor_tensor(Y[:, k, col(b, c * NB, NB)], h[:, k, :], r2[:, :], ALU.mult)
                        ins.then_inc(s_y, 1)
                        dve.wait_ge(s_y, ONE + upto(i, 1, 1))
                    link.close()


def split_stage(nc, g, d):
    with ExitStack() as ctx:
        s = Scope(nc, ctx, "sp")
        wqk = s.sb("wqk", [P, DK, 4, P])
        wv = s.sb("wv", [P, DK, D])
        bqk, bv = s.sb("bqk", [P, 4]), s.sb("bv", [P, D])
        xc, sq, hn = (s.sb(n, [P, DK, NB]) for n in ("xc", "sq", "hn"))
        lv, rs = s.sb("lv", [P, NB]), s.sb("rs", [P, NB])
        f, r1, r2 = (s.sb(n, [P, 4, NB]) for n in ("f", "r1", "r2"))
        part = s.sb("part", [P, 3, 4, NB], BF16)
        v = s.sb("v", [P, 4, A_H, 32])
        p_mean, p_var = s.ps("p_mean"), s.ps("p_var")
        p_x = [s.ps(f"p_x{k}") for k in range(4)]
        p_v = [s.ps(f"p_v{k}") for k in range(2)]
        names = "load ini mean xc sq var l rs v hn px fe c1 r1 c2 r2 c3 pv ve out".split()
        (s_load, s_ini, s_mean, s_xc, s_sq, s_var, s_l, s_rs, s_v, s_hn, s_px, s_fe, s_c1, s_r1, s_c2, s_r2, s_c3, s_pv, s_ve,
         s_out) = (s.sem("s" + x) for x in names)
        X, MOD = g["X"], g["MOD"]
        NTB = NB // P

        def blocks(eng):
            with eng.Fori(0, B) as b:
                with eng.Fori(0, NBLK) as c:
                    yield b, c, b * NBLK + c

        with nc.Block() as block:
            @block.sync
            def _(sp):
                sp.dma_start(wqk[:, :, :, :], d["wqk"].rearrange("(k p) x n -> p k x n", p=P)).then_inc(s_load, 16)
                sp.dma_start(wv[:, :, :], d["wv"].rearrange("(k p) n -> p k n", p=P)).then_inc(s_load, 16)
                sp.dma_start(bqk[:, :], d["bqk"]).then_inc(s_load, 16)
                sp.dma_start(bv[:, :], d["bv"].to_broadcast([P, D])).then_inc(s_load, 16)
                for b, c, i in blocks(sp):
                    tok = bass.ds(c * NB, NB)
                    sems = (s_c1, s_c2, s_c3)
                    for p in range(3):
                        sp.wait_ge(sems[p], ONE + i + 1)
                        for x in range(4):
                            for gg in range(2):
                                sp.dma_start(g["part_dram"][p, x // 2, bass.ds(b * A_G + 2 * (x % 2) + gg, 1), :, tok],
                                             part[gg * 64:gg * 64 + 64, p, x, :]).then_inc(s_out, 16)
                    sp.wait_ge(s_ve, ONE + 2 * i + 2)
                    for gr in range(A_G):
                        sp.dma_start(g["v_dram"][bass.ds(b * A_G + gr, 1), bass.ds(c * NTB, NTB)].rearrange("a t p e -> p (a t) e"),
                                     v[:, :, gr * 4:(gr + 1) * 4, :].rearrange("p t j e -> p t (j e)")).then_inc(s_out, 16)
                sp.wait_ge(s_out, ONE + 16 * 28 * B * NBLK)

            @block.tensor
            def _(pe):
                pe.wait_ge(s_load, ONE + 64)
                for b, c, i in blocks(pe):
                    pe.wait_ge(s_xc, ONE + 2 * i)
                    for k in range(DK):
                        ins = pe.matmul(p_mean[:, :], g["ones"][:, :], X[:, k, bass.ds(b * T + c * NB, NB)],
                                        start=(k == 0), stop=(k == DK - 1))
                    ins.then_inc(s_mean, 1)
                    pe.wait_ge(s_sq, ONE + i + 1)
                    for k in range(DK):
                        ins = pe.matmul(p_var[:, :], g["ones"][:, :], sq[:, k, :], start=(k == 0), stop=(k == DK - 1))
                    ins.then_inc(s_var, 1)
                    pe.wait_ge(s_hn, ONE + i + 1)
                    for x in range(4):
                        pe.wait_ge(s_fe, ONE + 4 * i)
                        for k in range(DK):
                            ins = pe.matmul(p_x[x][:, :], wqk[:, k, x, :], hn[:, k, :], start=(k == 0), stop=(k == DK - 1))
                        ins.then_inc(s_px, 1)
                    for n in range(2):
                        pe.wait_ge(s_ve, ONE + 2 * i)
                        for q in range(2):
                            t = 2 * n + q
                            for k in range(DK):
                                ins = pe.matmul(p_v[n][:, q * D:(q + 1) * D], hn[:, k, t * P:(t + 1) * P], wv[:, k, :],
                                                start=(k == 0), stop=(k == DK - 1))
                        ins.then_inc(s_pv, 1)

            @block.scalar
            def _(act):
                act.preload_act_table_set(LN_EXP)
                act.wait_ge(s_load, ONE + 64)
                for b, c, i in blocks(act):
                    act.wait_ge(s_xc, ONE + 2 * i + 2)
                    act.activation(sq[:, :, :], xc[:, :, :], ACT.Square).then_inc(s_sq, 1)
                    act.wait_ge(s_var, ONE + i + 1)
                    act.activation(lv[:, :], p_var[:, :], ACT.Ln, bias=g["bias"][:, 0:1]).then_inc(s_l, 1)
                    act.wait_ge(s_l, ONE + i + 1)
                    act.activation(rs[:, :], lv[:, :], ACT.Exp, scale=-0.5).then_inc(s_rs, 1)
                    act.wait_ge(s_out, ONE + 16 * 28 * i)
                    act.wait_ge(s_fe, ONE + 4 * i + 4)
                    act.activation(part[:, 0, :, :], f[:, :, :], ACT.Copy).then_inc(s_c1, 1)
                    act.wait_ge(s_r1, ONE + i + 1)
                    act.activation(part[:, 1, :, :], r1[:, :, :], ACT.Copy).then_inc(s_c2, 1)
                    act.wait_ge(s_r2, ONE + i + 1)
                    act.activation(part[:, 2, :, :], r2[:, :, :], ACT.Copy).then_inc(s_c3, 1)

            @block.gpsimd
            def _(pool):
                pool.memset(v[:, :, :, A_HD:A_HD + 1], 1.0).then_inc(s_ini, 1)
                pool.memset(v[:, :, :, A_HD + 1:32], 0.0).then_inc(s_ini, 1)
                for b, c, i in blocks(pool):
                    pool.wait_ge(s_c2, ONE + i + 1)
                    pool.wait_ge(s_c3, ONE + i)
                    pool.tensor_tensor(r2[:, :, :], r1[:, :, :], part[:, 1, :, :], ALU.subtract).then_inc(s_r2, 1)

            @block.vector
            def _(dve):
                dve.wait_ge(s_load, ONE + 64)
                dve.wait_ge(s_ini, ONE + 2)
                for b, c, i in blocks(dve):
                    link = Chain(dve, s_v, i, 2)
                    dve.wait_ge(s_hn, ONE + i)
                    dve.wait_ge(s_mean, ONE + i + 1)
                    for k in range(DK):
                        dve.tensor_tensor(xc[:, k, :], X[:, k, bass.ds(b * T + c * NB, NB)], p_mean[:, :],
                                          ALU.subtract).then_inc(s_xc, 1)
                    dve.wait_ge(s_rs, ONE + i + 1)
                    for k in range(DK):
                        link(dve.tensor_tensor(xc[:, k, :], xc[:, k, :], rs[:, :], ALU.mult))
                    dve.wait_ge(s_pv, ONE + 2 * i)
                    for k in range(DK):
                        ins = dve.tensor_scalar(hn[:, k, :], xc[:, k, :], MOD[:, 0, bass.ds(b, 1), 2 + k],
                                                MOD[:, 0, bass.ds(b, 1), k], ALU.mult, ALU.add)
                    ins.then_inc(s_hn, 1)
                    dve.wait_ge(s_c1, ONE + i)
                    dve.wait_ge(s_r1, ONE + i)
                    for x in range(4):
                        dve.wait_ge(s_px, ONE + upto(i, 4, x + 1))
                        dve.tensor_scalar(f[:, x, :], p_x[x][:, :], bqk[:, x:x + 1], float(A_HD) ** -0.5 if x < 2 else 1.0,
                                          ALU.add, ALU.mult).then_inc(s_fe, 1)
                    dve.wait_ge(s_out, ONE + 16 * 28 * i)
                    for n in range(2):
                        dve.wait_ge(s_pv, ONE + upto(i, 2, n + 1))
                        for q in range(2):
                            ins = dve.tensor_tensor(v[:, 2 * n + q, :, 0:A_HD],
                                                    p_v[n][:, q * D:(q + 1) * D].rearrange("p (h e) -> p h e", e=A_HD),
                                                    bv[:, :].rearrange("p (h e) -> p h e", e=A_HD), ALU.add)
                        ins.then_inc(s_ve, 1)
                    dve.wait_ge(s_c1, ONE + i + 1)
                    dve.wait_ge(s_fe, ONE + 4 * i + 4)
                    dve.wait_ge(s_r2, ONE + i)
                    dve.wait_ge(s_c2, ONE + i)
                    dve.tensor_tensor(r1[:, :, :], f[:, :, :], part[:, 0, :, :], ALU.subtract).then_inc(s_r1, 1)


def causal_stage(nc, g, d):
    QP, KP = (0, 0, 1, 0, 1, 2), (0, 1, 0, 2, 1, 0)
    R0 = 6 * A_HD
    NR, RING = B * A_G, 3
    NT = T // P
    steps = [(n, kt) for n in range(2) for kt in range(4 * n + 4)]
    units = [(t, c, j) for t in range(NT) for c in range(t // 4 + 1) for j in range(4)]
    NS, NU = 4 * len(steps), len(units)
    PER_STEP = -(-NU // (len(steps) - 2))
    with ExitStack() as ctx:
        s = Scope(nc, ctx, "ca")
        qs = [s.sb(f"qs{n}", [P, 4, T], BF16) for n in range(RING)]
        ks = [s.sb(f"ks{n}", [P, 4, T], BF16) for n in range(RING)]
        vg = [s.sb(f"vg{n}", [P, NT, 4, 32]) for n in range(RING)]
        mp, nm, m_r = s.sb("mp", [P, NT, 2, 4]), s.sb("nm", [P, NT, 4]), s.sb("m_r", [P, NT, 4])
        n3 = s.sb("n3", [P, NT, 4, 32], BF16)
        mt = s.sb("mt", [P, T], BF16)
        pt = s.sb("pt", [P, 2, 4, 512])
        osb, rden = s.sb("osb", [P, 2, 512]), s.sb("rden", [P, 2, 512])
        mqk, mkq, idb = (s.sb(n, [P, P], BF16) for n in ("mqk", "mkq", "idb"))
        den = s.sb("den", [P, P])
        p_1 = [s.ps(f"p_1{n}") for n in range(2)]
        p_s = [s.ps(f"p_s{n}") for n in range(4)]
        p_o, p_m = s.ps("p_o"), s.ps("p_m")
        names = "load ini lda ldb ldc s1 mxa mxb dv mt me md st ex pv oe dn l rd on".split()
        (s_load, s_ini, s_lda, s_ldb, s_ldc, s_s1, s_mxa, s_mxb, s_dv, s_mt, s_me, s_md, s_st, s_ex, s_pv, s_oe, s_dn, s_l, s_rd,
         s_on) = (s.sem(x) for x in names)
        s_ld = (s_lda, s_ldb, s_ldc)
        s_mx = (s_mxa, s_mxb)
        OA = g["OA"]
        LOADS = 16 * 13

        def rounds(eng, body):
            with eng.Fori(0, NR // RING) as i:
                for u in range(RING):
                    body(i * RING + u, i, u, True)
            body(NR - 1, NR // RING, (NR - 1) % RING, False)

        with nc.Block() as block:
            @block.sync
            def _(sp):
                for dst, name in ((mqk, "mqk"), (mkq, "mkq"), (idb, "idb"), (den, "den")):
                    sp.dma_start(dst[:, :], d[name]).then_inc(s_load, 16)

                def load(r, u):
                    for dst, x, parts in ((qs[u], 0, QP), (ks[u], 1, KP)):
                        for c, p in enumerate(parts):
                            sp.dma_start(dst[A_HD * c:A_HD * (c + 1), :, :],
                                         g["part_dram"][p, x, bass.ds(r, 1)].rearrange("a (j e) t -> e (a j) t", e=A_HD))\
                              .then_inc(s_ld[u], 16)
                    sp.dma_start(vg[u][:, :, :, :].rearrange("p t j e -> p t (j e)"),
                                 g["v_dram"][bass.ds(r, 1)].rearrange("a t p e -> p (a t) e")).then_inc(s_ld[u], 16)

                def maxima(r, u):
                    sp.wait_ge(s_me, ONE + r + 1)
                    for j in range(4):
                        sp.dma_start(qs[u][R0:R0 + 3, j, :], mt[32 * j:32 * j + 3, :]).then_inc(s_md, 16)

                load(0, 0)
                load(1, 1)
                maxima(0, 0)

                def body(r, u):
                    sp.wait_ge(s_pv, ONE + NS * r)
                    load(r + 2, (u + 2) % RING)
                    maxima(r + 1, (u + 1) % RING)

                with sp.Fori(0, NR // RING - 1) as i:
                    for u in range(RING):
                        body(i * RING + u, u)
                for r in range(NR - RING - 1, NR):
                    u = r % RING
                    sp.wait_ge(s_pv, ONE + NS * r)
                    if r + 2 < NR:
                        load(r + 2, (u + 2) % RING)
                    if r + 1 < NR:
                        maxima(r + 1, (u + 1) % RING)

            @block.gpsimd
            def _(pool):
                pool.memset(n3[:, :, :, :], 0.0).then_inc(s_ini, 1)
                pool.memset(mp[:, :, :, :], -3.0e38).then_inc(s_ini, 1)
                for n in range(RING):
                    pool.wait_ge(s_ini, ONE + 2 + n)
                    pool.memset(ks[n][R0:R0 + 32, :, :], 1.0).then_inc(s_ini, 1)

                def body(r, i, u, more):
                    for n in range(2):
                        pool.wait_ge(s_rd, ONE + upto(r, 2, n + 1))
                        pool.wait_ge(s_oe, ONE + upto(r, 2, n + 1))
                        pool.tensor_tensor(OA[:, bass.ds(r, 1), n * 512:(n + 1) * 512], osb[:, n:n + 1, :], rden[:, n:n + 1, :],
                                           ALU.mult).then_inc(s_on, 1)

                rounds(pool, body)

            @block.tensor
            def _(pe):
                pe.wait_ge(s_load, ONE + 64)
                pe.wait_ge(s_ini, ONE + 2 + RING)

                def first_pass(r, i, u, n):
                    t, c, j = units[n]
                    if n == 0:
                        pe.wait_ge(s_ld[u], ONE + LOADS * (i + 1))
                    pe.wait_ge(s_mx[n % 2], ONE + upto(r, NU // 2, n // 2))
                    c0, c1 = 512 * c, min((t + 1) * P, 512 * (c + 1))
                    diag = c == t // 4
                    ins = pe.matmul(p_1[n % 2][:, 0:c1 - c0], qs[u][0:R0, j, t * P:(t + 1) * P], ks[u][0:R0, j, c0:c1],
                                    start=True, stop=not diag)
                    if diag:
                        ins = pe.matmul(p_1[n % 2][:, c1 - c0 - P:c1 - c0], idb[:, :], mqk[:, :], start=False, stop=True)
                    ins.then_inc(s_s1, 1)

                def turn_maxima(r):
                    pe.wait_ge(s_dv, ONE + upto(r, 6, 6))
                    for t in range(NT):
                        ins = pe.transpose(p_m[:, :].bitcast(BF16)[:, t * P:(t + 1) * P],
                                           n3[:, t, :, :].rearrange("p j e -> p (j e)"), idb[:, :])
                    ins.then_inc(s_mt, 1)

                def scores(r, u, st):
                    n, kt = steps[st]
                    c0 = max(0, kt * P - n * 512)
                    diag = kt * P >= n * 512
                    for j in range(4):
                        pe.wait_ge(s_ex, ONE + upto(r, NS, max(0, 4 * st - 3 + j)))
                        ins = pe.matmul(p_s[j][:, c0:512], ks[u][0:R0 + 3, j, kt * P:(kt + 1) * P],
                                        qs[u][0:R0 + 3, j, n * 512 + c0:(n + 1) * 512], start=True, stop=not diag)
                        if diag:
                            ins = pe.matmul(p_s[j][:, c0:c0 + P], idb[:, :], mkq[:, :], start=False, stop=True)
                        ins.then_inc(s_st, 1)

                def values(r, u, st):
                    n, kt = steps[st]
                    c0 = max(0, kt * P - n * 512)
                    for j in range(4):
                        if j == 0 and kt == 0:
                            pe.wait_ge(s_oe, ONE + upto(r, 2, n))
                        pe.wait_ge(s_ex, ONE + upto(r, NS, 4 * st + j + 1))
                        pe.matmul(p_o[32 * j:32 * j + 32, c0:512], vg[u][:, kt, j, :], pt[:, st % 2, j, c0:512],
                                  start=(kt == 0), stop=(kt == 4 * n + 3), tile_position=(0, 32 * j)).then_inc(s_pv, 1)

                def denominators(r, n):
                    pe.wait_ge(s_oe, ONE + upto(r, 2, n + 1))
                    pe.matmul(p_m[:, :], den[:, :], osb[:, n, :], start=True, stop=True).then_inc(s_dn, 1)

                for n in range(NU):
                    first_pass(0, 0, 0, n)
                turn_maxima(0)

                def body(r, i, u, more):
                    pe.wait_ge(s_md, ONE + 64 * (r + 1))
                    done = 0
                    for st in range(len(steps)):
                        scores(r, u, st)
                        if more:
                            upper = min(NU, PER_STEP * (st + 1))
                            for n in range(done, upper):
                                first_pass(r + 1, i + (u + 1) // RING, (u + 1) % RING, n)
                            done = upper
                        if st:
                            values(r, u, st - 1)
                        if st == 6:
                            pe.wait_ge(s_me, ONE + r + 1)
                            pe.wait_ge(s_l, ONE + 2 * r)
                            denominators(r, 0)
                    values(r, u, len(steps) - 1)
                    pe.wait_ge(s_l, ONE + 2 * r + 1)
                    if more:
                        turn_maxima(r + 1)
                        pe.wait_ge(s_me, ONE + r + 2)
                    denominators(r, 1)

                rounds(pe, body)

            @block.scalar
            def _(act):
                act.preload_act_table_set(LN_EXP)

                def body(r, i, u, more):
                    def reciprocals(n):
                        act.wait_ge(s_dn, ONE + upto(r, 2, n + 1))
                        act.wait_ge(s_on, ONE + 2 * r)
                        act.activation(rden[:, n, :], p_m[:, :], ACT.Ln).then_inc(s_l, 1)
                        act.wait_ge(s_l, ONE + upto(r, 2, n + 1))
                        act.activation(rden[:, n, :], rden[:, n, :], ACT.Exp, scale=-1.0).then_inc(s_rd, 1)

                    for st, (n, kt) in enumerate(steps):
                        c0 = max(0, kt * P - n * 512)
                        for j in range(4):
                            act.wait_ge(s_st, ONE + upto(r, NS, 4 * st + j + 1))
                            act.wait_ge(s_pv, ONE + upto(r, NS, max(0, 4 * st - 7 + j)))
                            act.activation(pt[:, st % 2, j, c0:512], p_s[j][:, c0:512], ACT.Exp).then_inc(s_ex, 1)
                        if st == 7:
                            reciprocals(0)
                    reciprocals(1)

                rounds(act, body)

            @block.vector
            def _(dve):
                dve.wait_ge(s_ini, ONE + 2 + RING)

                def maximum(r, n):
                    t, c, j = units[n]
                    c0, c1 = 512 * c, min((t + 1) * P, 512 * (c + 1))
                    dve.wait_ge(s_s1, ONE + upto(r, NU, n + 1))
                    dve.tensor_reduce(mp[:, t, c, j:j + 1], p_1[n % 2][:, 0:c1 - c0], AX_X, ALU.max).then_inc(s_mx[n % 2], 1)

                def split_maxima(r):
                    link = Chain(dve, s_dv, r, 6)
                    for half in s_mx:
                        dve.wait_ge(half, ONE + upto(r, NU // 2, NU // 2))
                    dve.wait_ge(s_mt, ONE + r)
                    link(dve.tensor_tensor(nm[:, :, :], mp[:, :, 0, :], mp[:, :, 1, :], ALU.max))
                    link(dve.tensor_scalar(n3[:, :, :, 0], nm[:, :, :], -1.0, None, ALU.mult))
                    link(dve.scalar_tensor_tensor(m_r[:, :, :], nm[:, :, :], -1.0, n3[:, :, :, 0], ALU.mult, ALU.subtract))
                    link(dve.tensor_copy(n3[:, :, :, 1], m_r[:, :, :]))
                    link(dve.tensor_tensor(m_r[:, :, :], m_r[:, :, :], n3[:, :, :, 1], ALU.subtract))
                    link(dve.tensor_copy(n3[:, :, :, 2], m_r[:, :, :]))
                    link.close()

                def copy_turned(r):
                    dve.wait_ge(s_mt, ONE + r + 1)
                    dve.wait_ge(s_md, ONE + 64 * r)
                    dve.tensor_copy(mt[:, :], p_m[:, :].bitcast(BF16)).then_inc(s_me, 1)

                def copy_sums(r, n):
                    dve.wait_ge(s_pv, ONE + upto(r, NS, 16 if n == 0 else NS))
                    dve.wait_ge(s_on, ONE + 2 * r)
                    dve.tensor_copy(osb[:, n, :], p_o[:, :]).then_inc(s_oe, 1)

                for n in range(NU):
                    maximum(0, n)
                split_maxima(0)
                copy_turned(0)

                def body(r, i, u, more):
                    done = 0
                    for st in range(len(steps)):
                        if more:
                            upper = min(NU, PER_STEP * (st + 1))
                            for n in range(done, upper):
                                maximum(r + 1, n)
                            done = upper
                        if st == 4:
                            copy_sums(r, 0)
                        if st == len(steps) - 2 and more:
                            split_maxima(r + 1)
                    copy_sums(r, 1)
                    if more:
                        copy_turned(r + 1)

                rounds(dve, body)

    with ExitStack() as ctx:
        s = Scope(nc, ctx, "co")
        wo = s.sb("wo", [P, A_G, D])
        bo = s.sb("bo", [P, DK])
        t_ = s.sb("t", [P, DK, NB])
        p_w = [s.ps(f"p_w{k}") for k in range(DK)]
        s_load, s_mm, s_t, s_x = (s.sem(x) for x in ("load", "mm", "t_", "x"))
        X, MOD = g["X"], g["MOD"]

        def blocks(eng):
            with eng.Fori(0, B) as b:
                with eng.Fori(0, NBLK) as c:
                    yield b, c, b * NBLK + c

        with nc.Block() as block:
            @block.sync
            def _(sp):
                sp.dma_start(wo[:, :, :], d["wo16"].rearrange("(k p) n -> p k n", p=P)).then_inc(s_load, 16)
                sp.dma_start(bo[:, :], d["bo"]).then_inc(s_load, 16)

            @block.tensor
            def _(pe):
                pe.wait_ge(s_load, ONE + 32)
                for b, c, i in blocks(pe):
                    for n in range(DK):
                        pe.wait_ge(s_t, ONE + upto(i, DK, n))
                        for k in range(A_G):
                            ins = pe.matmul(p_w[n][:, :], wo[:, k, n * P:(n + 1) * P], OA[:, bass.ds(b * A_G + k, 1), bass.ds(c * NB, NB)],
                                            start=(k == 0), stop=(k == A_G - 1))
                        ins.then_inc(s_mm, 1)

            @block.scalar
            def _(act):
                act.wait_ge(s_load, ONE + 32)
                for b, c, i in blocks(act):
                    for n in range(DK):
                        act.wait_ge(s_mm, ONE + upto(i, DK, n + 1))
                        act.wait_ge(s_x, ONE + upto(i, DK, n))
                        act.activation(t_[:, n, :], p_w[n][:, :], ACT.Identity, bias=bo[:, n:n + 1]).then_inc(s_t, 1)

            @block.vector
            def _(dve):
                for b, c, i in blocks(dve):
                    for n in range(DK):
                        dve.wait_ge(s_t, ONE + upto(i, DK, n + 1))
                        x = X[:, n, bass.ds(b * T + c * NB, NB)]
                        dve.scalar_tensor_tensor(x, t_[:, n, :], MOD[:, 0, bass.ds(b, 1), 4 + n], x, ALU.mult,
                                                 ALU.add).then_inc(s_x, 1)


def routing_stage(nc, g, d):
    with ExitStack() as ctx:
        s = Scope(nc, ctx, "ro")
        CH = T // 16
        S, t, e, sc, gt, eq, cs, sel, f, one = (s.sb(n, [P, CH]) for n in "S t e sc gt eq cs sel f one".split())
        blk, low = s.sb("blk", [P, P]), s.sb("low", [P, P])
        rc = s.sb("rc", [P, 4])
        bits = s.sb("bits", [P, 32], I32)
        mx, u, nm, sm, L, Tt, C, cnt, tk, need = (s.sb(n, [P, 1]) for n in "mx u nm sm L Tt C cnt tk need".split())
        row, row8, rowr = s.sb("row", [1, P]), s.sb("row8", [1, 8]), s.sb("rowr", [1, P])
        slots, fs = s.sb("slots", [8, T]), s.sb("fs", [8, T])
        p_row, p_one, p_t = s.ps("p_row"), s.ps("p_one"), s.ps("p_t")
        names = "load v a pe low ini it_v it_a it_pe bi_v bi_pe end_v end_pe st ld tr fin".split()
        (s_load, s_v, s_a, s_pe, s_low, s_ini, s_iv, s_ia, s_ip, s_bv, s_bp, s_ev, s_ep, s_st, s_ld, s_tr,
         s_fin) = (s.sem(x) for x in names)
        NBITS = 30

        with nc.Block() as block:
            @block.sync
            def _(sp):
                sp.dma_start(S[:, :], g["s_dram"].rearrange("r (a c) -> (r a) c", c=CH)).then_inc(s_load, 16)
                for dst, name in ((blk, "blk16"), (low, "low16"), (rc, "rc"), (bits, "bits")):
                    sp.dma_start(dst[:, :], d[name]).then_inc(s_load, 16)
                sp.wait_ge(s_fin, ONE + 1)
                sp.dma_start(g["slot_dram"].rearrange("r (a c) -> (r a) c", c=CH), cs[:, :]).then_inc(s_st, 16)
                sp.dma_start(g["f_dram"].rearrange("r (a c) -> (r a) c", c=CH), f[:, :]).then_inc(s_st, 16)
                sp.wait_ge(s_st, ONE + 32)
                sp.dma_start(slots[:, :], g["slot_dram"]).then_inc(s_ld, 16)
                sp.dma_start(fs[:, :], g["f_dram"]).then_inc(s_ld, 16)

            @block.gpsimd
            def _(pool):
                pool.memset(one[:, :], 1.0).then_inc(s_ini, 1)
                pool.memset(Tt[:, :], 0.0).then_inc(s_ini, 1)
                pool.wait_ge(s_ini, ONE + 2)

            @block.tensor
            def _(pe):
                pe.wait_ge(s_load, ONE + 80)
                pe.wait_ge(s_v, ONE + 1)
                pe.matmul(p_row[0:1, 0:P], mx[:, :], g["ident"][:, :], start=True, stop=True).then_inc(s_pe, 1)
                pe.wait_ge(s_v, ONE + 3)
                pe.wait_ge(s_ini, ONE + 2)
                pe.matmul(p_one[:, 0:1], rowr[:, :], one[0:1, 0:1], start=True, stop=True).then_inc(s_pe, 1)
                pe.wait_ge(s_v, ONE + 5)
                with pe.Fori(0, N_ITERS - 1) as i:
                    pe.wait_ge(s_ia, ONE + 2 * i + 1)
                    pe.matmul(p_one[:, 0:1], blk[:, :], sm[:, :], start=True, stop=True).then_inc(s_ip, 1)
                pe.wait_ge(s_iv, ONE + 3 * (N_ITERS - 1))
                with pe.Fori(0, NBITS) as i:
                    pe.wait_ge(s_bv, ONE + 4 * i + 2)
                    pe.matmul(p_one[:, 0:1], blk[:, :], cnt[:, :], start=True, stop=True).then_inc(s_bp, 1)
                pe.wait_ge(s_ev, ONE + 1)
                pe.matmul(p_one[:, 0:1], blk[:, :], cnt[:, :], start=True, stop=True).then_inc(s_ep, 1)
                pe.wait_ge(s_ev, ONE + 4)
                pe.matmul(p_one[:, 0:1], low[:, :], cs[:, CH - 1:CH], start=True, stop=True).then_inc(s_ep, 1)
                pe.wait_ge(s_ev, ONE + 8)
                pe.matmul(p_one[:, 0:1], low[:, :], cs[:, CH - 1:CH], start=True, stop=True).then_inc(s_ep, 1)
                pe.wait_ge(s_ld, ONE + 32)
                for n, src in enumerate((slots, fs)):
                    for k in range(T // P):
                        ins = pe.transpose(p_t[:, n * 64 + k * 8:n * 64 + k * 8 + 8], src[:, k * P:(k + 1) * P],
                                           g["ident"][0:8, 0:8])
                ins.then_inc(s_tr, 1)

            @block.scalar
            def _(act):
                act.preload_act_table_set(LN_EXP)
                with act.Fori(0, N_ITERS - 1) as i:
                    act.wait_ge(s_iv, ONE + 3 * i + 2)
                    act.activation(e[:, :], t[:, :], ACT.Exp, bias=nm[:, :], accum_out=sm[:, :]).then_inc(s_ia, 1)
                    act.wait_ge(s_ip, ONE + i + 1)
                    act.activation(L[:, :], p_one[:, 0:1], ACT.Ln).then_inc(s_ia, 1)
                act.wait_ge(s_v, ONE + 6)
                act.activation(sc[:, :], t[:, :], ACT.Exp).then_inc(s_a, 1)

            @block.vector
            def _(dve):
                link = Chain(dve, s_v, 0, 6)
                dve.wait_ge(s_load, ONE + 80)
                dve.wait_ge(s_ini, ONE + 2)
                link(dve.tensor_reduce(mx[:, :], S[:, :], AX_X, ALU.max))
                dve.wait_ge(s_pe, ONE + 1)
                link(dve.tensor_reduce(row8[:, :], p_row[0:1, 0:P].rearrange("p (r a) -> p r a", a=16), AX_X, ALU.max))
                link(dve.tensor_copy(rowr[:, :].rearrange("p (r a) -> p r a", a=16),
                                     row8[:, :].rearrange("p (r a) -> p r a", a=1).to_broadcast([1, 8, 16])))
                dve.wait_ge(s_pe, ONE + 2)
                link(dve.tensor_copy(mx[:, :], p_one[:, 0:1]))
                link(dve.tensor_copy(u[:, :], rc[:, 0:1]))
                with dve.Fori(0, N_ITERS - 1) as i:
                    dve.tensor_scalar(t[:, :], S[:, :], u[:, :], None, ALU.min).then_inc(s_iv, 1)
                    dve.tensor_scalar(nm[:, :], mx[:, :], u[:, :], -1.0, ALU.min, ALU.mult).then_inc(s_iv, 1)
                    dve.wait_ge(s_iv, ONE + 3 * i + 2)
                    dve.wait_ge(s_ia, ONE + 2 * i + 2)
                    dve.tensor_scalar(u[:, :], L[:, :], nm[:, :], rc[:, 1:2], ALU.subtract, ALU.subtract).then_inc(s_iv, 1)
                    dve.wait_ge(s_iv, ONE + 3 * i + 3)
                link(dve.tensor_scalar(t[:, :], S[:, :], u[:, :], 0.0, ALU.subtract, ALU.min))
                link.close()
                dve.wait_ge(s_a, ONE + 1)
                with dve.Fori(0, NBITS) as i:
                    dve.tensor_tensor(C[:, :].bitcast(I32), Tt[:, :].bitcast(I32), bits[:, bass.ds(i, 1)],
                                      ALU.bitwise_or).then_inc(s_bv, 1)
                    dve.wait_ge(s_bv, ONE + 4 * i + 1)
                    dve.tensor_scalar(gt[:, :], sc[:, :], C[:, :], 0.0, ALU.is_ge, ALU.add,
                                      accum_out=cnt[:, :]).then_inc(s_bv, 1)
                    dve.wait_ge(s_bp, ONE + i + 1)
                    dve.wait_ge(s_bv, ONE + 4 * i + 2)
                    dve.tensor_scalar(tk[:, :], p_one[:, 0:1], rc[:, 2:3], None, ALU.is_ge).then_inc(s_bv, 1)
                    dve.wait_ge(s_bv, ONE + 4 * i + 3)
                    dve.scalar_tensor_tensor(Tt[:, :], C[:, :], tk[:, :], Tt[:, :], ALU.mult, ALU.max).then_inc(s_bv, 1)
                    dve.wait_ge(s_bv, ONE + 4 * i + 4)
                end = Chain(dve, s_ev, 0, 11)
                end(dve.tensor_scalar(gt[:, :], sc[:, :], Tt[:, :], 0.0, ALU.is_gt, ALU.add, accum_out=cnt[:, :]))
                end(dve.tensor_scalar(eq[:, :], sc[:, :], Tt[:, :], None, ALU.is_equal))
                dve.wait_ge(s_ep, ONE + 1)
                end(dve.tensor_scalar(need[:, :], p_one[:, 0:1], -1.0, rc[:, 2:3], ALU.mult, ALU.add))
                end(dve.tensor_tensor_scan(cs[:, :], one[:, :], eq[:, :], 0.0, ALU.mult, ALU.add))
                dve.wait_ge(s_ep, ONE + 2)
                end(dve.tensor_scalar(sel[:, :], cs[:, :], p_one[:, 0:1], need[:, :], ALU.add, ALU.is_le))
                end(dve.tensor_tensor(sel[:, :], sel[:, :], eq[:, :], ALU.mult))
                end(dve.tensor_tensor(sel[:, :], sel[:, :], gt[:, :], ALU.add))
                end(dve.tensor_tensor_scan(cs[:, :], one[:, :], sel[:, :], 0.0, ALU.mult, ALU.add))
                dve.wait_ge(s_ep, ONE + 3)
                end(dve.scalar_tensor_tensor(cs[:, :], cs[:, :], p_one[:, 0:1], sel[:, :], ALU.add, ALU.mult))
                end(dve.tensor_scalar(cs[:, :], cs[:, :], -1.0, None, ALU.add))
                end(dve.tensor_scalar(f[:, :], sc[:, :], -1.0, 1.0, ALU.mult, ALU.add))
                end.close()
                dve.tensor_tensor(f[:, :], f[:, :], sc[:, :], ALU.add).then_inc(s_fin, 1)
                dve.wait_ge(s_tr, ONE + 1)
                dve.tensor_copy(g["SLOT"][:, :], p_t[:, 0:64]).then_inc(s_low, 1)
                dve.tensor_copy(g["FAC"][:, :], p_t[:, 64:128]).then_inc(s_low, 1)


def window_stage(nc, g, d, tag, local, layer=0):
    with ExitStack() as ctx:
        s = Scope(nc, ctx, tag)
        KW = 2 * WIN if local else WIN
        RN = 2 if local else 1
        MH = HM // RN
        wq, wk, wv = (s.sb(n, [P, DK, HID]) for n in ("wq", "wk", "wv"))
        wo = s.sb("wo", [P, HM, D])
        gx = s.sb("gx", [P, DK, WIN])
        qt = s.sb("qt", [P, HM, WIN])
        kt = s.sb("kt", [P, HM, 2, WIN])
        v = s.sb("v", [P, 2, HID])
        pr = s.sb("pr", [P, 2, MH, KW])
        pt = s.sb("pt", [P, 2, 512])
        os_ = s.sb("os", [P, HM, WIN])
        nm, sm = s.sb("nm", [P, 2, MH]), s.sb("sm", [P, 2, MH])
        p_p, p_v, p_t, p_o = s.ps("p_p"), s.ps("p_v"), s.ps("p_t"), s.ps("p_o")
        p_s = [s.ps(f"p_s{e}") for e in range(2)]
        names = "load ini gx pq pk pv qe ke ve sc mx ex rs pr tr te o oe wo out ss ro sq x1 n a rt rn".split()
        (s_load, s_ini, s_gx, s_pq, s_pk, s_pv, s_qe, s_ke, s_ve, s_sc, s_mx, s_ex, s_rs, s_pr, s_tr, s_te,
         s_o, s_oe, s_wo, s_out, s_ss, s_ro, s_sq, s_x1, s_n, s_a, s_rt, s_rn) = (s.sem(x) for x in names)
        X, Y, Z, MOD = g["X"], g["Y"], g.get("Z"), g["MOD"]
        if local:
            gam = s.sb("gam", [P, 2])
            mask = s.sb("mask", [P, 5, KW], BF16)
            idb = s.sb("idb", [P, P], BF16)
            tab = s.sb("tab", [P, 4, T])
            sq, xe, n2, ta, tb = (s.sb(n, [P, 2, 512]) for n in ("sq", "xe", "n2", "ta", "tb"))
            p_ss, p_ro = s.ps("p_ss"), s.ps("p_ro")
            loads = ((wq, "lwq"), (wk, "lwk"), (wv, "lwv"))
            NLOAD = 8
        else:
            gam = s.sb("gam", [P, DK])
            NLOAD = 5

        def windows(eng):
            with eng.Fori(0, B) as b:
                with eng.Fori(0, NW // 2) as c:
                    for u in range(2):
                        yield b, c, u, b * NW + c * 2 + u

        def off(c, u):
            return c * 2 * WIN + u * WIN

        with nc.Block() as block:
            @block.sync
            def _(sp):
                src = d["local"][layer] if local else d["light"]
                for dst, name in ((wq, "wq"), (wk, "wk"), (wv, "wv"), (wo, "wo")):
                    sp.dma_start(dst[:, :, :], src[name].rearrange("(k p) n -> p k n", p=P)).then_inc(s_load, 16)
                sp.dma_start(gam[:, :], src["gam"]).then_inc(s_load, 16)
                if local:
                    sp.dma_start(mask[:, :, :], d["mask"]).then_inc(s_load, 16)
                    sp.dma_start(idb[:, :], d["idb"]).then_inc(s_load, 16)
                    sp.dma_start(tab[:, :, :], d["tab"]).then_inc(s_load, 16)

            @block.gpsimd
            def _(pool):
                pool.wait_ge(s_load, ONE + 16 * NLOAD)
                pool.memset(kt[:, :, :, :], 0.0).then_inc(s_ini, 1)
                pool.memset(v[:, :, :], 0.0).then_inc(s_ini, 1)
                pool.wait_ge(s_ini, ONE + 2)
                for b, c, u, i in windows(pool):
                    pool.wait_ge(s_pv, ONE + i)
                    for k in range(DK):
                        if local:
                            ins = pool.tensor_copy(gx[:, k, :], Y[:, k, col(b, off(c, u) - k, WIN)])
                        else:
                            ins = pool.tensor_tensor(gx[:, k, :], Y[:, k, col(b, off(c, u), WIN)],
                                                     gam[:, k:k + 1].to_broadcast([P, WIN]), ALU.mult)
                    ins.then_inc(s_gx, 1)
                    if local:
                        for x in range(2):
                            pool.wait_ge(s_x1, ONE + upto(i, 2, x + 1))
                            pool.wait_ge(s_rt, ONE + upto(i, 2, x))
                            t_ = tab[:, 2 * x:2 * x + 1, bass.ds(c * 2 * WIN + u * WIN, WIN)].to_broadcast([P, HM, WIN])
                            pool.tensor_tensor(ta[:, x].rearrange("p (m n) -> p m n", m=HM),
                                               xe[:, x].rearrange("p (m n) -> p m n", m=HM), t_, ALU.mult).then_inc(s_a, 1)

            @block.tensor
            def _(pe):
                pe.wait_ge(s_load, ONE + 16 * NLOAD)
                pe.wait_ge(s_ini, ONE + 2)
                for b, c, u, i in windows(pe):
                    pe.wait_ge(s_gx, ONE + i + 1)
                    for x, (w, sem) in enumerate(((wq, s_pq), (wk, s_pk))):
                        pe.wait_ge(s_ke if x == 0 else s_qe, ONE + i + x)
                        for m in range(HM):
                            for k in range(DK):
                                ins = pe.matmul(p_p[:, m * WIN:(m + 1) * WIN], w[:, k, m * P:(m + 1) * P], gx[:, k, :],
                                                start=(k == 0), stop=(k == DK - 1))
                        ins.then_inc(sem, 1)
                        if local:
                            pe.wait_ge(s_sq, ONE + upto(i, 2, x + 1))
                            pe.matmul(p_ss[:, :], g["blk64"][:, :], sq[:, x, :], start=True, stop=True).then_inc(s_ss, 1)
                            pe.wait_ge(s_x1, ONE + upto(i, 2, x + 1))
                            pe.matmul(p_ro[:, :], g["rot64"][:, :], xe[:, x, :], start=True, stop=True).then_inc(s_ro, 1)
                    pe.wait_ge(s_out, ONE + i)
                    for k in range(DK):
                        ins = pe.matmul(p_v[:, :], gx[:, k, :], wv[:, k, :], start=(k == 0), stop=(k == DK - 1))
                    ins.then_inc(s_pv, 1)
                    pe.wait_ge(s_qe, ONE + i + 1)
                    pe.wait_ge(s_ke, ONE + i + 1)
                    for r in range(RN):
                        for e in range(2):
                            pe.wait_ge(s_ex, ONE + upto(i, 8, 8 // RN * r))
                            rows = slice(64 * e, 64 * e + 64)
                            for mi in range(MH):
                                m = r * MH + mi
                                out = p_s[e][:, mi * KW:(mi + 1) * KW]
                                if local:
                                    mk = mask[:, bass.ds(c, 1), :] if u == 0 else mask[:, 4, :]
                                    pe.matmul(out, idb[:, :], mk, start=True, stop=False)
                                    ins = pe.matmul(out, qt[rows, m, :], kt[rows, m, :, :], start=False, stop=True)
                                else:
                                    ins = pe.matmul(out, qt[rows, m, :], kt[rows, m, 0, :], start=True, stop=True)
                            ins.then_inc(s_sc, 1)
                        for e in range(2):
                            j = 2 * r + e
                            pe.wait_ge(s_pr, ONE + upto(i, 2 * RN, j + 1))
                            pe.wait_ge(s_te, ONE + upto(i, 2 * RN, j))
                            flat = pr[:, e, :, :].rearrange("p m n -> p (m n)")
                            for x in range(4):
                                ins = pe.transpose(p_t[:, x * P:(x + 1) * P], flat[:, x * P:(x + 1) * P], g["ident"][:, :])
                            ins.then_inc(s_tr, 1)
                            pe.wait_ge(s_te, ONE + upto(i, 2 * RN, j + 1))
                            if j == 0:
                                pe.wait_ge(s_ve, ONE + i + 1)
                                pe.wait_ge(s_oe, ONE + i)
                            for mi in range(MH):
                                m = r * MH + mi
                                h = 2 * m + e
                                for x in range(KW // P):
                                    ins = pe.matmul(p_o[64 * e:64 * e + 64, m * WIN:(m + 1) * WIN],
                                                    v[:, x, h * DH:(h + 1) * DH],
                                                    pt[:, j % 2, (mi * (KW // P) + x) * P:(mi * (KW // P) + x + 1) * P],
                                                    start=(x == 0), stop=(x == KW // P - 1), tile_position=(0, 64 * e))
                            ins.then_inc(s_o, 1)
                    pe.wait_ge(s_oe, ONE + i + 1)
                    for n in range(DK):
                        for k in range(HM):
                            ins = pe.matmul(p_v[:, n * WIN:(n + 1) * WIN], wo[:, k, n * P:(n + 1) * P], os_[:, k, :],
                                            start=(k == 0), stop=(k == HM - 1))
                    ins.then_inc(s_wo, 1)

            @block.scalar
            def _(act):
                act.preload_act_table_set(LN_EXP)
                act.wait_ge(s_load, ONE + 16 * NLOAD)
                act.wait_ge(s_ini, ONE + 2)
                for b, c, u, i in windows(act):
                    slot = u if local else 0
                    if local:
                        for x in range(2):
                            act.wait_ge(s_pq if x == 0 else s_pk, ONE + i + 1)
                            act.wait_ge(s_ss, ONE + upto(i, 2, x))
                            act.activation(sq[:, x, :], p_p[:, :], ACT.Square).then_inc(s_sq, 1)
                            act.wait_ge(s_a, ONE + upto(i, 2, x))
                            act.activation(xe[:, x, :], p_p[:, :], ACT.Copy, scale=gam[:, x:x + 1]).then_inc(s_x1, 1)
                            act.wait_ge(s_n, ONE + upto(i, 2, x + 1))
                            act.activation(n2[:, x, :], n2[:, x, :], ACT.Ln, scale=float(2 ** LN_SHIFT)).then_inc(s_rn, 1)
                            act.wait_ge(s_rn, ONE + upto(i, 4, 2 * x + 1))
                            act.activation(n2[:, x, :], n2[:, x, :], ACT.Exp, scale=-0.5,
                                           bias=g["bias"][:, 2 - x:3 - x]).then_inc(s_rn, 1)
                    else:
                        act.wait_ge(s_pq, ONE + i + 1)
                        act.wait_ge(s_sc, ONE + 2 * RN * i)
                        act.activation(qt[:, :, :].rearrange("p m n -> p (m n)"), p_p[:, :], ACT.Copy,
                                       scale=float(DH) ** -0.5).then_inc(s_qe, 1)
                    act.wait_ge(s_pv, ONE + i + 1)
                    act.wait_ge(s_o, ONE + 2 * RN * i)
                    act.activation(v[:, slot, :], p_v[:, :], ACT.Copy).then_inc(s_ve, 1)
                    for r in range(RN):
                        for e in range(2):
                            j = 2 * r + e
                            act.wait_ge(s_mx, ONE + upto(i, 2 * RN, j + 1))
                            act.wait_ge(s_tr, ONE + (upto(i, 2 * RN, max(j - 1, 0)) if j < 2 else upto(i, 2 * RN, j - 1)))
                            for mi in range(MH):
                                act.activation(pr[:, e, mi, :], p_s[e][:, mi * KW:(mi + 1) * KW], ACT.Exp,
                                               bias=nm[:, e, mi:mi + 1], accum_out=sm[:, e, mi:mi + 1]).then_inc(s_ex, 1)
                    act.wait_ge(s_o, ONE + upto(i, 2 * RN, 2 * RN))
                    act.wait_ge(s_wo, ONE + i)
                    act.activation(os_[:, :, :].rearrange("p m n -> p (m n)"), p_o[:, :], ACT.Copy).then_inc(s_oe, 1)

            @block.vector
            def _(dve):
                dve.wait_ge(s_load, ONE + 16 * NLOAD)
                dve.wait_ge(s_ini, ONE + 2)
                for b, c, u, i in windows(dve):
                    slot = u if local else 0
                    if local:
                        for x in range(2):
                            dve.wait_ge(s_ss, ONE + upto(i, 2, x + 1))
                            dve.tensor_scalar(n2[:, x, :], p_ss[:, :], NORM2_MIN, None, ALU.max).then_inc(s_n, 1)
                            dve.wait_ge(s_ro, ONE + upto(i, 2, x + 1))
                            t_ = tab[:, 2 * x + 1:2 * x + 2, bass.ds(c * 2 * WIN + u * WIN, WIN)].to_broadcast([P, HM, WIN])
                            dve.tensor_tensor(tb[:, x].rearrange("p (m n) -> p m n", m=HM),
                                              p_ro[:, :].rearrange("p (m n) -> p m n", m=HM), t_, ALU.mult).then_inc(s_rt, 1)
                            dve.wait_ge(s_rt, ONE + upto(i, 2, x + 1))
                            dve.wait_ge(s_a, ONE + upto(i, 2, x + 1))
                            dve.tensor_tensor(tb[:, x, :], tb[:, x, :], ta[:, x, :], ALU.add).then_inc(s_rs, 1)
                            dve.wait_ge(s_rs, ONE + upto(i, 2 + 2 * RN, x + 1))
                            dve.wait_ge(s_rn, ONE + upto(i, 4, 2 * x + 2))
                            dst = qt[:, :, :] if x == 0 else kt[:, :, slot, :]
                            dve.tensor_tensor(dst, tb[:, x].rearrange("p (m n) -> p m n", m=HM),
                                              n2[:, x].rearrange("p (m n) -> p m n", m=HM),
                                              ALU.mult).then_inc(s_qe if x == 0 else s_ke, 1)
                    else:
                        dve.wait_ge(s_pk, ONE + i + 1)
                        dve.wait_ge(s_sc, ONE + 2 * RN * i)
                        dve.tensor_copy(kt[:, :, 0, :], p_p[:, :].rearrange("p (m n) -> p m n", m=HM)).then_inc(s_ke, 1)
                    for r in range(RN):
                        for e in range(2):
                            j = 2 * r + e
                            dve.wait_ge(s_sc, ONE + upto(i, 2 * RN, j + 1))
                            dve.wait_ge(s_ex, ONE + upto(i, 8, max(0, (j - 1) * MH)))
                            dve.tensor_reduce(nm[:, e, :], p_s[e][:, :].rearrange("p (m n) -> p m n", m=MH), AX_X,
                                              ALU.max, negate=True).then_inc(s_mx, 1)
                        for e in range(2):
                            j = 2 * r + e
                            dve.wait_ge(s_ex, ONE + upto(i, 8, (j + 1) * MH))
                            dve.reciprocal(sm[:, e, :], sm[:, e, :]).then_inc(s_rs, 1)
                            dve.wait_ge(s_rs, ONE + (upto(i, (2 if local else 0) + 2 * RN, (2 if local else 0) + j + 1)))
                            dve.tensor_tensor(pr[:, e, :, :], pr[:, e, :, :],
                                              sm[:, e, :].rearrange("p (m o) -> p m o", o=1).to_broadcast([P, MH, KW]),
                                              ALU.mult).then_inc(s_pr, 1)
                        for e in range(2):
                            j = 2 * r + e
                            dve.wait_ge(s_tr, ONE + upto(i, 2 * RN, j + 1))
                            dve.wait_ge(s_o, ONE + upto(i, 2 * RN, max(0, j - 1)))
                            dve.tensor_copy(pt[:, j % 2, :], p_t[:, :]).then_inc(s_te, 1)
                    dve.wait_ge(s_wo, ONE + i + 1)
                    if local:
                        dve.tensor_tensor(Z[:, :, col(b, off(c, u), WIN)], Y[:, :, col(b, off(c, u), WIN)],
                                          p_v[:, 0:DK * WIN].rearrange("p (n t) -> p n t", n=DK), ALU.add).then_inc(s_out, 1)
                    else:
                        for n in range(DK):
                            x = X[:, n, bass.ds(b * T + off(c, u), WIN)]
                            ins = dve.scalar_tensor_tensor(x, p_v[:, n * WIN:(n + 1) * WIN], MOD[:, 0, bass.ds(b, 1), 10 + n],
                                                           x, ALU.mult, ALU.add)
                        ins.then_inc(s_out, 1)


def routed_stage(nc, g, d):
    with ExitStack() as ctx:
        s = Scope(nc, ctx, "rt")
        NTL = T // P
        wq, wk, wv = (s.sb(n, [P, DK, HID]) for n in ("wq", "wk", "wv"))
        wo = s.sb("wo", [P, HM, D])
        gam = s.sb("gam", [P, DK])
        hb = s.sb("hb", [P, DK, T])
        xt = s.sb("xt", [P, NTL, D])
        gk, gq = s.sb("gk", [P, NTL, NKV]), s.sb("gq", [P, NTL, NQ])
        ck, cq = s.sb("ck", [P, DK, NKV]), s.sb("cq", [P, DK, NQ])
        fs = s.sb("fs", [P, NKV // P])
        kT, qT = s.sb("kT", [P, HM, NKV]), s.sb("qT", [P, HM, NQ])
        v = s.sb("v", [P, NKV // P, HID])
        pr, pt = s.sb("pr", [P, 2, NKV]), s.sb("pt", [P, 2, NKV])
        nm, sm = s.sb("nm", [P, 2]), s.sb("sm", [P, 2])
        os_ = s.sb("os", [P, 2, HM, P])
        rt = s.sb("rt", [P, 2, D])
        sb_, fb = s.sb("sb", [P, T]), s.sb("fb", [P, T])
        st = s.sb("st", [P, 2, T])
        iota, iop = s.sb("iota", [P, NKV]), s.sb("iop", [P, 2])
        pa = [s.ps(f"pa{i}") for i in range(2)]
        ps, p_t, p_o, p_f = [s.ps(f"ps{i}") for i in range(2)], s.ps("p_t"), s.ps("p_o"), s.ps("p_f")
        names = "load in tr te oh ga ge f fe pj pe sc mx ex rs pr tp tc o oe r re st x out".split()
        (s_load, s_in, s_tr, s_te, s_oh, s_ga, s_ge, s_f, s_fe, s_pj, s_pe, s_sc, s_mx, s_ex, s_rs, s_pr,
         s_tp, s_tc, s_o, s_oe, s_r, s_re, s_st, s_x, s_out) = (s.sem(x) for x in names)
        X, Y, MOD, SLOT, FAC = g["X"], g["Y"], g["MOD"], g["SLOT"], g["FAC"]
        NU = 2 * HEADS

        with nc.Block() as block:
            @block.sync
            def _(sp):
                src = d["heavy"]
                for dst, name in ((wq, "wq"), (wk, "wk"), (wv, "wv"), (wo, "wo")):
                    sp.dma_start(dst[:, :, :], src[name].rearrange("(k p) n -> p k n", p=P)).then_inc(s_load, 16)
                for dst, a in ((gam, src["gam"]), (iota, d["iota"]), (iop, d["iop"])):
                    sp.dma_start(dst[:, :], a).then_inc(s_load, 16)
                with sp.Fori(0, B) as b:
                    sp.wait_ge(s_out, ONE + 4 * b)
                    sp.dma_start(hb[:, :, :], Y[:, :, col(b, 0, T)]).then_inc(s_in, 16)
                    sp.dma_start(sb_[:, :], g["slot_dram"][bass.ds(2 * b, 1), :].to_broadcast([P, T])).then_inc(s_in, 16)
                    sp.dma_start(fb[:, :], g["f_dram"][bass.ds(2 * b, 1), :].to_broadcast([P, T])).then_inc(s_in, 16)

            @block.tensor
            def _(pe):
                pe.wait_ge(s_load, ONE + 16 * 7)
                with pe.Fori(0, B) as b:
                    pe.wait_ge(s_in, ONE + 48 * b + 48)
                    pe.wait_ge(s_x, ONE + 4 * b)
                    for n in range(4):
                        if n >= 2:
                            pe.wait_ge(s_te, ONE + upto(b, 4, n - 1))
                        for q in range(2):
                            for k in range(DK):
                                t = 2 * n + q
                                ins = pe.transpose(pa[n % 2][:, q * D + k * P:q * D + (k + 1) * P], hb[:, k, t * P:(t + 1) * P],
                                                   g["ident"][:, :])
                        ins.then_inc(s_tr, 1)
                    pe.wait_ge(s_te, ONE + upto(b, 4, 4))
                    pe.wait_ge(s_oh, ONE + 2 * NTL * b + 2 * NTL)
                    for k in range(DK):
                        for t in range(NTL):
                            ins = pe.matmul(pa[k][:, :], xt[:, t, k * P:(k + 1) * P], gk[:, t, :], start=(t == 0), stop=(t == NTL - 1))
                        ins.then_inc(s_ga, 1)
                    for k in range(DK):
                        for t in range(NTL):
                            ins = pe.matmul(ps[0][:, k * NQ:(k + 1) * NQ], xt[:, t, k * P:(k + 1) * P], gq[:, t, :],
                                            start=(t == 0), stop=(t == NTL - 1))
                    ins.then_inc(s_ga, 1)
                    for m in range(NKV // P):
                        for t in range(NTL):
                            ins = pe.matmul(p_f[:, m:m + 1], gk[:, t, m * P:(m + 1) * P], FAC[:, bass.ds(t * 8 + 2 * b + 1, 1)],
                                            start=(t == 0), stop=(t == NTL - 1))
                    ins.then_inc(s_f, 1)
                    pe.wait_ge(s_ge, ONE + upto(b, 3, 3))
                    pe.wait_ge(s_fe, ONE + b + 1)
                    n = 0
                    for m in range(HM):
                        if n >= 2:
                            pe.wait_ge(s_pe, ONE + upto(b, 10, n - 1))
                        for k in range(DK):
                            ins = pe.matmul(pa[n % 2][:, :], wk[:, k, m * P:(m + 1) * P], ck[:, k, :], start=(k == 0), stop=(k == DK - 1))
                        ins.then_inc(s_pj, 1)
                        n += 1
                    for m in range(NKV // P):
                        pe.wait_ge(s_pe, ONE + upto(b, 10, n - 1))
                        for k in range(DK):
                            ins = pe.matmul(pa[n % 2][:, :], ck[:, k, m * P:(m + 1) * P], wv[:, k, :], start=(k == 0), stop=(k == DK - 1))
                        ins.then_inc(s_pj, 1)
                        n += 1
                    for m2 in range(2):
                        pe.wait_ge(s_pe, ONE + upto(b, 10, n - 1))
                        for m in (2 * m2, 2 * m2 + 1):
                            for k in range(DK):
                                ins = pe.matmul(pa[n % 2][:, (m % 2) * NQ:(m % 2 + 1) * NQ], wq[:, k, m * P:(m + 1) * P], cq[:, k, :],
                                                start=(k == 0), stop=(k == DK - 1))
                        ins.then_inc(s_pj, 1)
                        n += 1
                    pe.wait_ge(s_pe, ONE + upto(b, 10, 10))

                    def score(j):
                        qt_, h = divmod(j, HEADS)
                        m, e = divmod(h, 2)
                        rows = slice(64 * e, 64 * e + 64)
                        if j >= 2:
                            pe.wait_ge(s_ex, ONE + upto(b, NU, j - 1))
                        pe.matmul(ps[j % 2][:, :], qT[rows, m, qt_ * P:(qt_ + 1) * P], kT[rows, m, :], start=True, stop=True)\
                          .then_inc(s_sc, 1)

                    score(0)
                    for j in range(NU):
                        qt_, h = divmod(j, HEADS)
                        m, e = divmod(h, 2)
                        if j + 1 < NU:
                            score(j + 1)
                        pe.wait_ge(s_pr, ONE + upto(b, NU, j + 1))
                        pe.wait_ge(s_tc, ONE + upto(b, NU, j))
                        for x in range(4):
                            ins = pe.transpose(p_t[:, x * P:(x + 1) * P], pr[:, j % 2, x * P:(x + 1) * P], g["ident"][:, :])
                        ins.then_inc(s_tp, 1)
                        pe.wait_ge(s_tc, ONE + upto(b, NU, j + 1))
                        if h == 0:
                            pe.wait_ge(s_oe, ONE + upto(b, 2, qt_))
                        for x in range(4):
                            ins = pe.matmul(p_o[64 * e:64 * e + 64, m * P:(m + 1) * P], v[:, x, h * DH:(h + 1) * DH],
                                            pt[:, j % 2, x * P:(x + 1) * P], start=(x == 0), stop=(x == 3), tile_position=(0, 64 * e))
                        ins.then_inc(s_o, 1)
                    for q in range(2):
                        pe.wait_ge(s_oe, ONE + upto(b, 2, q + 1))
                        for k in range(HM):
                            ins = pe.matmul(pa[q][:, 0:D], os_[:, q, k, :], wo[:, k, :], start=(k == 0), stop=(k == HM - 1))
                        ins.then_inc(s_r, 1)
                    pe.wait_ge(s_re, ONE + upto(b, 2, 2))
                    pe.wait_ge(s_st, ONE + upto(b, 2, 2))
                    n = 0
                    for k in range(DK):
                        for hf in range(2):
                            if n >= 2:
                                pe.wait_ge(s_x, ONE + upto(b, 4, n - 1))
                            for q in range(2):
                                ins = pe.matmul(pa[n % 2][:, :], rt[:, q, k * P:(k + 1) * P], st[:, q, hf * 512:(hf + 1) * 512],
                                                start=(q == 0), stop=(q == 1))
                            ins.then_inc(s_out, 1)
                            n += 1

            @block.scalar
            def _(act):
                act.wait_ge(s_load, ONE + 16 * 7)
                with act.Fori(0, B) as b:
                    for n in range(4):
                        act.wait_ge(s_tr, ONE + upto(b, 4, n + 1))
                        act.activation(xt[:, 2 * n:2 * n + 2, :].rearrange("p t n -> p (t n)"), pa[n % 2][:, :], ACT.Copy).then_inc(s_te, 1)
                    for k in range(DK):
                        act.wait_ge(s_ga, ONE + upto(b, 3, k + 1))
                        act.activation(ck[:, k, :], pa[k][:, :], ACT.Copy, scale=gam[:, k:k + 1]).then_inc(s_ge, 1)
                    act.wait_ge(s_ga, ONE + upto(b, 3, 3))
                    for k in range(DK):
                        ins = act.activation(cq[:, k, :], ps[0][:, k * NQ:(k + 1) * NQ], ACT.Copy, scale=gam[:, k:k + 1])
                    ins.then_inc(s_ge, 1)
                    for n in range(HM):
                        act.wait_ge(s_pj, ONE + upto(b, 10, n + 1))
                        act.activation(kT[:, n, :], pa[n % 2][:, :], ACT.Copy).then_inc(s_pe, 1)
                    act.wait_ge(s_fe, ONE + b + 1)
                    for n in range(NKV // P):
                        act.wait_ge(s_pj, ONE + upto(b, 10, n + 5))
                        act.activation(v[:, n, :], pa[n % 2][:, :], ACT.Copy, scale=fs[:, n:n + 1]).then_inc(s_pe, 1)
                    for n in range(2):
                        act.wait_ge(s_pj, ONE + upto(b, 10, n + 9))
                        act.activation(qT[:, 2 * n:2 * n + 2, :].rearrange("p m n -> p (m n)"), pa[n % 2][:, :], ACT.Copy,
                                       scale=float(DH) ** -0.5).then_inc(s_pe, 1)
                    for j in range(NU):
                        act.wait_ge(s_mx, ONE + upto(b, NU, j + 1))
                        if j >= 2:
                            act.wait_ge(s_tp, ONE + upto(b, NU, j - 1))
                        act.activation(pr[:, j % 2, :], ps[j % 2][:, :], ACT.Exp, bias=nm[:, j % 2:j % 2 + 1],
                                       accum_out=sm[:, j % 2:j % 2 + 1]).then_inc(s_ex, 1)
                        if j % HEADS == HEADS - 1:
                            q = j // HEADS
                            act.wait_ge(s_o, ONE + upto(b, NU, j + 1))
                            act.activation(os_[:, q, :, :].rearrange("p m n -> p (m n)"), p_o[:, :], ACT.Copy).then_inc(s_oe, 1)
                    for q in range(2):
                        act.wait_ge(s_r, ONE + upto(b, 2, q + 1))
                        act.activation(rt[:, q, :], pa[q][:, 0:D], ACT.Copy).then_inc(s_re, 1)

            @block.vector
            def _(dve):
                dve.wait_ge(s_load, ONE + 16 * 7)
                with dve.Fori(0, B) as b:
                    for t in range(NTL):
                        dve.tensor_scalar(gk[:, t, :], iota[:, :], SLOT[:, bass.ds(t * 8 + 2 * b + 1, 1)], None,
                                          ALU.is_equal).then_inc(s_oh, 1)
                        dve.tensor_scalar(gq[:, t, :], iota[:, 0:NQ], SLOT[:, bass.ds(t * 8 + 2 * b, 1)], None,
                                          ALU.is_equal).then_inc(s_oh, 1)
                    dve.wait_ge(s_in, ONE + 48 * b + 48)
                    for q in range(2):
                        dve.scalar_tensor_tensor(st[:, q, :], sb_[:, :], iop[:, q:q + 1], fb[:, :], ALU.is_equal,
                                                 ALU.mult).then_inc(s_st, 1)
                    dve.wait_ge(s_f, ONE + b + 1)
                    dve.tensor_copy(fs[:, :], p_f[:, 0:NKV // P]).then_inc(s_fe, 1)
                    for j in range(NU):
                        dve.wait_ge(s_sc, ONE + upto(b, NU, j + 1))
                        dve.tensor_reduce(nm[:, j % 2:j % 2 + 1], ps[j % 2][:, :], AX_X, ALU.max, negate=True).then_inc(s_mx, 1)
                        dve.wait_ge(s_ex, ONE + upto(b, NU, j + 1))
                        dve.reciprocal(sm[:, j % 2:j % 2 + 1], sm[:, j % 2:j % 2 + 1]).then_inc(s_rs, 1)
                        dve.wait_ge(s_rs, ONE + upto(b, NU, j + 1))
                        dve.tensor_scalar(pr[:, j % 2, :], pr[:, j % 2, :], sm[:, j % 2:j % 2 + 1], None, ALU.mult).then_inc(s_pr, 1)
                        dve.wait_ge(s_tp, ONE + upto(b, NU, j + 1))
                        if j >= 2:
                            dve.wait_ge(s_o, ONE + upto(b, NU, j - 1))
                        dve.tensor_copy(pt[:, j % 2, :], p_t[:, :]).then_inc(s_tc, 1)
                    n = 0
                    for k in range(DK):
                        for hf in range(2):
                            dve.wait_ge(s_out, ONE + upto(b, 4, n + 1))
                            x = X[:, k, bass.ds(b * T + hf * 512, 512)]
                            dve.scalar_tensor_tensor(x, pa[n % 2][:, :], MOD[:, 0, bass.ds(b, 1), 10 + k], x, ALU.mult,
                                                     ALU.add).then_inc(s_x, 1)
                            n += 1


def mixing_stage(nc, g, d):
    with ExitStack() as ctx:
        s = Scope(nc, ctx, "mx")
        wv, wr, wo = (s.sb(n, [P, DK, D]) for n in ("wv", "wr", "wo"))
        pv = s.sb("pv", [P, 3, DK])
        dd, om = s.sb("dd", [P, DK]), s.sb("om", [P, 2, DK])
        st = s.sb("st", [P, DK, TP])
        tv = s.sb("tv", [P, 2, DK, T])
        inp = s.sb("inp", [P, 2, DK, T])
        vv, rr, oo = (s.sb(n, [P, DK, 512]) for n in ("vv", "rr", "oo"))
        p_v, p_r, p_w = ([s.ps(f"{n}{k}") for k in range(DK)] for n in ("p_v", "p_r", "p_w"))
        names = "load ini d om scan t in v r ve re w oo x".split()
        s_load, s_ini, s_d, s_om, s_scan, s_t, s_in, s_v, s_r, s_ve, s_re, s_w, s_oo, s_x = (s.sem(x) for x in names)
        X, Y, MOD = g["X"], g["Y"], g["MOD"]

        with nc.Block() as block:
            @block.sync
            def _(sp):
                for dst, name in ((wv, "WvT"), (wr, "WrT"), (wo, "WoT")):
                    sp.dma_start(dst[:, :, :], d["mix"][name].rearrange("(k p) n -> p k n", p=P)).then_inc(s_load, 16)
                sp.dma_start(pv[:, :, :], d["mix"]["vec"]).then_inc(s_load, 16)

            @block.gpsimd
            def _(pool):
                pool.wait_ge(s_load, ONE + 64)
                pool.memset(st[:, :, 0:1], 0.0).then_inc(s_ini, 1)
                pool.tensor_scalar(om[:, :, :], pv[:, 1:3, :], -1.0, 1.0, ALU.mult, ALU.add).then_inc(s_om, 1)
                pool.wait_ge(s_om, ONE + 1)
                pool.wait_ge(s_ini, ONE + 1)
                with pool.Fori(0, B) as b:
                    for k in range(DK):
                        pool.wait_ge(s_scan, ONE + upto(b, DK, k + 1))
                        pool.wait_ge(s_in, ONE + 4 * b)
                        for n in range(2):
                            pool.tensor_tensor(tv[:, n, k, :], st[:, k, 0:T], om[:, n, k:k + 1].to_broadcast([P, T]), ALU.mult).then_inc(s_t, 1)

            @block.tensor
            def _(pe):
                pe.wait_ge(s_load, ONE + 64)
                with pe.Fori(0, B) as b:
                    pe.wait_ge(s_in, ONE + 4 * b + 4)
                    for c in range(2):
                        cs = slice(c * 512, (c + 1) * 512)
                        for m in range(DK):
                            pe.wait_ge(s_ve, ONE + upto(b, 4, 2 * c))
                            for k in range(DK):
                                ins = pe.matmul(p_v[m][:, :], wv[:, k, m * P:(m + 1) * P], inp[:, 0, k, cs], start=(k == 0), stop=(k == DK - 1))
                            ins.then_inc(s_v, 1)
                        for m in range(DK):
                            pe.wait_ge(s_re, ONE + upto(b, 4, 2 * c))
                            for k in range(DK):
                                ins = pe.matmul(p_r[m][:, :], wr[:, k, m * P:(m + 1) * P], inp[:, 1, k, cs], start=(k == 0), stop=(k == DK - 1))
                            ins.then_inc(s_r, 1)
                        pe.wait_ge(s_ve, ONE + upto(b, 4, 2 * c + 2))
                        for m in range(DK):
                            pe.wait_ge(s_oo, ONE + upto(b, 4, 2 * c))
                            for k in range(DK):
                                ins = pe.matmul(p_w[m][:, :], wo[:, k, m * P:(m + 1) * P], vv[:, k, :], start=(k == 0), stop=(k == DK - 1))
                            ins.then_inc(s_w, 1)

            @block.scalar
            def _(act):
                act.wait_ge(s_load, ONE + 64)
                act.activation(dd[:, :], pv[:, 0, :], ACT.Exp).then_inc(s_d, 1)
                act.wait_ge(s_d, ONE + 1)
                act.activation(dd[:, :], dd[:, :], ACT.Exp, scale=-1.0).then_inc(s_d, 1)
                with act.Fori(0, B) as b:
                    for c in range(2):
                        for m in range(DK):
                            act.wait_ge(s_v, ONE + upto(b, 4, 2 * c + m + 1))
                            act.wait_ge(s_w, ONE + upto(b, 4, 2 * c))
                            act.activation(vv[:, m, :], p_v[m][:, :], ACT.Copy).then_inc(s_ve, 1)
                        for m in range(DK):
                            act.wait_ge(s_r, ONE + upto(b, 4, 2 * c + m + 1))
                            act.wait_ge(s_oo, ONE + upto(b, 4, 2 * c))
                            act.activation(rr[:, m, :], p_r[m][:, :], ACT.Sigmoid).then_inc(s_re, 1)

            @block.vector
            def _(dve):
                dve.wait_ge(s_load, ONE + 64)
                dve.wait_ge(s_d, ONE + 2)
                dve.wait_ge(s_ini, ONE + 1)
                with dve.Fori(0, B) as b:
                    for k in range(DK):
                        dve.wait_ge(s_t, ONE + 4 * b)
                        dve.tensor_tensor_scan(st[:, k, 1:TP], dd[:, k:k + 1].to_broadcast([P, T]), Y[:, k, col(b, 0, T)],
                                               0.0, ALU.mult, ALU.add).then_inc(s_scan, 1)
                    dve.wait_ge(s_r, ONE + 4 * b)
                    for k in range(DK):
                        for n in range(2):
                            dve.wait_ge(s_t, ONE + upto(b, 4, 2 * k + n + 1))
                            dve.scalar_tensor_tensor(inp[:, n, k, :], Y[:, k, col(b, 0, T)], pv[:, n + 1, k:k + 1],
                                                     tv[:, n, k, :], ALU.mult, ALU.add).then_inc(s_in, 1)
                    for c in range(2):
                        for m in range(DK):
                            dve.wait_ge(s_w, ONE + upto(b, 4, 2 * c + m + 1))
                            dve.wait_ge(s_re, ONE + upto(b, 4, 2 * c + m + 1))
                            dve.wait_ge(s_x, ONE + upto(b, 4, 2 * c))
                            dve.tensor_tensor(oo[:, m, :], p_w[m][:, :], rr[:, m, :], ALU.mult).then_inc(s_oo, 1)
                            dve.wait_ge(s_oo, ONE + upto(b, 4, 2 * c + m + 1))
                            x = X[:, m, bass.ds(b * T + c * 512, 512)]
                            dve.scalar_tensor_tensor(x, oo[:, m, :], MOD[:, 1, bass.ds(b, 1), 4 + m], x, ALU.mult,
                                                     ALU.add).then_inc(s_x, 1)


def mlp_stage(nc, g, d, tag, layer):
    with ExitStack() as ctx:
        s = Scope(nc, ctx, tag)
        w1 = s.sb("w1", [P, DK, 2, FM * P])
        w2 = s.sb("w2", [P, FM, D])
        vec = s.sb("vec", [P, 2 * FM + 3 * DK])
        xc, sq, hn = (s.sb(n, [P, DK, NB]) for n in ("xc", "sq", "hn"))
        lv, rs = s.sb("lv", [P, NB]), s.sb("rs", [P, NB])
        ge = s.sb("ge", [P, 2, NB])
        hh = s.sb("hh", [P, FM, NB])
        p_mean, p_var = s.ps("p_mean"), s.ps("p_var")
        p_a, p_g = ([s.ps(f"{n}{k}") for k in range(2)] for n in ("p_a", "p_g"))
        p_w = [s.ps(f"p_w{k}") for k in range(DK)]
        names = "load mean xc sq var rs a v hn a_ ge hh w y".split()
        s_load, s_mean, s_xc, s_sq, s_var, s_rs, s_l, s_v, s_hn, s_a, s_ge, s_hh, s_w, s_y = (s.sem("s" + x) for x in names)
        Y, Z = g["Y"], g["Z"]
        V_B2, V_G, V_B = 2 * FM, 2 * FM + DK, 2 * FM + 2 * DK

        def blocks(eng):
            with eng.Fori(0, B) as b:
                with eng.Fori(0, NBLK) as c:
                    yield b, c, b * NBLK + c

        with nc.Block() as block:
            @block.sync
            def _(sp):
                src = d["mlp"][layer]
                sp.dma_start(w1[:, :, :, :], src["w1"].rearrange("(k p) a n -> p k a n", p=P)).then_inc(s_load, 16)
                sp.dma_start(w2[:, :, :], src["w2"].rearrange("(k p) n -> p k n", p=P)).then_inc(s_load, 16)
                sp.dma_start(vec[:, :], src["vec"]).then_inc(s_load, 16)

            @block.tensor
            def _(pe):
                pe.wait_ge(s_load, ONE + 48)
                for b, c, i in blocks(pe):
                    pe.wait_ge(s_xc, ONE + 2 * i)
                    for k in range(DK):
                        ins = pe.matmul(p_mean[:, :], g["ones"][:, :], Z[:, k, col(b, c * NB - k, NB)], start=(k == 0), stop=(k == DK - 1))
                    ins.then_inc(s_mean, 1)
                    pe.wait_ge(s_sq, ONE + i + 1)
                    for k in range(DK):
                        ins = pe.matmul(p_var[:, :], g["ones"][:, :], sq[:, k, :], start=(k == 0), stop=(k == DK - 1))
                    ins.then_inc(s_var, 1)
                    pe.wait_ge(s_hn, ONE + i + 1)
                    for m in range(FM):
                        for x, pp in enumerate((p_a, p_g)):
                            pe.wait_ge((s_hh, s_ge)[x], ONE + (upto(i, FM, m - 1) if m >= 2 else upto(i, FM, 0)))
                            for k in range(DK):
                                ins = pe.matmul(pp[m % 2][:, :], w1[:, k, x, m * P:(m + 1) * P], hn[:, k, :], start=(k == 0), stop=(k == DK - 1))
                            ins.then_inc(s_a, 1)
                    for n in range(DK):
                        pe.wait_ge(s_hh, ONE + upto(i, FM, FM))
                        pe.wait_ge(s_y, ONE + upto(i, DK, 0))
                        for k in range(FM):
                            ins = pe.matmul(p_w[n][:, :], w2[:, k, n * P:(n + 1) * P], hh[:, k, :], start=(k == 0), stop=(k == FM - 1))
                        ins.then_inc(s_w, 1)

            @block.scalar
            def _(act):
                act.wait_ge(s_load, ONE + 48)
                for b, c, i in blocks(act):
                    act.wait_ge(s_xc, ONE + 2 * i + 2)
                    act.activation(sq[:, :, :], xc[:, :, :], ACT.Square).then_inc(s_sq, 1)
                    act.wait_ge(s_var, ONE + i + 1)
                    act.activation(lv[:, :], p_var[:, :], ACT.Ln, bias=g["bias"][:, 0:1]).then_inc(s_l, 1)
                    act.wait_ge(s_l, ONE + i + 1)
                    act.activation(rs[:, :], lv[:, :], ACT.Exp, scale=-0.5).then_inc(s_rs, 1)
                    for m in range(FM):
                        act.wait_ge(s_a, ONE + upto(i, 2 * FM, 2 * m + 2))
                        act.wait_ge(s_hh, ONE + upto(i, FM, max(0, m - 1)))
                        act.activation(ge[:, m % 2, :], p_g[m % 2][:, :], ACT.Gelu, bias=vec[:, FM + m:FM + m + 1]).then_inc(s_ge, 1)

            @block.vector
            def _(dve):
                dve.wait_ge(s_load, ONE + 48)
                for b, c, i in blocks(dve):
                    link = Chain(dve, s_v, i, 2)
                    dve.wait_ge(s_hn, ONE + i)
                    dve.wait_ge(s_mean, ONE + i + 1)
                    for k in range(DK):
                        dve.tensor_tensor(xc[:, k, :], Z[:, k, col(b, c * NB - k, NB)], p_mean[:, :], ALU.subtract).then_inc(s_xc, 1)
                    dve.wait_ge(s_rs, ONE + i + 1)
                    for k in range(DK):
                        link(dve.tensor_tensor(xc[:, k, :], xc[:, k, :], rs[:, :], ALU.mult))
                    for k in range(DK):
                        ins = dve.tensor_scalar(hn[:, k, :], xc[:, k, :], vec[:, V_G + k:V_G + k + 1], vec[:, V_B + k:V_B + k + 1],
                                                ALU.mult, ALU.add)
                    ins.then_inc(s_hn, 1)
                    dve.wait_ge(s_w, ONE + DK * i)
                    for m in range(FM):
                        dve.wait_ge(s_ge, ONE + upto(i, FM, m + 1))
                        dve.scalar_tensor_tensor(hh[:, m, :], p_a[m % 2][:, :], vec[:, m:m + 1], ge[:, m % 2, :], ALU.add,
                                                 ALU.mult).then_inc(s_hh, 1)
                    for n in range(DK):
                        dve.wait_ge(s_w, ONE + upto(i, DK, n + 1))
                        dve.scalar_tensor_tensor(Y[:, n, col(b, c * NB, NB)], p_w[n][:, :], vec[:, V_B2 + n:V_B2 + n + 1],
                                                 Z[:, n, col(b, c * NB, NB)], ALU.add, ALU.add).then_inc(s_y, 1)


def output_stage(nc, g, d, out, last=True):
    with ExitStack() as ctx:
        s = Scope(nc, ctx, "out")
        s_x, s_out = s.sem("x"), s.sem("o")
        X, Y, MOD = g["X"], g["Y"], g["MOD"]
        with nc.Block() as block:
            @block.vector
            def _(dve):
                with dve.Fori(0, B) as b:
                    for k in range(DK):
                        x = X[:, k, bass.ds(b * T, T)]
                        if last:
                            ins = dve.scalar_tensor_tensor(x, Y[:, k, col(b, 0, T)], MOD[:, 1, bass.ds(b, 1), 10 + k], x, ALU.mult, ALU.add)
                        else:
                            ins = dve.tensor_copy(x, x)
                        ins.then_inc(s_x, 1)

            @block.sync
            def _(sp):
                with sp.Fori(0, B) as b:
                    for k in range(DK):
                        sp.wait_ge(s_x, ONE + upto(b, DK, k + 1))
                        sp.dma_start(out[k * P:(k + 1) * P, bass.ds(b * T, T)], X[:, k, bass.ds(b * T, T)]).then_inc(s_out, 16)
                sp.wait_ge(s_out, ONE + 16 * B * DK)


def build(nc, d, out, stages=99, dump=None):
    with ExitStack() as ctx:
        g = {}

        def keep(name, shape, dt=F32):
            g[name] = ctx.enter_context(nc.sbuf_tensor(f"g_{name}", shape, dt))

        keep("X", [P, DK, B * T])
        keep("MOD", [P, 2, B, 12])
        keep("SLOT", [P, 64])
        keep("FAC", [P, 64])
        keep("bias", [P, 4])
        for name in ("ones", "ident", "blk64", "rot64"):
            keep(name, [P, P])
        for name in ("s_dram", "slot_dram", "f_dram"):
            g[name] = nc.dram_tensor(name, [2 * B, T], F32, kind="Internal").ap()
        g["part_dram"] = nc.dram_tensor("part_dram", [3, 2, B * A_G, 64, T], BF16, kind="Internal").ap()
        g["v_dram"] = nc.dram_tensor("v_dram", [B * A_G, T // P, P, P], F32, kind="Internal").ap()
        modulation_stage(nc, g, d)
        if stages >= 1:
            with ExitStack() as c1:
                g["OA"] = c1.enter_context(nc.sbuf_tensor("g_OA", [P, A_G * B, T], F32))
                split_stage(nc, g, d)
                causal_stage(nc, g, d)
        keep("Y", [P, DK, B * TP])
        zero_columns(nc, g, "Y")
        if stages >= 2:
            norm_stage(nc, g, d, "n1", 0, 1, route=True)
            routing_stage(nc, g, d)
            window_stage(nc, g, d, "li", False)
        if stages >= 3:
            routed_stage(nc, g, d)
        if stages >= 4:
            norm_stage(nc, g, d, "n2", 1, 0)
            mixing_stage(nc, g, d)
        if stages >= 5:
            g["Z"] = ctx.enter_context(nc.sbuf_tensor("g_Z2", [P, DK, B * TP], F32))
            zero_columns(nc, g, "Z")
            norm_stage(nc, g, d, "n3", 1, 1)
            for layer in range(2):
                window_stage(nc, g, d, f"lo{layer}", True, layer)
                mlp_stage(nc, g, d, f"ml{layer}", layer)
        output_stage(nc, g, d, out, last=stages >= 5)


def zero_columns(nc, g, name):
    with ExitStack() as ctx:
        s_zero = Scope(nc, ctx, "zc" + name).sem("zero")
        with nc.Block() as block:
            @block.gpsimd
            def _(pool):
                for b in range(B):
                    pool.memset(g[name][:, :, b * TP:b * TP + 1], 0.0).then_inc(s_zero, 1)
                pool.wait_ge(s_zero, ONE + B)


def constants():
    def bf(v):
        return (np.ascontiguousarray(v, np.float32).view(np.uint32) >> 16).astype(np.uint16)

    i = np.arange(P)
    c = {"ones": np.full((P, P), 1.0 / D, np.float32), "ident": np.eye(P, dtype=np.float32)}
    c["blk64"] = (i[:, None] // 64 == i[None, :] // 64).astype(np.float32)
    rot = np.zeros((P, P), np.float32)
    for p in range(P):
        rot[p + 32 if p % 64 < 32 else p - 32, p] = -1.0 if p % 64 < 32 else 1.0
    c["rot64"] = rot
    c["idb"] = bf(np.eye(P))
    c["mqk"] = bf(np.where(i[None, :] > i[:, None], NEG, 0.0))
    c["mkq"] = bf(np.where(i[None, :] > i[:, None], NEG, 0.0).T)
    den = np.zeros((P, P), np.float32)
    den[(i // 32) * 32 + 16, i] = 1.0
    c["den"] = den
    c["blk16"] = (i[:, None] // 16 == i[None, :] // 16).astype(np.float32)
    c["low16"] = ((i[:, None] // 16 == i[None, :] // 16) & (i[:, None] < i[None, :])).astype(np.float32)
    rc = np.zeros((P, 4), np.float32)
    for p in range(P):
        num = (NQ, NKV)[(p // 16) % 2]
        k = min(num * FETCH, T)
        rc[p, :3] = np.log(T / k), np.log(k), num
    c["rc"] = rc
    c["bits"] = np.tile(np.array([1 << max(29 - n, 0) for n in range(32)], np.int32), (P, 1))
    cur = np.where(i[None, :] > i[:, None], NEG, 0.0)
    prev = np.where(i[None, :] < i[:, None], NEG, 0.0)
    none = np.full((P, P), NEG)
    m = [np.concatenate([cur, none], 1)] + [np.concatenate([cur, prev], 1)] * 3 + [np.concatenate([prev, cur], 1)]
    c["mask"] = bf(np.stack(m, 1))
    half = np.arange(0, DH, 2, dtype=np.float32)
    inv = (1.0 / 10000.0 ** (half / DH)).astype(np.float32)
    t = np.arange(T, dtype=np.float32)
    fr = (t[:, None] * inv[None, :]).astype(np.float32)
    fr = np.concatenate([fr, fr], -1)
    base = ((half + np.float32(0.4 * DH)) / np.float32(1.4 * DH)).astype(np.float32)
    power = ((t - T // 2) / np.float32(WIN // 2)).astype(np.float32)
    sc = (base[None, :] ** power[:, None]).astype(np.float32)
    sc = np.concatenate([sc, sc], -1)
    cos, sin = np.cos(fr), np.sin(fr)
    tabs = [cos * sc, sin * sc, cos / sc, sin / sc]
    c["tab"] = np.ascontiguousarray(np.stack([np.concatenate([x.T, x.T], 0) for x in tabs], 1)).astype(np.float32)
    c["iota"] = np.tile(np.arange(NKV, dtype=np.float32), (P, 1))
    c["iop"] = np.stack([i, i + P], 1).astype(np.float32)
    return c


STAGES = 99


def kernel(**a):
    import concourse.bacc as _bacc
    from concourse.bass_utils import run_bass_kernel_spmd as _run

    a = {k: np.asarray(v) for k, v in a.items()}
    f32 = np.float32

    def cols(v):
        return np.ascontiguousarray(v.reshape(-1, P).T)

    def head_rows(w):
        out = np.zeros((A_H, 32) + w.shape[1:], f32)
        out[:, :A_HD] = w.reshape((A_H, A_HD) + w.shape[1:])
        return out.reshape((A_H * 32,) + w.shape[1:])

    h = {"xT": a["L0_attn_x"].reshape(B * T, D).T}
    for l in range(2):
        h[f"cT{l}"] = a[f"L{l}_c"].T
        h[f"wmod{l}"] = a[f"L{l}_wmod"]
    h["wqk"] = np.concatenate([a["L0_attn_Wq"].T, a["L0_attn_Wk"].T], 1).reshape(D, 4, P)
    h["bqk"] = np.concatenate([cols(a["L0_attn_bq"]), cols(a["L0_attn_bk"])], 1)
    h["wv"], h["bv"] = a["L0_attn_Wv"].T, a["L0_attn_bv"].reshape(1, D)
    h["wo16"] = head_rows(a["L0_attn_Wo"].T)
    h["bo"] = cols(a["L0_attn_bo"])
    h["rtok"] = np.stack([a["L0_ffn_q_routing_token"], a["L0_ffn_kv_routing_token"]], 1)
    wkv = a["L0_ffn_wkv_light"]
    h["light_wq"], h["light_wk"], h["light_wv"] = a["L0_ffn_wq_light"], wkv[:, :HID], wkv[:, HID:]
    h["light_wo"], h["light_gam"] = a["L0_ffn_wo_light"], cols(a["L0_ffn_gamma_light"])
    kv = a["L0_ffn_wkv_heavy"].reshape(HEADS, 2, DH, D)
    h["heavy_wq"], h["heavy_wo"] = a["L0_ffn_wq_heavy"], a["L0_ffn_wo_heavy"]
    h["heavy_wk"], h["heavy_wv"] = kv[:, 0].reshape(HID, D).T, kv[:, 1].reshape(HID, D).T
    h["heavy_gam"] = cols(a["L0_ffn_gamma_heavy"])
    for n in ("Wv", "Wr", "Wo"):
        h["mix_" + n + "T"] = a["L1_attn_" + n].T
    h["mix_vec"] = np.stack([cols(a["L1_attn_" + n]) for n in ("time_decay", "time_mix_v", "time_mix_r")], 1)
    for l in range(2):
        w = a["L1_ffn_wqkv"][l]
        for n, x in enumerate("qkv"):
            h[f"local{l}_w{x}"] = w[:, n * HID:(n + 1) * HID]
        h[f"local{l}_wo"] = a["L1_ffn_wo"][l]
        h[f"local{l}_gam"] = np.stack([np.concatenate([a[f"L1_ffn_{x}_scale"][l]] * 2) for x in "qk"], 1)
        w1 = np.zeros((D, 2, FM * P), f32)
        w1[:, :, :FFN] = a["L1_ffn_w1"][l].reshape(D, 2, FFN)
        b1 = np.zeros((2, FM * P), f32)
        b1[:, :FFN] = a["L1_ffn_b1"][l].reshape(2, FFN)
        w2 = np.zeros((FM * P, D), f32)
        w2[:FFN] = a["L1_ffn_w2"][l]
        h[f"mlp{l}_w1"], h[f"mlp{l}_w2"] = w1, w2
        h[f"mlp{l}_vec"] = np.concatenate([cols(b1[0]), cols(b1[1]), cols(a["L1_ffn_b2"][l]), cols(a["L1_ffn_ln_g"][l]),
                                           cols(a["L1_ffn_ln_b"][l])], 1)
    h.update(constants())

    nc = _bacc.Bacc("TRN2", target_bir_lowering=False, num_devices=1)
    arrays, t = {}, {}
    for name, v in h.items():
        v = np.ascontiguousarray(v)
        arrays[f"in_{name}_dram"] = v
        t[name] = nc.dram_tensor(f"in_{name}_dram", v.shape, mybir.dt.from_np(v.dtype), kind="ExternalInput").ap()
    d = dict(t)
    for name in ("idb", "mqk", "mkq", "mask"):
        d[name] = t[name].bitcast(BF16)
    d["cT"], d["wmod"] = [t["cT0"], t["cT1"]], [t["wmod0"], t["wmod1"]]
    for grp_ in ("light", "heavy", "mix"):
        d[grp_] = {k[len(grp_) + 1:]: v for k, v in t.items() if k.startswith(grp_ + "_")}
    for grp_ in ("local", "mlp"):
        d[grp_] = [{k[len(grp_) + 2:]: v for k, v in t.items() if k.startswith(f"{grp_}{l}_")} for l in range(2)]
    out = nc.dram_tensor("out_0_dram", (D, B * T), F32, kind="ExternalOutput").ap()
    build(nc, d, out, STAGES)
    r = _run(nc, [arrays], core_ids=[0])
    return np.ascontiguousarray(r.results[0]["out_0_dram"].T).reshape(B, T, D)
```

```python
from contextlib import ExitStack

import numpy as np
import concourse.bass as bass
from concourse import mybir

F32 = mybir.dt.float32
BF16 = mybir.dt.bfloat16
I32 = mybir.dt.int32
ACT = mybir.ActivationFunctionType
ALU = mybir.AluOpType
AX_X = mybir.AxisListType.X

P = 128
B, T, D = 4, 1024, 256
DK = D // P
TP = T + 1
NB = 512
NBLK = T // NB
WIN = 128
NW = T // WIN
A_H, A_HD = 16, 16
A_G = 4
HEADS, DH = 8, 64
HID = HEADS * DH
HM = HID // P
NQ, NKV, FETCH = 256, 512, 9.0 / 8.0
N_ITERS = 50
FFN = int(D * 4 * 2 / 3)
FM = -(-FFN // P)
NEG = -1e30
LN_EXP = "natural_log_exp_and_others"
EXP = "exp_and_others"
LN_EPS = 1e-5
NORM2_MIN = 1e-24
LN2 = float(np.log(2.0))
LN_SHIFT = 20


ONE = 1


def upto(i, per, k):
    return i * per + k


class Chain:

    def __init__(self, eng, sem, i, per):
        self.eng, self.sem, self.i, self.per, self.n = eng, sem, i, per, 0

    def __call__(self, ins):
        ins.then_inc(self.sem, 1)
        self.n += 1
        self.eng.wait_ge(self.sem, ONE + upto(self.i, self.per, self.n))

    def close(self):
        assert self.n == self.per, (self.n, self.per)


class Scope:

    def __init__(self, nc, ctx, tag):
        self.nc, self.ctx, self.tag, self.sems = nc, ctx, tag, []

    def sb(self, name, shape, dt=F32):
        return self.ctx.enter_context(self.nc.sbuf_tensor(f"{self.tag}_{name}", shape, dt))

    def ps(self, name, shape=(P, 512), dt=F32):
        return self.ctx.enter_context(self.nc.psum_tensor(f"{self.tag}_{name}", list(shape), dt))

    def sem(self, name):
        if not self.sems:
            self.ctx.callback(self.clear)
        self.sems.append(self.nc.alloc_semaphore(f"{self.tag}_{name}"))
        self.nc.sync.sem_inc(self.sems[-1], ONE)
        return self.sems[-1]

    def clear(self):
        self.nc.clear_and_free_semaphores(self.sems)
        self.nc.all_engine_barrier()


def col(b, off, n):
    return bass.ds(b * TP + 1 + off, n)


def modulation_stage(nc, g, d):
    with ExitStack() as ctx:
        s = Scope(nc, ctx, "mod")
        c = s.sb("c", [P, 2, DK, B])
        e = s.sb("e", [P, 2, DK, B])
        w = s.sb("w", [P, 2, DK, 6 * D])
        ng = s.sb("ng", [P, 2, B, 12])
        sg = s.sb("sg", [P, 2, B, 12])
        pm = s.ps("pm", [P, 2, 12, B])
        s_load, s_exp, s_c, s_mm, s_v, s_zero = (s.sem(x) for x in ("load", "exp", "c", "mm", "v", "zero"))
        MOD = g["MOD"]
        with nc.Block() as block:
            @block.sync
            def _(sp):
                for l in range(2):
                    sp.dma_start(c[:, l], d["cT"][l].rearrange("(k p) b -> p k b", p=P)).then_inc(s_load, 16)
                    sp.dma_start(w[:, l], d["wmod"][l].rearrange("(k p) n -> p k n", p=P)).then_inc(s_load, 16)
                sp.dma_start(g["X"][:, :, :], d["xT"].rearrange("(k p) n -> p k n", p=P)).then_inc(s_load, 16)
                for name in ("ones", "ident", "blk64", "rot64"):
                    sp.dma_start(g[name][:, :], d[name]).then_inc(s_load, 16)
                sp.wait_ge(s_load, ONE + 16 * 9)

            @block.gpsimd
            def _(pool):
                pool.memset(g["bias"][:, 0:1], LN_EPS).then_inc(s_zero, 1)
                for n, v in enumerate((1.0, 8.0, 16.0)):
                    pool.memset(g["bias"][:, n + 1:n + 2], float(np.log(v)) + 0.5 * LN_SHIFT * LN2).then_inc(s_zero, 1)
                pool.wait_ge(s_zero, ONE + 4)

            @block.scalar
            def _(act):
                act.wait_ge(s_load, ONE + 16 * 9)
                act.activation(e[:, :, :, :], c[:, :, :, :], ACT.Exp, scale=-1.0).then_inc(s_exp, 1)

            @block.tensor
            def _(pe):
                pe.wait_ge(s_c, ONE + 3)
                for l in range(2):
                    for m in range(12):
                        for k in range(DK):
                            ins = pe.matmul(pm[:, l, m, :], w[:, l, k, m * P:(m + 1) * P], c[:, l, k, :],
                                            start=(k == 0), stop=(k == DK - 1))
                ins.then_inc(s_mm, 1)

            @block.vector
            def _(dve):
                link = Chain(dve, s_v, 0, 8)
                dve.wait_ge(s_exp, ONE + 1)
                dve.tensor_scalar(e[:, :, :, :], e[:, :, :, :], 1.0, None, ALU.add).then_inc(s_c, 1)
                dve.wait_ge(s_c, ONE + 1)
                dve.reciprocal(e[:, :, :, :], e[:, :, :, :]).then_inc(s_c, 1)
                dve.wait_ge(s_c, ONE + 2)
                dve.tensor_tensor(c[:, :, :, :], c[:, :, :, :], e[:, :, :, :], ALU.mult).then_inc(s_c, 1)
                dve.wait_ge(s_mm, ONE + 1)
                for l in range(2):
                    link(dve.tensor_copy(MOD[:, l, :, :], pm[:, l].rearrange("p m b -> p b m")))
                v = MOD[:, :, :, :].rearrange("p l b (s k) -> p (l b) s k", k=DK)
                sc = v[:, :, 1:5:3, :]
                link(dve.tensor_scalar(sc, sc, 1.0, None, ALU.add))
                gt = v[:, :, 2:6:3, :]
                n_ = ng[:, :, :, 0:4].rearrange("p l b (s k) -> p (l b) s k", k=DK)
                s_ = sg[:, :, :, 0:4].rearrange("p l b (s k) -> p (l b) s k", k=DK)
                link(dve.tensor_scalar(n_, gt, -1.0, None, ALU.mult))
                link(dve.tensor_tensor(n_, n_, gt, ALU.max))
                link(dve.tensor_scalar(n_, n_, 0.25, 2.0, ALU.max, ALU.mult))
                link(dve.tensor_scalar(s_, gt, 0.0, -0.5, ALU.is_ge, ALU.add))
                link(dve.tensor_tensor(gt, s_, n_, ALU.mult))
                link.close()


def norm_stage(nc, g, d, tag, layer, which, route=False):
    with ExitStack() as ctx:
        s = Scope(nc, ctx, tag)
        xc, sq, h, hs = (s.sb(n, [P, DK, NB]) for n in ("xc", "sq", "h", "hs"))
        lv, rs, l2, r2 = (s.sb(n, [P, NB]) for n in ("lv", "rs", "l2", "r2"))
        p_mean, p_var, p_nn = s.ps("p_mean"), s.ps("p_var"), s.ps("p_nn")
        s_mean, s_xc, s_sq, s_var, s_rs, s_v, s_a, s_h = (
            s.sem(x) for x in ("mean", "xc", "sq", "var", "rs", "v", "a", "h"))
        s_h2, s_nn, s_n2, s_r2, s_rt, s_st, s_out, s_load, s_y = (
            s.sem(x) for x in ("h2", "nn", "n2", "r2_", "rt", "st", "out", "load", "y"))
        MOD, X, Y = g["MOD"], g["X"], g["Y"]
        if route:
            p_rt = s.ps("p_rt", (2, NB))
            rtok = s.sb("rtok", [P, DK, 2])
            srow = s.sb("srow", [2, NB])

        def blocks(eng):
            with eng.Fori(0, B) as b:
                with eng.Fori(0, NBLK) as c:
                    yield b, c

        with nc.Block() as block:
            @block.sync
            def _(sp):
                if route:
                    sp.dma_start(rtok[:, :, :], d["rtok"].rearrange("(k p) r -> p k r", p=P)).then_inc(s_load, 16)
                    for b, c in blocks(sp):
                        i = b * NBLK + c
                        sp.wait_ge(s_st, ONE + i + 1)
                        sp.dma_start(g["s_dram"][bass.ds(2 * b, 2), bass.ds(c * NB, NB)], srow[:, :]).then_inc(s_out, 16)
                    sp.wait_ge(s_out, ONE + 16 * B * NBLK)

            @block.tensor
            def _(pe):
                if route:
                    pe.wait_ge(s_load, ONE + 16)
                for b, c in blocks(pe):
                    i = b * NBLK + c
                    pe.wait_ge(s_xc, ONE + 2 * i)
                    for k in range(DK):
                        ins = pe.matmul(p_mean[:, :], g["ones"][:, :], X[:, k, bass.ds(b * T + c * NB, NB)],
                                        start=(k == 0), stop=(k == DK - 1))
                    ins.then_inc(s_mean, 1)
                    pe.wait_ge(s_sq, ONE + upto(i, 1, 1))
                    for k in range(DK):
                        ins = pe.matmul(p_var[:, :], g["ones"][:, :], sq[:, k, :], start=(k == 0), stop=(k == DK - 1))
                    ins.then_inc(s_var, 1)
                    if route:
                        pe.wait_ge(s_h, ONE + upto(i, 1, 1))
                        pe.wait_ge(s_st, ONE + i)
                        for k in range(DK):
                            ins = pe.matmul(p_rt[:, :], rtok[:, k, :], h[:, k, :], start=(k == 0), stop=(k == DK - 1))
                        ins.then_inc(s_rt, 1)
                        pe.wait_ge(s_h2, ONE + upto(i, 1, 1))
                        for k in range(DK):
                            ins = pe.matmul(p_nn[:, :], g["ones"][:, :], hs[:, k, :], start=(k == 0), stop=(k == DK - 1))
                        ins.then_inc(s_nn, 1)

            @block.scalar
            def _(act):
                act.preload_act_table_set(EXP)
                for b, c in blocks(act):
                    i = b * NBLK + c
                    act.wait_ge(s_xc, ONE + upto(i, 2, 2))
                    act.wait_ge(s_var, ONE + i)
                    act.activation(sq[:, :, :], xc[:, :, :], ACT.Square).then_inc(s_sq, 1)
                    act.wait_ge(s_var, ONE + upto(i, 1, 1))
                    act.activation(lv[:, :], p_var[:, :], ACT.Ln, bias=g["bias"][:, 0:1]).then_inc(s_a, 1)
                    act.wait_ge(s_a, ONE + upto(i, 1, 1))
                    act.activation(rs[:, :], lv[:, :], ACT.Exp, scale=-0.5).then_inc(s_rs, 1)
                    if route:
                        act.wait_ge(s_h, ONE + upto(i, 1, 1))
                        act.activation(hs[:, :, :], h[:, :, :], ACT.Square).then_inc(s_h2, 1)
                        act.wait_ge(s_n2, ONE + upto(i, 1, 1))
                        act.activation(l2[:, :], r2[:, :], ACT.Ln, scale=float(2 ** LN_SHIFT)).then_inc(s_r2, 1)
                        act.wait_ge(s_r2, ONE + upto(i, 2, 1))
                        act.activation(r2[:, :], l2[:, :], ACT.Exp, scale=-0.5, bias=g["bias"][:, 1:2]).then_inc(s_r2, 1)

            @block.vector
            def _(dve):
                for b, c in blocks(dve):
                    i = b * NBLK + c
                    link = Chain(dve, s_v, i, 2)
                    dve.wait_ge(s_h, ONE + i)
                    dve.wait_ge(s_mean, ONE + upto(i, 1, 1))
                    for k in range(DK):
                        dve.tensor_tensor(xc[:, k, :], X[:, k, bass.ds(b * T + c * NB, NB)], p_mean[:, :],
                                          ALU.subtract).then_inc(s_xc, 1)
                    dve.wait_ge(s_rs, ONE + upto(i, 1, 1))
                    for k in range(DK):
                        ins = dve.tensor_tensor(xc[:, k, :], xc[:, k, :], rs[:, :], ALU.mult)
                        link(ins)
                    for k in range(DK):
                        if route:
                            out = h[:, k, :]
                        else:
                            out = Y[:, k, col(b, c * NB, NB)]
                        ins = dve.tensor_scalar(out, xc[:, k, :], MOD[:, layer, bass.ds(b, 1), which * 6 + 2 + k],
                                                MOD[:, layer, bass.ds(b, 1), which * 6 + k], ALU.mult, ALU.add)
                    ins.then_inc(s_h, 1)
                    if route:
                        dve.wait_ge(s_rt, ONE + upto(i, 1, 1))
                        dve.wait_ge(s_out, ONE + 16 * i)
                        dve.tensor_copy(srow[:, :], p_rt[:, :]).then_inc(s_st, 1)
                        dve.wait_ge(s_nn, ONE + upto(i, 1, 1))
                        dve.tensor_scalar(r2[:, :], p_nn[:, :], NORM2_MIN / D, None, ALU.max).then_inc(s_n2, 1)
                        dve.wait_ge(s_r2, ONE + upto(i, 2, 2))
                        for k in range(DK):
                            ins = dve.tensor_tensor(Y[:, k, col(b, c * NB, NB)], h[:, k, :], r2[:, :], ALU.mult)
                        ins.then_inc(s_y, 1)
                        dve.wait_ge(s_y, ONE + upto(i, 1, 1))
                    link.close()


def split_stage(nc, g, d):
    with ExitStack() as ctx:
        s = Scope(nc, ctx, "sp")
        wqk = s.sb("wqk", [P, DK, 4, P])
        wv = s.sb("wv", [P, DK, D])
        bqk, bv = s.sb("bqk", [P, 4]), s.sb("bv", [P, D])
        xc, sq, hn = (s.sb(n, [P, DK, NB]) for n in ("xc", "sq", "hn"))
        lv, rs = s.sb("lv", [P, NB]), s.sb("rs", [P, NB])
        f, r1, r2 = (s.sb(n, [P, 4, NB]) for n in ("f", "r1", "r2"))
        part = s.sb("part", [P, 3, 4, NB], BF16)
        v = s.sb("v", [P, 4, A_H, 32])
        p_mean, p_var = s.ps("p_mean"), s.ps("p_var")
        p_x = [s.ps(f"p_x{k}") for k in range(4)]
        p_v = [s.ps(f"p_v{k}") for k in range(2)]
        names = "load ini mean xc sq var l rs v hn px fe c1 r1 c2 r2 c3 pv ve out".split()
        (s_load, s_ini, s_mean, s_xc, s_sq, s_var, s_l, s_rs, s_v, s_hn, s_px, s_fe, s_c1, s_r1, s_c2, s_r2, s_c3, s_pv, s_ve,
         s_out) = (s.sem("s" + x) for x in names)
        X, MOD = g["X"], g["MOD"]
        NTB = NB // P

        def blocks(eng):
            with eng.Fori(0, B) as b:
                with eng.Fori(0, NBLK) as c:
                    yield b, c, b * NBLK + c

        with nc.Block() as block:
            @block.sync
            def _(sp):
                sp.dma_start(wqk[:, :, :, :], d["wqk"].rearrange("(k p) x n -> p k x n", p=P)).then_inc(s_load, 16)
                sp.dma_start(wv[:, :, :], d["wv"].rearrange("(k p) n -> p k n", p=P)).then_inc(s_load, 16)
                sp.dma_start(bqk[:, :], d["bqk"]).then_inc(s_load, 16)
                sp.dma_start(bv[:, :], d["bv"].to_broadcast([P, D])).then_inc(s_load, 16)
                for b, c, i in blocks(sp):
                    tok = bass.ds(c * NB, NB)
                    sems = (s_c1, s_c2, s_c3)
                    for p in range(3):
                        sp.wait_ge(sems[p], ONE + i + 1)
                        for x in range(4):
                            for gg in range(2):
                                sp.dma_start(g["part_dram"][p, x // 2, bass.ds(b * A_G + 2 * (x % 2) + gg, 1), :, tok],
                                             part[gg * 64:gg * 64 + 64, p, x, :]).then_inc(s_out, 16)
                    sp.wait_ge(s_ve, ONE + 2 * i + 2)
                    for gr in range(A_G):
                        sp.dma_start(g["v_dram"][bass.ds(b * A_G + gr, 1), bass.ds(c * NTB, NTB)].rearrange("a t p e -> p (a t) e"),
                                     v[:, :, gr * 4:(gr + 1) * 4, :].rearrange("p t j e -> p t (j e)")).then_inc(s_out, 16)
                sp.wait_ge(s_out, ONE + 16 * 28 * B * NBLK)

            @block.tensor
            def _(pe):
                pe.wait_ge(s_load, ONE + 64)
                for b, c, i in blocks(pe):
                    pe.wait_ge(s_xc, ONE + 2 * i)
                    for k in range(DK):
                        ins = pe.matmul(p_mean[:, :], g["ones"][:, :], X[:, k, bass.ds(b * T + c * NB, NB)],
                                        start=(k == 0), stop=(k == DK - 1))
                    ins.then_inc(s_mean, 1)
                    pe.wait_ge(s_sq, ONE + i + 1)
                    for k in range(DK):
                        ins = pe.matmul(p_var[:, :], g["ones"][:, :], sq[:, k, :], start=(k == 0), stop=(k == DK - 1))
                    ins.then_inc(s_var, 1)
                    pe.wait_ge(s_hn, ONE + i + 1)
                    for x in range(4):
                        pe.wait_ge(s_fe, ONE + 4 * i)
                        for k in range(DK):
                            ins = pe.matmul(p_x[x][:, :], wqk[:, k, x, :], hn[:, k, :], start=(k == 0), stop=(k == DK - 1))
                        ins.then_inc(s_px, 1)
                    for n in range(2):
                        pe.wait_ge(s_ve, ONE + 2 * i)
                        for q in range(2):
                            t = 2 * n + q
                            for k in range(DK):
                                ins = pe.matmul(p_v[n][:, q * D:(q + 1) * D], hn[:, k, t * P:(t + 1) * P], wv[:, k, :],
                                                start=(k == 0), stop=(k == DK - 1))
                        ins.then_inc(s_pv, 1)

            @block.scalar
            def _(act):
                act.preload_act_table_set(LN_EXP)
                act.wait_ge(s_load, ONE + 64)
                for b, c, i in blocks(act):
                    act.wait_ge(s_xc, ONE + 2 * i + 2)
                    act.activation(sq[:, :, :], xc[:, :, :], ACT.Square).then_inc(s_sq, 1)
                    act.wait_ge(s_var, ONE + i + 1)
                    act.activation(lv[:, :], p_var[:, :], ACT.Ln, bias=g["bias"][:, 0:1]).then_inc(s_l, 1)
                    act.wait_ge(s_l, ONE + i + 1)
                    act.activation(rs[:, :], lv[:, :], ACT.Exp, scale=-0.5).then_inc(s_rs, 1)
                    act.wait_ge(s_out, ONE + 16 * 28 * i)
                    act.wait_ge(s_fe, ONE + 4 * i + 4)
                    act.activation(part[:, 0, :, :], f[:, :, :], ACT.Copy).then_inc(s_c1, 1)
                    act.wait_ge(s_r1, ONE + i + 1)
                    act.activation(part[:, 1, :, :], r1[:, :, :], ACT.Copy).then_inc(s_c2, 1)
                    act.wait_ge(s_r2, ONE + i + 1)
                    act.activation(part[:, 2, :, :], r2[:, :, :], ACT.Copy).then_inc(s_c3, 1)

            @block.gpsimd
            def _(pool):
                pool.memset(v[:, :, :, A_HD:A_HD + 1], 1.0).then_inc(s_ini, 1)
                pool.memset(v[:, :, :, A_HD + 1:32], 0.0).then_inc(s_ini, 1)
                for b, c, i in blocks(pool):
                    pool.wait_ge(s_c2, ONE + i + 1)
                    pool.wait_ge(s_c3, ONE + i)
                    pool.tensor_tensor(r2[:, :, :], r1[:, :, :], part[:, 1, :, :], ALU.subtract).then_inc(s_r2, 1)

            @block.vector
            def _(dve):
                dve.wait_ge(s_load, ONE + 64)
                dve.wait_ge(s_ini, ONE + 2)
                for b, c, i in blocks(dve):
                    link = Chain(dve, s_v, i, 2)
                    dve.wait_ge(s_hn, ONE + i)
                    dve.wait_ge(s_mean, ONE + i + 1)
                    for k in range(DK):
                        dve.tensor_tensor(xc[:, k, :], X[:, k, bass.ds(b * T + c * NB, NB)], p_mean[:, :],
                                          ALU.subtract).then_inc(s_xc, 1)
                    dve.wait_ge(s_rs, ONE + i + 1)
                    for k in range(DK):
                        link(dve.tensor_tensor(xc[:, k, :], xc[:, k, :], rs[:, :], ALU.mult))
                    dve.wait_ge(s_pv, ONE + 2 * i)
                    for k in range(DK):
                        ins = dve.tensor_scalar(hn[:, k, :], xc[:, k, :], MOD[:, 0, bass.ds(b, 1), 2 + k],
                                                MOD[:, 0, bass.ds(b, 1), k], ALU.mult, ALU.add)
                    ins.then_inc(s_hn, 1)
                    dve.wait_ge(s_c1, ONE + i)
                    dve.wait_ge(s_r1, ONE + i)
                    for x in range(4):
                        dve.wait_ge(s_px, ONE + upto(i, 4, x + 1))
                        dve.tensor_scalar(f[:, x, :], p_x[x][:, :], bqk[:, x:x + 1], float(A_HD) ** -0.5 if x < 2 else 1.0,
                                          ALU.add, ALU.mult).then_inc(s_fe, 1)
                    dve.wait_ge(s_out, ONE + 16 * 28 * i)
                    for n in range(2):
                        dve.wait_ge(s_pv, ONE + upto(i, 2, n + 1))
                        for q in range(2):
                            ins = dve.tensor_tensor(v[:, 2 * n + q, :, 0:A_HD],
                                                    p_v[n][:, q * D:(q + 1) * D].rearrange("p (h e) -> p h e", e=A_HD),
                                                    bv[:, :].rearrange("p (h e) -> p h e", e=A_HD), ALU.add)
                        ins.then_inc(s_ve, 1)
                    dve.wait_ge(s_c1, ONE + i + 1)
                    dve.wait_ge(s_fe, ONE + 4 * i + 4)
                    dve.wait_ge(s_r2, ONE + i)
                    dve.wait_ge(s_c2, ONE + i)
                    dve.tensor_tensor(r1[:, :, :], f[:, :, :], part[:, 0, :, :], ALU.subtract).then_inc(s_r1, 1)


def causal_stage(nc, g, d):
    QP, KP = (2, 1, 0, 1, 0, 0), (0, 1, 2, 0, 1, 0)
    R0 = 6 * A_HD
    NR, RING = B * A_G, 3
    NT = T // P
    steps = [(n, kt) for n in range(2) for kt in range(4 * n + 4)]
    units = [(t, c, j) for t in range(NT) for c in range(t // 4 + 1) for j in range(4)]
    NS, NU = 4 * len(steps), len(units)
    PER_STEP = -(-NU // (len(steps) - 4))
    SPLIT, TURN = len(steps) - 4, len(steps) - 2
    with ExitStack() as ctx:
        s = Scope(nc, ctx, "ca")
        qs = [s.sb(f"qs{n}", [P, 4, T], BF16) for n in range(RING)]
        ks = [s.sb(f"ks{n}", [P, 4, T], BF16) for n in range(RING)]
        vg = [s.sb(f"vg{n}", [P, NT, 4, 32]) for n in range(RING)]
        mp, nm, m_r = s.sb("mp", [P, NT, 2, 4]), s.sb("nm", [P, NT, 4]), s.sb("m_r", [P, NT, 4])
        n3 = s.sb("n3", [P, NT, 4, 32], BF16)
        mt = s.sb("mt", [P, T], BF16)
        pt = s.sb("pt", [P, 2, 4, 512])
        osb, rden = s.sb("osb", [P, 2, 512]), s.sb("rden", [P, 2, 512])
        mqk, mkq, idb = (s.sb(n, [P, P], BF16) for n in ("mqk", "mkq", "idb"))
        den = s.sb("den", [P, P])
        p_1 = [s.ps(f"p_1{n}") for n in range(2)]
        p_s = [s.ps(f"p_s{n}") for n in range(4)]
        p_o, p_m = s.ps("p_o"), s.ps("p_m")
        names = "load ini lda ldb ldc s1 mxa mxb dv mt me md st ex pv oe dn rd on".split()
        (s_load, s_ini, s_lda, s_ldb, s_ldc, s_s1, s_mxa, s_mxb, s_dv, s_mt, s_me, s_md, s_st, s_ex, s_pv, s_oe, s_dn, s_rd,
         s_on) = (s.sem(x) for x in names)
        s_ld = (s_lda, s_ldb, s_ldc)
        s_mx = (s_mxa, s_mxb)
        OA = g["OA"]
        LOADS = 16 * 13

        def rounds(eng, body):
            with eng.Fori(0, NR // RING) as i:
                for u in range(RING):
                    body(i * RING + u, i, u, True)
            body(NR - 1, NR // RING, (NR - 1) % RING, False)

        with nc.Block() as block:
            @block.sync
            def _(sp):
                for dst, name in ((mqk, "mqk"), (mkq, "mkq"), (idb, "idb"), (den, "den")):
                    sp.dma_start(dst[:, :], d[name]).then_inc(s_load, 16)

                def load(r, u):
                    for dst, x, parts in ((qs[u], 0, QP), (ks[u], 1, KP)):
                        for c, p in enumerate(parts):
                            sp.dma_start(dst[A_HD * c:A_HD * (c + 1), :, :],
                                         g["part_dram"][p, x, bass.ds(r, 1)].rearrange("a (j e) t -> e (a j) t", e=A_HD))\
                              .then_inc(s_ld[u], 16)
                    sp.dma_start(vg[u][:, :, :, :].rearrange("p t j e -> p t (j e)"),
                                 g["v_dram"][bass.ds(r, 1)].rearrange("a t p e -> p (a t) e")).then_inc(s_ld[u], 16)

                def maxima(r, u):
                    sp.wait_ge(s_me, ONE + r + 1)
                    for j in range(4):
                        sp.dma_start(qs[u][R0:R0 + 3, j, :], mt[32 * j:32 * j + 3, :]).then_inc(s_md, 16)

                load(0, 0)
                load(1, 1)
                maxima(0, 0)

                def body(r, u):
                    sp.wait_ge(s_pv, ONE + NS * r)
                    load(r + 2, (u + 2) % RING)
                    maxima(r + 1, (u + 1) % RING)

                with sp.Fori(0, NR // RING - 1) as i:
                    for u in range(RING):
                        body(i * RING + u, u)
                for r in range(NR - RING - 1, NR):
                    u = r % RING
                    sp.wait_ge(s_pv, ONE + NS * r)
                    if r + 2 < NR:
                        load(r + 2, (u + 2) % RING)
                    if r + 1 < NR:
                        maxima(r + 1, (u + 1) % RING)

            @block.gpsimd
            def _(pool):
                pool.memset(n3[:, :, :, :], 0.0).then_inc(s_ini, 1)
                pool.memset(mp[:, :, :, :], -3.0e38).then_inc(s_ini, 1)
                for n in range(RING):
                    pool.wait_ge(s_ini, ONE + 2 + n)
                    pool.memset(ks[n][R0:R0 + 32, :, :], 1.0).then_inc(s_ini, 1)

                def body(r, i, u, more):
                    for n in range(2):
                        pool.wait_ge(s_rd, ONE + upto(r, 2, n + 1))
                        pool.wait_ge(s_oe, ONE + upto(r, 2, n + 1))
                        pool.tensor_tensor(OA[:, bass.ds(r, 1), n * 512:(n + 1) * 512], osb[:, n:n + 1, :], rden[:, n:n + 1, :],
                                           ALU.mult).then_inc(s_on, 1)

                rounds(pool, body)

            @block.tensor
            def _(pe):
                pe.wait_ge(s_load, ONE + 64)
                pe.wait_ge(s_ini, ONE + 2 + RING)

                def first_pass(r, i, u, n):
                    t, c, j = units[n]
                    if n == 0:
                        pe.wait_ge(s_ld[u], ONE + LOADS * (i + 1))
                    pe.wait_ge(s_mx[n % 2], ONE + upto(r, NU // 2, n // 2))
                    c0, c1 = 512 * c, min((t + 1) * P, 512 * (c + 1))
                    diag = c == t // 4
                    ins = pe.matmul(p_1[n % 2][:, 0:c1 - c0], qs[u][0:R0, j, t * P:(t + 1) * P], ks[u][0:R0, j, c0:c1],
                                    start=True, stop=not diag)
                    if diag:
                        ins = pe.matmul(p_1[n % 2][:, c1 - c0 - P:c1 - c0], idb[:, :], mqk[:, :], start=False, stop=True)
                    ins.then_inc(s_s1, 1)

                def turn_maxima(r):
                    pe.wait_ge(s_dv, ONE + upto(r, 6, 6))
                    for t in range(NT):
                        ins = pe.transpose(p_m[:, :].bitcast(BF16)[:, t * P:(t + 1) * P],
                                           n3[:, t, :, :].rearrange("p j e -> p (j e)"), idb[:, :])
                    ins.then_inc(s_mt, 1)

                def scores(r, u, st, j):
                    n, kt = steps[st]
                    c0 = max(0, kt * P - n * 512)
                    diag = kt * P >= n * 512
                    pe.wait_ge(s_ex, ONE + upto(r, NS, max(0, 4 * st - 3 + j)))
                    ins = pe.matmul(p_s[j][:, c0:512], ks[u][0:R0 + 3, j, kt * P:(kt + 1) * P],
                                    qs[u][0:R0 + 3, j, n * 512 + c0:(n + 1) * 512], start=True, stop=not diag)
                    if diag:
                        ins = pe.matmul(p_s[j][:, c0:c0 + P], idb[:, :], mkq[:, :], start=False, stop=True)
                    ins.then_inc(s_st, 1)

                def values(r, u, st, j):
                    n, kt = steps[st]
                    c0 = max(0, kt * P - n * 512)
                    if j == 0 and kt == 0:
                        pe.wait_ge(s_oe, ONE + upto(r, 2, n))
                    pe.wait_ge(s_ex, ONE + upto(r, NS, 4 * st + j + 1))
                    pe.matmul(p_o[32 * j:32 * j + 32, c0:512], vg[u][:, kt, j, :], pt[:, st % 2, j, c0:512],
                              start=(kt == 0), stop=(kt == 4 * n + 3), tile_position=(0, 32 * j)).then_inc(s_pv, 1)

                def denominators(r, n):
                    pe.wait_ge(s_oe, ONE + upto(r, 2, n + 1))
                    pe.matmul(p_m[:, :], den[:, :], osb[:, n, :], start=True, stop=True).then_inc(s_dn, 1)

                for n in range(NU):
                    first_pass(0, 0, 0, n)
                turn_maxima(0)

                def body(r, i, u, more):
                    pe.wait_ge(s_md, ONE + 64 * (r + 1))
                    done = 0
                    for st in range(len(steps)):
                        ahead = min(PER_STEP, NU - done) if more else 0
                        for j in range(4):
                            scores(r, u, st, j)
                            for _ in range(ahead * (j + 1) // 4 - ahead * j // 4):
                                first_pass(r + 1, i + (u + 1) // RING, (u + 1) % RING, done)
                                done += 1
                            if st:
                                values(r, u, st - 1, j)
                        if st == 6:
                            pe.wait_ge(s_me, ONE + r + 1)
                            pe.wait_ge(s_rd, ONE + 2 * r)
                            denominators(r, 0)
                        if st == TURN and more:
                            pe.wait_ge(s_rd, ONE + 2 * r + 1)
                            turn_maxima(r + 1)
                    for j in range(4):
                        values(r, u, len(steps) - 1, j)
                    pe.wait_ge(s_rd, ONE + 2 * r + 1)
                    if more:
                        pe.wait_ge(s_me, ONE + r + 2)
                    denominators(r, 1)

                rounds(pe, body)

            @block.scalar
            def _(act):
                act.preload_act_table_set("exp_and_others")

                def body(r, i, u, more):
                    for st, (n, kt) in enumerate(steps):
                        c0 = max(0, kt * P - n * 512)
                        for j in range(4):
                            act.wait_ge(s_st, ONE + upto(r, NS, 4 * st + j + 1))
                            act.wait_ge(s_pv, ONE + upto(r, NS, max(0, 4 * st - 7 + j)))
                            act.activation(pt[:, st % 2, j, c0:512], p_s[j][:, c0:512], ACT.Exp).then_inc(s_ex, 1)

                rounds(act, body)

            @block.vector
            def _(dve):
                dve.wait_ge(s_ini, ONE + 2 + RING)

                def maximum(r, n):
                    t, c, j = units[n]
                    c0, c1 = 512 * c, min((t + 1) * P, 512 * (c + 1))
                    dve.wait_ge(s_s1, ONE + upto(r, NU, n + 1))
                    dve.tensor_reduce(mp[:, t, c, j:j + 1], p_1[n % 2][:, 0:c1 - c0], AX_X, ALU.max).then_inc(s_mx[n % 2], 1)

                def split_maxima(r):
                    link = Chain(dve, s_dv, r, 6)
                    for half in s_mx:
                        dve.wait_ge(half, ONE + upto(r, NU // 2, NU // 2))
                    dve.wait_ge(s_mt, ONE + r)
                    link(dve.tensor_tensor(nm[:, :, :], mp[:, :, 0, :], mp[:, :, 1, :], ALU.max))
                    link(dve.tensor_scalar(n3[:, :, :, 0], nm[:, :, :], -1.0, None, ALU.mult))
                    link(dve.scalar_tensor_tensor(m_r[:, :, :], nm[:, :, :], -1.0, n3[:, :, :, 0], ALU.mult, ALU.subtract))
                    link(dve.tensor_copy(n3[:, :, :, 1], m_r[:, :, :]))
                    link(dve.tensor_tensor(m_r[:, :, :], m_r[:, :, :], n3[:, :, :, 1], ALU.subtract))
                    link(dve.tensor_copy(n3[:, :, :, 2], m_r[:, :, :]))
                    link.close()

                def copy_turned(r):
                    dve.wait_ge(s_mt, ONE + r + 1)
                    dve.wait_ge(s_md, ONE + 64 * r)
                    dve.tensor_copy(mt[:, :], p_m[:, :].bitcast(BF16)).then_inc(s_me, 1)

                def copy_sums(r, n):
                    dve.wait_ge(s_pv, ONE + upto(r, NS, 16 if n == 0 else NS))
                    dve.wait_ge(s_on, ONE + 2 * r)
                    dve.tensor_copy(osb[:, n, :], p_o[:, :]).then_inc(s_oe, 1)

                def reciprocals(r, n):
                    dve.wait_ge(s_dn, ONE + upto(r, 2, n + 1))
                    dve.reciprocal(rden[:, n, :], p_m[:, :]).then_inc(s_rd, 1)

                for n in range(NU):
                    maximum(0, n)
                split_maxima(0)
                copy_turned(0)

                def body(r, i, u, more):
                    done = 0
                    for st in range(len(steps)):
                        if more:
                            upper = min(NU, PER_STEP * (st + 1))
                            for n in range(done, upper):
                                maximum(r + 1, n)
                            done = upper
                        if st == 4:
                            copy_sums(r, 0)
                        if st == 6:
                            reciprocals(r, 0)
                        if st == SPLIT and more:
                            split_maxima(r + 1)
                        if st == TURN and more:
                            copy_turned(r + 1)
                    copy_sums(r, 1)
                    reciprocals(r, 1)

                rounds(dve, body)

    with ExitStack() as ctx:
        s = Scope(nc, ctx, "co")
        wo = s.sb("wo", [P, A_G, D])
        bo = s.sb("bo", [P, DK])
        t_ = s.sb("t", [P, DK, NB])
        p_w = [s.ps(f"p_w{k}") for k in range(DK)]
        s_load, s_mm, s_t, s_x = (s.sem(x) for x in ("load", "mm", "t_", "x"))
        X, MOD = g["X"], g["MOD"]

        def blocks(eng):
            with eng.Fori(0, B) as b:
                with eng.Fori(0, NBLK) as c:
                    yield b, c, b * NBLK + c

        with nc.Block() as block:
            @block.sync
            def _(sp):
                sp.dma_start(wo[:, :, :], d["wo16"].rearrange("(k p) n -> p k n", p=P)).then_inc(s_load, 16)
                sp.dma_start(bo[:, :], d["bo"]).then_inc(s_load, 16)

            @block.tensor
            def _(pe):
                pe.wait_ge(s_load, ONE + 32)
                for b, c, i in blocks(pe):
                    for n in range(DK):
                        pe.wait_ge(s_t, ONE + upto(i, DK, n))
                        for k in range(A_G):
                            ins = pe.matmul(p_w[n][:, :], wo[:, k, n * P:(n + 1) * P], OA[:, bass.ds(b * A_G + k, 1), bass.ds(c * NB, NB)],
                                            start=(k == 0), stop=(k == A_G - 1))
                        ins.then_inc(s_mm, 1)

            @block.scalar
            def _(act):
                act.wait_ge(s_load, ONE + 32)
                for b, c, i in blocks(act):
                    for n in range(DK):
                        act.wait_ge(s_mm, ONE + upto(i, DK, n + 1))
                        act.wait_ge(s_x, ONE + upto(i, DK, n))
                        act.activation(t_[:, n, :], p_w[n][:, :], ACT.Identity, bias=bo[:, n:n + 1]).then_inc(s_t, 1)

            @block.vector
            def _(dve):
                for b, c, i in blocks(dve):
                    for n in range(DK):
                        dve.wait_ge(s_t, ONE + upto(i, DK, n + 1))
                        x = X[:, n, bass.ds(b * T + c * NB, NB)]
                        dve.scalar_tensor_tensor(x, t_[:, n, :], MOD[:, 0, bass.ds(b, 1), 4 + n], x, ALU.mult,
                                                 ALU.add).then_inc(s_x, 1)


def routing_stage(nc, g, d):
    with ExitStack() as ctx:
        s = Scope(nc, ctx, "ro")
        CH = T // 16
        S, t, e, sc, gt, eq, cs, sel, f, one = (s.sb(n, [P, CH]) for n in "S t e sc gt eq cs sel f one".split())
        blk, low = s.sb("blk", [P, P]), s.sb("low", [P, P])
        rc = s.sb("rc", [P, 4])
        bits = s.sb("bits", [P, 32], I32)
        mx, u, nm, sm, L, Tt, C, cnt, tk, need = (s.sb(n, [P, 1]) for n in "mx u nm sm L Tt C cnt tk need".split())
        row, row8, rowr = s.sb("row", [1, P]), s.sb("row8", [1, 8]), s.sb("rowr", [1, P])
        slots, fs = s.sb("slots", [8, T]), s.sb("fs", [8, T])
        p_row, p_one, p_t = s.ps("p_row"), s.ps("p_one"), s.ps("p_t")
        names = "load v a pe low ini it_v it_a it_pe bi_v bi_pe end_v end_pe st ld tr fin".split()
        (s_load, s_v, s_a, s_pe, s_low, s_ini, s_iv, s_ia, s_ip, s_bv, s_bp, s_ev, s_ep, s_st, s_ld, s_tr,
         s_fin) = (s.sem(x) for x in names)
        NBITS = 30

        with nc.Block() as block:
            @block.sync
            def _(sp):
                sp.dma_start(S[:, :], g["s_dram"].rearrange("r (a c) -> (r a) c", c=CH)).then_inc(s_load, 16)
                for dst, name in ((blk, "blk16"), (low, "low16"), (rc, "rc"), (bits, "bits")):
                    sp.dma_start(dst[:, :], d[name]).then_inc(s_load, 16)
                sp.wait_ge(s_fin, ONE + 1)
                sp.dma_start(g["slot_dram"].rearrange("r (a c) -> (r a) c", c=CH), cs[:, :]).then_inc(s_st, 16)
                sp.dma_start(g["f_dram"].rearrange("r (a c) -> (r a) c", c=CH), f[:, :]).then_inc(s_st, 16)
                sp.wait_ge(s_st, ONE + 32)
                sp.dma_start(slots[:, :], g["slot_dram"]).then_inc(s_ld, 16)
                sp.dma_start(fs[:, :], g["f_dram"]).then_inc(s_ld, 16)

            @block.gpsimd
            def _(pool):
                pool.memset(one[:, :], 1.0).then_inc(s_ini, 1)
                pool.memset(Tt[:, :], 0.0).then_inc(s_ini, 1)
                pool.wait_ge(s_ini, ONE + 2)

            @block.tensor
            def _(pe):
                pe.wait_ge(s_load, ONE + 80)
                pe.wait_ge(s_v, ONE + 1)
                pe.matmul(p_row[0:1, 0:P], mx[:, :], g["ident"][:, :], start=True, stop=True).then_inc(s_pe, 1)
                pe.wait_ge(s_v, ONE + 3)
                pe.wait_ge(s_ini, ONE + 2)
                pe.matmul(p_one[:, 0:1], rowr[:, :], one[0:1, 0:1], start=True, stop=True).then_inc(s_pe, 1)
                pe.wait_ge(s_v, ONE + 5)
                with pe.Fori(0, N_ITERS - 1) as i:
                    pe.wait_ge(s_ia, ONE + 2 * i + 1)
                    pe.matmul(p_one[:, 0:1], blk[:, :], sm[:, :], start=True, stop=True).then_inc(s_ip, 1)
                pe.wait_ge(s_iv, ONE + 3 * (N_ITERS - 1))
                with pe.Fori(0, NBITS) as i:
                    pe.wait_ge(s_bv, ONE + 4 * i + 2)
                    pe.matmul(p_one[:, 0:1], blk[:, :], cnt[:, :], start=True, stop=True).then_inc(s_bp, 1)
                pe.wait_ge(s_ev, ONE + 1)
                pe.matmul(p_one[:, 0:1], blk[:, :], cnt[:, :], start=True, stop=True).then_inc(s_ep, 1)
                pe.wait_ge(s_ev, ONE + 4)
                pe.matmul(p_one[:, 0:1], low[:, :], cs[:, CH - 1:CH], start=True, stop=True).then_inc(s_ep, 1)
                pe.wait_ge(s_ev, ONE + 8)
                pe.matmul(p_one[:, 0:1], low[:, :], cs[:, CH - 1:CH], start=True, stop=True).then_inc(s_ep, 1)
                pe.wait_ge(s_ld, ONE + 32)
                for n, src in enumerate((slots, fs)):
                    for k in range(T // P):
                        ins = pe.transpose(p_t[:, n * 64 + k * 8:n * 64 + k * 8 + 8], src[:, k * P:(k + 1) * P],
                                           g["ident"][0:8, 0:8])
                ins.then_inc(s_tr, 1)

            @block.scalar
            def _(act):
                act.preload_act_table_set(LN_EXP)
                with act.Fori(0, N_ITERS - 1) as i:
                    act.wait_ge(s_iv, ONE + 3 * i + 2)
                    act.activation(e[:, :], t[:, :], ACT.Exp, bias=nm[:, :], accum_out=sm[:, :]).then_inc(s_ia, 1)
                    act.wait_ge(s_ip, ONE + i + 1)
                    act.activation(L[:, :], p_one[:, 0:1], ACT.Ln).then_inc(s_ia, 1)
                act.wait_ge(s_v, ONE + 6)
                act.activation(sc[:, :], t[:, :], ACT.Exp).then_inc(s_a, 1)

            @block.vector
            def _(dve):
                link = Chain(dve, s_v, 0, 6)
                dve.wait_ge(s_load, ONE + 80)
                dve.wait_ge(s_ini, ONE + 2)
                link(dve.tensor_reduce(mx[:, :], S[:, :], AX_X, ALU.max))
                dve.wait_ge(s_pe, ONE + 1)
                link(dve.tensor_reduce(row8[:, :], p_row[0:1, 0:P].rearrange("p (r a) -> p r a", a=16), AX_X, ALU.max))
                link(dve.tensor_copy(rowr[:, :].rearrange("p (r a) -> p r a", a=16),
                                     row8[:, :].rearrange("p (r a) -> p r a", a=1).to_broadcast([1, 8, 16])))
                dve.wait_ge(s_pe, ONE + 2)
                link(dve.tensor_copy(mx[:, :], p_one[:, 0:1]))
                link(dve.tensor_copy(u[:, :], rc[:, 0:1]))
                with dve.Fori(0, N_ITERS - 1) as i:
                    dve.tensor_scalar(t[:, :], S[:, :], u[:, :], None, ALU.min).then_inc(s_iv, 1)
                    dve.tensor_scalar(nm[:, :], mx[:, :], u[:, :], -1.0, ALU.min, ALU.mult).then_inc(s_iv, 1)
                    dve.wait_ge(s_iv, ONE + 3 * i + 2)
                    dve.wait_ge(s_ia, ONE + 2 * i + 2)
                    dve.tensor_scalar(u[:, :], L[:, :], nm[:, :], rc[:, 1:2], ALU.subtract, ALU.subtract).then_inc(s_iv, 1)
                    dve.wait_ge(s_iv, ONE + 3 * i + 3)
                link(dve.tensor_scalar(t[:, :], S[:, :], u[:, :], 0.0, ALU.subtract, ALU.min))
                link.close()
                dve.wait_ge(s_a, ONE + 1)
                with dve.Fori(0, NBITS) as i:
                    dve.tensor_tensor(C[:, :].bitcast(I32), Tt[:, :].bitcast(I32), bits[:, bass.ds(i, 1)],
                                      ALU.bitwise_or).then_inc(s_bv, 1)
                    dve.wait_ge(s_bv, ONE + 4 * i + 1)
                    dve.tensor_scalar(gt[:, :], sc[:, :], C[:, :], 0.0, ALU.is_ge, ALU.add,
                                      accum_out=cnt[:, :]).then_inc(s_bv, 1)
                    dve.wait_ge(s_bp, ONE + i + 1)
                    dve.wait_ge(s_bv, ONE + 4 * i + 2)
                    dve.tensor_scalar(tk[:, :], p_one[:, 0:1], rc[:, 2:3], None, ALU.is_ge).then_inc(s_bv, 1)
                    dve.wait_ge(s_bv, ONE + 4 * i + 3)
                    dve.scalar_tensor_tensor(Tt[:, :], C[:, :], tk[:, :], Tt[:, :], ALU.mult, ALU.max).then_inc(s_bv, 1)
                    dve.wait_ge(s_bv, ONE + 4 * i + 4)
                end = Chain(dve, s_ev, 0, 11)
                end(dve.tensor_scalar(gt[:, :], sc[:, :], Tt[:, :], 0.0, ALU.is_gt, ALU.add, accum_out=cnt[:, :]))
                end(dve.tensor_scalar(eq[:, :], sc[:, :], Tt[:, :], None, ALU.is_equal))
                dve.wait_ge(s_ep, ONE + 1)
                end(dve.tensor_scalar(need[:, :], p_one[:, 0:1], -1.0, rc[:, 2:3], ALU.mult, ALU.add))
                end(dve.tensor_tensor_scan(cs[:, :], one[:, :], eq[:, :], 0.0, ALU.mult, ALU.add))
                dve.wait_ge(s_ep, ONE + 2)
                end(dve.tensor_scalar(sel[:, :], cs[:, :], p_one[:, 0:1], need[:, :], ALU.add, ALU.is_le))
                end(dve.tensor_tensor(sel[:, :], sel[:, :], eq[:, :], ALU.mult))
                end(dve.tensor_tensor(sel[:, :], sel[:, :], gt[:, :], ALU.add))
                end(dve.tensor_tensor_scan(cs[:, :], one[:, :], sel[:, :], 0.0, ALU.mult, ALU.add))
                dve.wait_ge(s_ep, ONE + 3)
                end(dve.scalar_tensor_tensor(cs[:, :], cs[:, :], p_one[:, 0:1], sel[:, :], ALU.add, ALU.mult))
                end(dve.tensor_scalar(cs[:, :], cs[:, :], -1.0, None, ALU.add))
                end(dve.tensor_scalar(f[:, :], sc[:, :], -1.0, 1.0, ALU.mult, ALU.add))
                end.close()
                dve.tensor_tensor(f[:, :], f[:, :], sc[:, :], ALU.add).then_inc(s_fin, 1)
                dve.wait_ge(s_tr, ONE + 1)
                dve.tensor_copy(g["SLOT"][:, :], p_t[:, 0:64]).then_inc(s_low, 1)
                dve.tensor_copy(g["FAC"][:, :], p_t[:, 64:128]).then_inc(s_low, 1)


def window_stage(nc, g, d, tag, local, layer=0):
    with ExitStack() as ctx:
        s = Scope(nc, ctx, tag)
        KW = 2 * WIN if local else WIN
        RN = 2 if local else 1
        MH = HM // RN
        NJ, NE = 2 * RN, 2 * RN * MH
        wq, wk, wv = (s.sb(n, [P, DK, HID]) for n in ("wq", "wk", "wv"))
        wo = s.sb("wo", [P, HM, D])
        gx = s.sb("gx", [P, DK, WIN])
        qt = s.sb("qt", [P, 2, HM, WIN])
        kt = s.sb("kt", [P, HM, 2, WIN])
        v = s.sb("v", [P, 2, HID])
        pr = s.sb("pr", [P, 2, 2, MH, KW])
        pt = s.sb("pt", [P, 2, 512])
        os_ = s.sb("os", [P, HM, WIN])
        nm, sm = s.sb("nm", [P, 2, 2, MH]), s.sb("sm", [P, 2, 2, MH])
        p_q, p_v, p_t, p_o = s.ps("p_q"), s.ps("p_v"), s.ps("p_t"), s.ps("p_o")
        p_s = [s.ps(f"p_s{e}") for e in range(2)]
        names = "load ini gx pq pk pv qe ke ve sc mx ex rs pr tr tea teb o oe wo out ss ro sq x1 n rn a rt ad".split()
        (s_load, s_ini, s_gx, s_pq, s_pk, s_pv, s_qe, s_ke, s_ve, s_sc, s_mx, s_ex, s_rs, s_pr, s_tr, s_tea, s_teb,
         s_o, s_oe, s_wo, s_out, s_ss, s_ro, s_sq, s_x1, s_n, s_rn, s_a, s_rt, s_ad) = (s.sem(x) for x in names)
        s_te = (s_tea, s_teb)
        X, Y, Z, MOD = g["X"], g["Y"], g.get("Z"), g["MOD"]
        if local:
            gam = s.sb("gam", [P, 2])
            mask = s.sb("mask", [P, 5, KW], BF16)
            idb = s.sb("idb", [P, P], BF16)
            tab = s.sb("tab", [P, 4, T])
            sq, xe, n2, ta, tb = (s.sb(n, [P, 2, 512]) for n in ("sq", "xe", "n2", "ta", "tb"))
            p_ss, p_ro = s.ps("p_ss"), s.ps("p_ro")
            p_k, p_w, p_tt = p_q, p_v, (p_t, p_t)
            NLOAD = 8
        else:
            gam = s.sb("gam", [P, DK])
            p_k, p_w = s.ps("p_k"), p_v
            p_tt = (p_t, s.ps("p_t2"))
            NLOAD = 5

        def windows(eng, body):
            last = NW // 2 - 1
            with eng.Fori(0, B) as b:
                with eng.Fori(0, last) as c:
                    body((b, c, 0), b * NW + c * 2, (b, c, 1))
                    body((b, c, 1), b * NW + c * 2 + 1, (b, c + 1, 0))
                body((b, last, 0), b * NW + NW - 2, (b, last, 1))
                body((b, last, 1), b * NW + NW - 1, (b + 1, 0, 0))

        def off(w):
            return w[1] * 2 * WIN + w[2] * WIN

        def halves(t):
            return t.rearrange("p (m n) -> p m n", m=HM)

        with nc.Block() as block:
            @block.sync
            def _(sp):
                src = d["local"][layer] if local else d["light"]
                for dst, name in ((wq, "wq"), (wk, "wk"), (wv, "wv"), (wo, "wo")):
                    sp.dma_start(dst[:, :, :], src[name].rearrange("(k p) n -> p k n", p=P)).then_inc(s_load, 16)
                sp.dma_start(gam[:, :], src["gam"]).then_inc(s_load, 16)
                if local:
                    sp.dma_start(mask[:, :, :], d["mask"]).then_inc(s_load, 16)
                    sp.dma_start(idb[:, :], d["idb"]).then_inc(s_load, 16)
                    sp.dma_start(tab[:, :, :], d["tab"]).then_inc(s_load, 16)

            @block.gpsimd
            def _(pool):
                pool.wait_ge(s_load, ONE + 16 * NLOAD)
                for buf in (kt, qt):
                    pool.memset(buf[:, :, :, :], 0.0).then_inc(s_ini, 1)
                pool.memset(v[:, :, :], 0.0).then_inc(s_ini, 1)
                pool.wait_ge(s_ini, ONE + 3)

                def prepare(w, i):
                    b = w[0]
                    pool.wait_ge(s_pv, ONE + i)
                    for k in range(DK):
                        if local:
                            ins = pool.tensor_copy(gx[:, k, :], Y[:, k, col(b, off(w) - k, WIN)])
                        else:
                            ins = pool.tensor_tensor(gx[:, k, :], Y[:, k, col(b, off(w), WIN)],
                                                     gam[:, k:k + 1].to_broadcast([P, WIN]), ALU.mult)
                    ins.then_inc(s_gx, 1)
                    if local:
                        for x in range(2):
                            pool.wait_ge(s_x1, ONE + upto(i, 2, x + 1))
                            pool.wait_ge(s_ad, ONE + upto(i, 2, x))
                            t_ = tab[:, 2 * x:2 * x + 1, bass.ds(off(w), WIN)].to_broadcast([P, HM, WIN])
                            pool.tensor_tensor(halves(ta[:, x]), halves(xe[:, x]), t_, ALU.mult).then_inc(s_a, 1)
                            pool.wait_ge(s_a, ONE + upto(i, 2, x + 1))
                            pool.wait_ge(s_rt, ONE + upto(i, 2, x + 1))
                            pool.wait_ge(s_qe if x == 0 else s_ke, ONE + i)
                            pool.tensor_tensor(tb[:, x, :], tb[:, x, :], ta[:, x, :], ALU.add).then_inc(s_ad, 1)

                prepare((0, 0, 0), 0)
                windows(pool, lambda w, i, nxt: prepare(nxt, i + 1))

            @block.tensor
            def _(pe):
                pe.wait_ge(s_load, ONE + 16 * NLOAD)
                pe.wait_ge(s_ini, ONE + 3)

                def project_q(i):
                    pe.wait_ge(s_gx, ONE + i + 1)
                    pe.wait_ge(s_x1 if local else s_qe, ONE + (2 * i if local else i))
                    for m in range(HM):
                        for k in range(DK):
                            ins = pe.matmul(p_q[:, m * WIN:(m + 1) * WIN], wq[:, k, m * P:(m + 1) * P], gx[:, k, :],
                                            start=(k == 0), stop=(k == DK - 1))
                    ins.then_inc(s_pq, 1)

                def project_k(i):
                    pe.wait_ge(s_x1 if local else s_ke, ONE + (2 * i + 1 if local else i))
                    for m in range(HM):
                        for k in range(DK):
                            ins = pe.matmul(p_k[:, m * WIN:(m + 1) * WIN], wk[:, k, m * P:(m + 1) * P], gx[:, k, :],
                                            start=(k == 0), stop=(k == DK - 1))
                    ins.then_inc(s_pk, 1)

                def project_v(i, older=True):
                    pe.wait_ge(s_ve, ONE + i)
                    pe.wait_ge(s_out, ONE + (i - 1 if older else 0))
                    for k in range(DK):
                        ins = pe.matmul(p_v[:, :], gx[:, k, :], wv[:, k, :], start=(k == 0), stop=(k == DK - 1))
                    ins.then_inc(s_pv, 1)

                def squares(i, x):
                    pe.wait_ge(s_sq, ONE + upto(i, 2, x + 1))
                    pe.wait_ge(s_n, ONE + upto(i, 2, x))
                    pe.matmul(p_ss[:, :], g["blk64"][:, :], sq[:, x, :], start=True, stop=True).then_inc(s_ss, 1)

                def turn(i, x):
                    pe.wait_ge(s_x1, ONE + upto(i, 2, x + 1))
                    pe.wait_ge(s_rt, ONE + upto(i, 2, x))
                    pe.matmul(p_ro[:, :], g["rot64"][:, :], xe[:, x, :], start=True, stop=True).then_inc(s_ro, 1)

                def scores(w, i, r):
                    if r == 0:
                        pe.wait_ge(s_qe, ONE + i + 1)
                        pe.wait_ge(s_ke, ONE + i + 1)
                    for e in range(2):
                        pe.wait_ge(s_ex, ONE + upto(i, NE, ((r - 1) * 2 + e + 1) * MH if r else 0))
                        for mi in range(MH):
                            m = r * MH + mi
                            out = p_s[e][:, mi * KW:(mi + 1) * KW]
                            if local:
                                mk = mask[:, 4, :] if w[2] else mask[:, w[1], :] if isinstance(w[1], int) else mask[:, bass.ds(w[1], 1), :]
                                pe.matmul(out, idb[:, :], mk, start=True, stop=False)
                                ins = pe.matmul(out, qt[:, e, m, :], kt[:, m, :, :], start=False, stop=True)
                            else:
                                ins = pe.matmul(out, qt[:, e, m, :], kt[:, m, 0, :], start=True, stop=True)
                        ins.then_inc(s_sc, 1)

                def transposes(i, j):
                    r, e = j // 2, j % 2
                    pe.wait_ge(s_pr, ONE + upto(i, NJ, j + 1))
                    if local:
                        pe.wait_ge(s_te[1 - e], ONE + upto(i, RN, (j + 1) // 2))
                    else:
                        pe.wait_ge(s_te[e], ONE + i)
                    flat = pr[:, r, e, :, :].rearrange("p m n -> p (m n)")
                    for x in range(4):
                        ins = pe.transpose(p_tt[e][:, x * P:(x + 1) * P], flat[:, x * P:(x + 1) * P], g["ident"][:, :])
                    ins.then_inc(s_tr, 1)

                def values(w, i, j):
                    r, e = j // 2, j % 2
                    pe.wait_ge(s_te[e], ONE + upto(i, RN, r + 1))
                    if j == 0:
                        pe.wait_ge(s_ve, ONE + i + 1)
                        pe.wait_ge(s_oe, ONE + i)
                    for mi in range(MH):
                        m = r * MH + mi
                        h = 2 * m + e
                        for x in range(KW // P):
                            ins = pe.matmul(p_o[64 * e:64 * e + 64, m * WIN:(m + 1) * WIN],
                                            v[:, x if local else w[2], h * DH:(h + 1) * DH],
                                            pt[:, e, (mi * (KW // P) + x) * P:(mi * (KW // P) + x + 1) * P],
                                            start=(x == 0), stop=(x == KW // P - 1), tile_position=(0, 64 * e))
                    ins.then_inc(s_o, 1)

                def output(i):
                    pe.wait_ge(s_oe, ONE + i + 1)
                    pe.wait_ge(s_ve, ONE + i + 2)
                    for n in range(DK):
                        for k in range(HM):
                            ins = pe.matmul(p_w[:, n * WIN:(n + 1) * WIN], wo[:, k, n * P:(n + 1) * P], os_[:, k, :],
                                            start=(k == 0), stop=(k == HM - 1))
                    ins.then_inc(s_wo, 1)

                def body(w, i, nxt):
                    n = i + 1
                    project_q(n)
                    if local:
                        scores(w, i, 1)
                        transposes(i, 0)
                        squares(n, 0)
                        project_k(n)
                        values(w, i, 0)
                        transposes(i, 1)
                        turn(n, 0)
                        squares(n, 1)
                        values(w, i, 1)
                        transposes(i, 2)
                        turn(n, 1)
                        values(w, i, 2)
                        transposes(i, 3)
                        project_v(n)
                        values(w, i, 3)
                    else:
                        project_k(n)
                        project_v(n)
                        for j in range(2):
                            transposes(i, j)
                        for j in range(2):
                            values(w, i, j)
                    scores(nxt, n, 0)
                    output(i)

                project_q(0)
                if local:
                    squares(0, 0)
                    turn(0, 0)
                project_k(0)
                if local:
                    squares(0, 1)
                    turn(0, 1)
                project_v(0, older=False)
                scores((0, 0, 0), 0, 0)
                windows(pe, body)

            @block.scalar
            def _(act):
                act.preload_act_table_set(EXP)
                act.wait_ge(s_load, ONE + 16 * NLOAD)
                act.wait_ge(s_ini, ONE + 3)

                def square(i, x):
                    act.wait_ge(s_pq if x == 0 else s_pk, ONE + i + 1)
                    act.wait_ge(s_ss, ONE + 2 * i)
                    act.activation(sq[:, x, :], (p_q, p_k)[x][:, :], ACT.Square).then_inc(s_sq, 1)

                def scaled(i, x):
                    act.wait_ge(s_ad, ONE + 2 * i)
                    act.wait_ge(s_ro, ONE + 2 * i)
                    act.activation(xe[:, x, :], (p_q, p_k)[x][:, :], ACT.Copy, scale=gam[:, x:x + 1]).then_inc(s_x1, 1)

                def roots(i):
                    act.wait_ge(s_n, ONE + 2 * i + 2)
                    act.activation(n2[:, :, :], n2[:, :, :], ACT.Ln, scale=float(2 ** LN_SHIFT)).then_inc(s_rn, 1)
                    act.wait_ge(s_rn, ONE + upto(i, 2, 1))
                    act.activation(n2[:, :, :], n2[:, :, :], ACT.Exp, scale=-0.5, bias=g["bias"][:, 1:2]).then_inc(s_rn, 1)

                def queries(i):
                    act.wait_ge(s_pq, ONE + i + 1)
                    act.wait_ge(s_sc, ONE + NJ * i)
                    for e in range(2):
                        rows = slice(64 * e, 64 * e + 64)
                        ins = act.activation(qt[rows, e, :, :].rearrange("p m n -> p (m n)"), p_q[rows, :], ACT.Copy,
                                             scale=float(DH) ** -0.5)
                    ins.then_inc(s_qe, 1)

                def value_copy(w, i):
                    act.wait_ge(s_pv, ONE + i + 1)
                    act.wait_ge(s_o, ONE + NJ * i)
                    act.activation(v[:, w[2], :], p_v[:, :], ACT.Copy).then_inc(s_ve, 1)

                def exps(i, r, e):
                    j = 2 * r + e
                    act.wait_ge(s_mx, ONE + upto(i, NJ, j + 1))
                    act.wait_ge(s_tr, ONE + NJ * i)
                    for mi in range(MH):
                        act.activation(pr[:, r, e, mi, :], p_s[e][:, mi * KW:(mi + 1) * KW], ACT.Exp,
                                       bias=nm[:, r, e, mi:mi + 1], accum_out=sm[:, r, e, mi:mi + 1]).then_inc(s_ex, 1)

                def turned(i, j):
                    act.wait_ge(s_tr, ONE + upto(i, NJ, j + 1))
                    act.wait_ge(s_o, ONE + upto(i, NJ, max(0, j - 1)))
                    act.activation(pt[:, 1, :], p_tt[1][:, :], ACT.Copy).then_inc(s_te[1], 1)

                def body(w, i, nxt):
                    n = i + 1
                    exps(i, 0, 0)
                    exps(i, 0, 1)
                    if local:
                        square(n, 0)
                        scaled(n, 0)
                        exps(i, 1, 0)
                        exps(i, 1, 1)
                        square(n, 1)
                        turned(i, 1)
                        scaled(n, 1)
                        roots(n)
                        turned(i, 3)
                    else:
                        queries(n)
                        turned(i, 1)
                    act.wait_ge(s_o, ONE + upto(i, NJ, NJ))
                    act.wait_ge(s_wo, ONE + i)
                    act.activation(os_[:, :, :].rearrange("p m n -> p (m n)"), p_o[:, :], ACT.Copy).then_inc(s_oe, 1)
                    value_copy(nxt, n)

                if local:
                    for x in range(2):
                        square(0, x)
                        scaled(0, x)
                    roots(0)
                else:
                    queries(0)
                value_copy((0, 0, 0), 0)
                windows(act, body)

            @block.vector
            def _(dve):
                dve.wait_ge(s_load, ONE + 16 * NLOAD)
                dve.wait_ge(s_ini, ONE + 3)

                def norms(i, x):
                    dve.wait_ge(s_ss, ONE + upto(i, 2, x + 1))
                    dve.wait_ge(s_qe if x == 0 else s_ke, ONE + i)
                    dve.tensor_scalar(n2[:, x, :], p_ss[:, :], NORM2_MIN, None, ALU.max).then_inc(s_n, 1)

                def rotated(w, i, x):
                    dve.wait_ge(s_ro, ONE + upto(i, 2, x + 1))
                    dve.wait_ge(s_qe if x == 0 else s_ke, ONE + i)
                    t_ = tab[:, 2 * x + 1:2 * x + 2, bass.ds(off(w), WIN)].to_broadcast([P, HM, WIN])
                    dve.tensor_tensor(halves(tb[:, x]), halves(p_ro[:, :]), t_, ALU.mult).then_inc(s_rt, 1)

                def finish(w, i, x):
                    dve.wait_ge(s_ad, ONE + upto(i, 2, x + 1))
                    dve.wait_ge(s_rn, ONE + 2 * i + 2)
                    dve.wait_ge(s_sc, ONE + NJ * i)
                    if x == 0:
                        for e in range(2):
                            rows = slice(64 * e, 64 * e + 64)
                            ins = dve.scalar_tensor_tensor(qt[rows, e, :, :], halves(tb[rows, 0]), 8.0, halves(n2[rows, 0]),
                                                           ALU.mult, ALU.mult)
                        ins.then_inc(s_qe, 1)
                    else:
                        dve.tensor_tensor(kt[:, :, w[2], :], halves(tb[:, 1]), halves(n2[:, 1]), ALU.mult).then_inc(s_ke, 1)

                def keys(i):
                    dve.wait_ge(s_pk, ONE + i + 1)
                    dve.wait_ge(s_sc, ONE + NJ * i)
                    dve.tensor_copy(kt[:, :, 0, :], halves(p_k[:, :])).then_inc(s_ke, 1)

                def maxima(i, r):
                    for e in range(2):
                        dve.wait_ge(s_sc, ONE + upto(i, NJ, 2 * r + e + 1))
                        dve.tensor_reduce(nm[:, r, e, :], p_s[e][:, :].rearrange("p (m n) -> p m n", m=MH), AX_X,
                                          ALU.max, negate=True).then_inc(s_mx, 1)

                def normalise(i, r):
                    for e in range(2):
                        j = 2 * r + e
                        dve.wait_ge(s_ex, ONE + upto(i, NE, (j + 1) * MH))
                        dve.reciprocal(sm[:, r, e, :], sm[:, r, e, :]).then_inc(s_rs, 1)
                        dve.wait_ge(s_rs, ONE + upto(i, NJ, j + 1))
                        dve.tensor_tensor(pr[:, r, e, :, :], pr[:, r, e, :, :],
                                          sm[:, r, e, :].rearrange("p (m o) -> p m o", o=1).to_broadcast([P, MH, KW]),
                                          ALU.mult).then_inc(s_pr, 1)

                def turned(i, j):
                    dve.wait_ge(s_tr, ONE + upto(i, NJ, j + 1))
                    dve.wait_ge(s_o, ONE + upto(i, NJ, max(0, j - 1)))
                    dve.tensor_copy(pt[:, 0, :], p_tt[0][:, :]).then_inc(s_te[0], 1)

                def add(w, i):
                    b = w[0]
                    dve.wait_ge(s_wo, ONE + i + 1)
                    if local:
                        dve.tensor_tensor(Z[:, :, col(b, off(w), WIN)], Y[:, :, col(b, off(w), WIN)],
                                          p_w[:, 0:DK * WIN].rearrange("p (n t) -> p n t", n=DK), ALU.add).then_inc(s_out, 1)
                    else:
                        for n in range(DK):
                            x = X[:, n, bass.ds(b * T + off(w), WIN)]
                            ins = dve.scalar_tensor_tensor(x, p_w[:, n * WIN:(n + 1) * WIN], MOD[:, 0, bass.ds(b, 1), 10 + n],
                                                           x, ALU.mult, ALU.add)
                        ins.then_inc(s_out, 1)

                def body(w, i, nxt):
                    n = i + 1
                    normalise(i, 0)
                    if local:
                        maxima(i, 1)
                        turned(i, 0)
                        norms(n, 0)
                        normalise(i, 1)
                        rotated(nxt, n, 0)
                        norms(n, 1)
                        turned(i, 2)
                        rotated(nxt, n, 1)
                        finish(nxt, n, 0)
                        finish(nxt, n, 1)
                    else:
                        keys(n)
                        turned(i, 0)
                    maxima(n, 0)
                    add(w, i)

                if local:
                    for x in range(2):
                        norms(0, x)
                        rotated((0, 0, 0), 0, x)
                    for x in range(2):
                        finish((0, 0, 0), 0, x)
                else:
                    keys(0)
                maxima(0, 0)
                windows(dve, body)


def routed_stage(nc, g, d):
    with ExitStack() as ctx:
        s = Scope(nc, ctx, "rt")
        NTL = T // P
        wq, wk, wv = (s.sb(n, [P, DK, HID]) for n in ("wq", "wk", "wv"))
        wo = s.sb("wo", [P, HM, D])
        gam = s.sb("gam", [P, DK])
        hb = s.sb("hb", [P, DK, T])
        xt = s.sb("xt", [P, NTL, D])
        gk, gq = s.sb("gk", [P, NTL, NKV]), s.sb("gq", [P, NTL, NQ])
        ck, cq = s.sb("ck", [P, DK, NKV]), s.sb("cq", [P, DK, NQ])
        fs = s.sb("fs", [P, NKV // P])
        kT, qT = s.sb("kT", [P, HM, NKV]), s.sb("qT", [P, HM, NQ])
        v = s.sb("v", [P, NKV // P, HID])
        pr, pt = s.sb("pr", [P, 2, NKV]), s.sb("pt", [P, 2, NKV])
        nm, sm = s.sb("nm", [P, 2]), s.sb("sm", [P, 2])
        os_ = s.sb("os", [P, 2, HM, P])
        rt = s.sb("rt", [P, 2, D])
        sb_, fb = s.sb("sb", [P, T]), s.sb("fb", [P, T])
        st = s.sb("st", [P, 2, T])
        iota, iop = s.sb("iota", [P, NKV]), s.sb("iop", [P, 2])
        pa = [s.ps(f"pa{i}") for i in range(2)]
        ps, p_t, p_o, p_f = [s.ps(f"ps{i}") for i in range(2)], s.ps("p_t"), s.ps("p_o"), s.ps("p_f")
        names = "load in tr te oh ga ge f fe pj pe sc mx ex rs pr tp tc o oe r re st x out".split()
        (s_load, s_in, s_tr, s_te, s_oh, s_ga, s_ge, s_f, s_fe, s_pj, s_pe, s_sc, s_mx, s_ex, s_rs, s_pr,
         s_tp, s_tc, s_o, s_oe, s_r, s_re, s_st, s_x, s_out) = (s.sem(x) for x in names)
        X, Y, MOD, SLOT, FAC = g["X"], g["Y"], g["MOD"], g["SLOT"], g["FAC"]
        NU = 2 * HEADS

        with nc.Block() as block:
            @block.sync
            def _(sp):
                src = d["heavy"]
                for dst, name in ((wq, "wq"), (wk, "wk"), (wv, "wv"), (wo, "wo")):
                    sp.dma_start(dst[:, :, :], src[name].rearrange("(k p) n -> p k n", p=P)).then_inc(s_load, 16)
                for dst, a in ((gam, src["gam"]), (iota, d["iota"]), (iop, d["iop"])):
                    sp.dma_start(dst[:, :], a).then_inc(s_load, 16)
                with sp.Fori(0, B) as b:
                    sp.wait_ge(s_out, ONE + 4 * b)
                    sp.dma_start(hb[:, :, :], Y[:, :, col(b, 0, T)]).then_inc(s_in, 16)
                    sp.dma_start(sb_[:, :], g["slot_dram"][bass.ds(2 * b, 1), :].to_broadcast([P, T])).then_inc(s_in, 16)
                    sp.dma_start(fb[:, :], g["f_dram"][bass.ds(2 * b, 1), :].to_broadcast([P, T])).then_inc(s_in, 16)

            @block.tensor
            def _(pe):
                pe.wait_ge(s_load, ONE + 16 * 7)
                with pe.Fori(0, B) as b:
                    pe.wait_ge(s_in, ONE + 48 * b + 48)
                    pe.wait_ge(s_x, ONE + 4 * b)
                    for n in range(4):
                        if n >= 2:
                            pe.wait_ge(s_te, ONE + upto(b, 4, n - 1))
                        for q in range(2):
                            for k in range(DK):
                                t = 2 * n + q
                                ins = pe.transpose(pa[n % 2][:, q * D + k * P:q * D + (k + 1) * P], hb[:, k, t * P:(t + 1) * P],
                                                   g["ident"][:, :])
                        ins.then_inc(s_tr, 1)
                    pe.wait_ge(s_te, ONE + upto(b, 4, 4))
                    pe.wait_ge(s_oh, ONE + 2 * NTL * b + 2 * NTL)
                    for k in range(DK):
                        for t in range(NTL):
                            ins = pe.matmul(pa[k][:, :], xt[:, t, k * P:(k + 1) * P], gk[:, t, :], start=(t == 0), stop=(t == NTL - 1))
                        ins.then_inc(s_ga, 1)
                    for k in range(DK):
                        for t in range(NTL):
                            ins = pe.matmul(ps[0][:, k * NQ:(k + 1) * NQ], xt[:, t, k * P:(k + 1) * P], gq[:, t, :],
                                            start=(t == 0), stop=(t == NTL - 1))
                    ins.then_inc(s_ga, 1)
                    for m in range(NKV // P):
                        for t in range(NTL):
                            ins = pe.matmul(p_f[:, m:m + 1], gk[:, t, m * P:(m + 1) * P], FAC[:, bass.ds(t * 8 + 2 * b + 1, 1)],
                                            start=(t == 0), stop=(t == NTL - 1))
                    ins.then_inc(s_f, 1)
                    pe.wait_ge(s_ge, ONE + upto(b, 3, 3))
                    pe.wait_ge(s_fe, ONE + b + 1)
                    n = 0
                    for m in range(HM):
                        if n >= 2:
                            pe.wait_ge(s_pe, ONE + upto(b, 10, n - 1))
                        for k in range(DK):
                            ins = pe.matmul(pa[n % 2][:, :], wk[:, k, m * P:(m + 1) * P], ck[:, k, :], start=(k == 0), stop=(k == DK - 1))
                        ins.then_inc(s_pj, 1)
                        n += 1
                    for m in range(NKV // P):
                        pe.wait_ge(s_pe, ONE + upto(b, 10, n - 1))
                        for k in range(DK):
                            ins = pe.matmul(pa[n % 2][:, :], ck[:, k, m * P:(m + 1) * P], wv[:, k, :], start=(k == 0), stop=(k == DK - 1))
                        ins.then_inc(s_pj, 1)
                        n += 1
                    for m2 in range(2):
                        pe.wait_ge(s_pe, ONE + upto(b, 10, n - 1))
                        for m in (2 * m2, 2 * m2 + 1):
                            for k in range(DK):
                                ins = pe.matmul(pa[n % 2][:, (m % 2) * NQ:(m % 2 + 1) * NQ], wq[:, k, m * P:(m + 1) * P], cq[:, k, :],
                                                start=(k == 0), stop=(k == DK - 1))
                        ins.then_inc(s_pj, 1)
                        n += 1
                    pe.wait_ge(s_pe, ONE + upto(b, 10, 10))

                    def score(j):
                        qt_, h = divmod(j, HEADS)
                        m, e = divmod(h, 2)
                        rows = slice(64 * e, 64 * e + 64)
                        if j >= 2:
                            pe.wait_ge(s_ex, ONE + upto(b, NU, j - 1))
                        pe.matmul(ps[j % 2][:, :], qT[rows, m, qt_ * P:(qt_ + 1) * P], kT[rows, m, :], start=True, stop=True)\
                          .then_inc(s_sc, 1)

                    score(0)
                    for j in range(NU):
                        qt_, h = divmod(j, HEADS)
                        m, e = divmod(h, 2)
                        if j + 1 < NU:
                            score(j + 1)
                        pe.wait_ge(s_pr, ONE + upto(b, NU, j + 1))
                        pe.wait_ge(s_tc, ONE + upto(b, NU, j))
                        for x in range(4):
                            ins = pe.transpose(p_t[:, x * P:(x + 1) * P], pr[:, j % 2, x * P:(x + 1) * P], g["ident"][:, :])
                        ins.then_inc(s_tp, 1)
                        pe.wait_ge(s_tc, ONE + upto(b, NU, j + 1))
                        if h == 0:
                            pe.wait_ge(s_oe, ONE + upto(b, 2, qt_))
                        for x in range(4):
                            ins = pe.matmul(p_o[64 * e:64 * e + 64, m * P:(m + 1) * P], v[:, x, h * DH:(h + 1) * DH],
                                            pt[:, j % 2, x * P:(x + 1) * P], start=(x == 0), stop=(x == 3), tile_position=(0, 64 * e))
                        ins.then_inc(s_o, 1)
                    for q in range(2):
                        pe.wait_ge(s_oe, ONE + upto(b, 2, q + 1))
                        for k in range(HM):
                            ins = pe.matmul(pa[q][:, 0:D], os_[:, q, k, :], wo[:, k, :], start=(k == 0), stop=(k == HM - 1))
                        ins.then_inc(s_r, 1)
                    pe.wait_ge(s_re, ONE + upto(b, 2, 2))
                    pe.wait_ge(s_st, ONE + upto(b, 2, 2))
                    n = 0
                    for k in range(DK):
                        for hf in range(2):
                            if n >= 2:
                                pe.wait_ge(s_x, ONE + upto(b, 4, n - 1))
                            for q in range(2):
                                ins = pe.matmul(pa[n % 2][:, :], rt[:, q, k * P:(k + 1) * P], st[:, q, hf * 512:(hf + 1) * 512],
                                                start=(q == 0), stop=(q == 1))
                            ins.then_inc(s_out, 1)
                            n += 1

            @block.scalar
            def _(act):
                act.wait_ge(s_load, ONE + 16 * 7)
                with act.Fori(0, B) as b:
                    for n in range(4):
                        act.wait_ge(s_tr, ONE + upto(b, 4, n + 1))
                        act.activation(xt[:, 2 * n:2 * n + 2, :].rearrange("p t n -> p (t n)"), pa[n % 2][:, :], ACT.Copy).then_inc(s_te, 1)
                    for k in range(DK):
                        act.wait_ge(s_ga, ONE + upto(b, 3, k + 1))
                        act.activation(ck[:, k, :], pa[k][:, :], ACT.Copy, scale=gam[:, k:k + 1]).then_inc(s_ge, 1)
                    act.wait_ge(s_ga, ONE + upto(b, 3, 3))
                    for k in range(DK):
                        ins = act.activation(cq[:, k, :], ps[0][:, k * NQ:(k + 1) * NQ], ACT.Copy, scale=gam[:, k:k + 1])
                    ins.then_inc(s_ge, 1)
                    for n in range(HM):
                        act.wait_ge(s_pj, ONE + upto(b, 10, n + 1))
                        act.activation(kT[:, n, :], pa[n % 2][:, :], ACT.Copy).then_inc(s_pe, 1)
                    act.wait_ge(s_fe, ONE + b + 1)
                    for n in range(NKV // P):
                        act.wait_ge(s_pj, ONE + upto(b, 10, n + 5))
                        act.activation(v[:, n, :], pa[n % 2][:, :], ACT.Copy, scale=fs[:, n:n + 1]).then_inc(s_pe, 1)
                    for n in range(2):
                        act.wait_ge(s_pj, ONE + upto(b, 10, n + 9))
                        act.activation(qT[:, 2 * n:2 * n + 2, :].rearrange("p m n -> p (m n)"), pa[n % 2][:, :], ACT.Copy,
                                       scale=float(DH) ** -0.5).then_inc(s_pe, 1)
                    for j in range(NU):
                        act.wait_ge(s_mx, ONE + upto(b, NU, j + 1))
                        if j >= 2:
                            act.wait_ge(s_tp, ONE + upto(b, NU, j - 1))
                        act.activation(pr[:, j % 2, :], ps[j % 2][:, :], ACT.Exp, bias=nm[:, j % 2:j % 2 + 1],
                                       accum_out=sm[:, j % 2:j % 2 + 1]).then_inc(s_ex, 1)
                        if j % HEADS == HEADS - 1:
                            q = j // HEADS
                            act.wait_ge(s_o, ONE + upto(b, NU, j + 1))
                            act.activation(os_[:, q, :, :].rearrange("p m n -> p (m n)"), p_o[:, :], ACT.Copy).then_inc(s_oe, 1)
                    for q in range(2):
                        act.wait_ge(s_r, ONE + upto(b, 2, q + 1))
                        act.activation(rt[:, q, :], pa[q][:, 0:D], ACT.Copy).then_inc(s_re, 1)

            @block.vector
            def _(dve):
                dve.wait_ge(s_load, ONE + 16 * 7)
                with dve.Fori(0, B) as b:
                    for t in range(NTL):
                        dve.tensor_scalar(gk[:, t, :], iota[:, :], SLOT[:, bass.ds(t * 8 + 2 * b + 1, 1)], None,
                                          ALU.is_equal).then_inc(s_oh, 1)
                        dve.tensor_scalar(gq[:, t, :], iota[:, 0:NQ], SLOT[:, bass.ds(t * 8 + 2 * b, 1)], None,
                                          ALU.is_equal).then_inc(s_oh, 1)
                    dve.wait_ge(s_in, ONE + 48 * b + 48)
                    for q in range(2):
                        dve.scalar_tensor_tensor(st[:, q, :], sb_[:, :], iop[:, q:q + 1], fb[:, :], ALU.is_equal,
                                                 ALU.mult).then_inc(s_st, 1)
                    dve.wait_ge(s_f, ONE + b + 1)
                    dve.tensor_copy(fs[:, :], p_f[:, 0:NKV // P]).then_inc(s_fe, 1)
                    for j in range(NU):
                        dve.wait_ge(s_sc, ONE + upto(b, NU, j + 1))
                        dve.tensor_reduce(nm[:, j % 2:j % 2 + 1], ps[j % 2][:, :], AX_X, ALU.max, negate=True).then_inc(s_mx, 1)
                        dve.wait_ge(s_ex, ONE + upto(b, NU, j + 1))
                        dve.reciprocal(sm[:, j % 2:j % 2 + 1], sm[:, j % 2:j % 2 + 1]).then_inc(s_rs, 1)
                        dve.wait_ge(s_rs, ONE + upto(b, NU, j + 1))
                        dve.tensor_scalar(pr[:, j % 2, :], pr[:, j % 2, :], sm[:, j % 2:j % 2 + 1], None, ALU.mult).then_inc(s_pr, 1)
                        dve.wait_ge(s_tp, ONE + upto(b, NU, j + 1))
                        if j >= 2:
                            dve.wait_ge(s_o, ONE + upto(b, NU, j - 1))
                        dve.tensor_copy(pt[:, j % 2, :], p_t[:, :]).then_inc(s_tc, 1)
                    n = 0
                    for k in range(DK):
                        for hf in range(2):
                            dve.wait_ge(s_out, ONE + upto(b, 4, n + 1))
                            x = X[:, k, bass.ds(b * T + hf * 512, 512)]
                            dve.scalar_tensor_tensor(x, pa[n % 2][:, :], MOD[:, 0, bass.ds(b, 1), 10 + k], x, ALU.mult,
                                                     ALU.add).then_inc(s_x, 1)
                            n += 1


def mixing_stage(nc, g, d):
    with ExitStack() as ctx:
        s = Scope(nc, ctx, "mx")
        wv, wr, wo = (s.sb(n, [P, DK, D]) for n in ("wv", "wr", "wo"))
        pv = s.sb("pv", [P, 3, DK])
        dd, om = s.sb("dd", [P, DK]), s.sb("om", [P, 2, DK])
        st = s.sb("st", [P, DK, TP])
        tv = s.sb("tv", [P, 2, DK, T])
        inp = s.sb("inp", [P, 2, DK, T])
        vv, rr, oo = (s.sb(n, [P, DK, 512]) for n in ("vv", "rr", "oo"))
        p_v, p_r, p_w = ([s.ps(f"{n}{k}") for k in range(DK)] for n in ("p_v", "p_r", "p_w"))
        names = "load ini d om scan t in v r ve re w oo x".split()
        s_load, s_ini, s_d, s_om, s_scan, s_t, s_in, s_v, s_r, s_ve, s_re, s_w, s_oo, s_x = (s.sem(x) for x in names)
        X, Y, MOD = g["X"], g["Y"], g["MOD"]

        with nc.Block() as block:
            @block.sync
            def _(sp):
                for dst, name in ((wv, "WvT"), (wr, "WrT"), (wo, "WoT")):
                    sp.dma_start(dst[:, :, :], d["mix"][name].rearrange("(k p) n -> p k n", p=P)).then_inc(s_load, 16)
                sp.dma_start(pv[:, :, :], d["mix"]["vec"]).then_inc(s_load, 16)

            @block.gpsimd
            def _(pool):
                pool.wait_ge(s_load, ONE + 64)
                pool.memset(st[:, :, 0:1], 0.0).then_inc(s_ini, 1)
                pool.tensor_scalar(om[:, :, :], pv[:, 1:3, :], -1.0, 1.0, ALU.mult, ALU.add).then_inc(s_om, 1)
                pool.wait_ge(s_om, ONE + 1)
                pool.wait_ge(s_ini, ONE + 1)
                with pool.Fori(0, B) as b:
                    for k in range(DK):
                        pool.wait_ge(s_scan, ONE + upto(b, DK, k + 1))
                        pool.wait_ge(s_in, ONE + 4 * b)
                        for n in range(2):
                            pool.tensor_tensor(tv[:, n, k, :], st[:, k, 0:T], om[:, n, k:k + 1].to_broadcast([P, T]), ALU.mult).then_inc(s_t, 1)

            @block.tensor
            def _(pe):
                pe.wait_ge(s_load, ONE + 64)
                with pe.Fori(0, B) as b:
                    pe.wait_ge(s_in, ONE + 4 * b + 4)
                    for c in range(2):
                        cs = slice(c * 512, (c + 1) * 512)
                        for m in range(DK):
                            pe.wait_ge(s_ve, ONE + upto(b, 4, 2 * c))
                            for k in range(DK):
                                ins = pe.matmul(p_v[m][:, :], wv[:, k, m * P:(m + 1) * P], inp[:, 0, k, cs], start=(k == 0), stop=(k == DK - 1))
                            ins.then_inc(s_v, 1)
                        for m in range(DK):
                            pe.wait_ge(s_re, ONE + upto(b, 4, 2 * c))
                            for k in range(DK):
                                ins = pe.matmul(p_r[m][:, :], wr[:, k, m * P:(m + 1) * P], inp[:, 1, k, cs], start=(k == 0), stop=(k == DK - 1))
                            ins.then_inc(s_r, 1)
                        pe.wait_ge(s_ve, ONE + upto(b, 4, 2 * c + 2))
                        for m in range(DK):
                            pe.wait_ge(s_oo, ONE + upto(b, 4, 2 * c))
                            for k in range(DK):
                                ins = pe.matmul(p_w[m][:, :], wo[:, k, m * P:(m + 1) * P], vv[:, k, :], start=(k == 0), stop=(k == DK - 1))
                            ins.then_inc(s_w, 1)

            @block.scalar
            def _(act):
                act.wait_ge(s_load, ONE + 64)
                act.activation(dd[:, :], pv[:, 0, :], ACT.Exp).then_inc(s_d, 1)
                act.wait_ge(s_d, ONE + 1)
                act.activation(dd[:, :], dd[:, :], ACT.Exp, scale=-1.0).then_inc(s_d, 1)
                with act.Fori(0, B) as b:
                    for c in range(2):
                        for m in range(DK):
                            act.wait_ge(s_v, ONE + upto(b, 4, 2 * c + m + 1))
                            act.wait_ge(s_w, ONE + upto(b, 4, 2 * c))
                            act.activation(vv[:, m, :], p_v[m][:, :], ACT.Copy).then_inc(s_ve, 1)
                        for m in range(DK):
                            act.wait_ge(s_r, ONE + upto(b, 4, 2 * c + m + 1))
                            act.wait_ge(s_oo, ONE + upto(b, 4, 2 * c))
                            act.activation(rr[:, m, :], p_r[m][:, :], ACT.Sigmoid).then_inc(s_re, 1)

            @block.vector
            def _(dve):
                dve.wait_ge(s_load, ONE + 64)
                dve.wait_ge(s_d, ONE + 2)
                dve.wait_ge(s_ini, ONE + 1)
                with dve.Fori(0, B) as b:
                    for k in range(DK):
                        dve.wait_ge(s_t, ONE + 4 * b)
                        dve.tensor_tensor_scan(st[:, k, 1:TP], dd[:, k:k + 1].to_broadcast([P, T]), Y[:, k, col(b, 0, T)],
                                               0.0, ALU.mult, ALU.add).then_inc(s_scan, 1)
                    dve.wait_ge(s_r, ONE + 4 * b)
                    for k in range(DK):
                        for n in range(2):
                            dve.wait_ge(s_t, ONE + upto(b, 4, 2 * k + n + 1))
                            dve.scalar_tensor_tensor(inp[:, n, k, :], Y[:, k, col(b, 0, T)], pv[:, n + 1, k:k + 1],
                                                     tv[:, n, k, :], ALU.mult, ALU.add).then_inc(s_in, 1)
                    for c in range(2):
                        for m in range(DK):
                            dve.wait_ge(s_w, ONE + upto(b, 4, 2 * c + m + 1))
                            dve.wait_ge(s_re, ONE + upto(b, 4, 2 * c + m + 1))
                            dve.wait_ge(s_x, ONE + upto(b, 4, 2 * c))
                            dve.tensor_tensor(oo[:, m, :], p_w[m][:, :], rr[:, m, :], ALU.mult).then_inc(s_oo, 1)
                            dve.wait_ge(s_oo, ONE + upto(b, 4, 2 * c + m + 1))
                            x = X[:, m, bass.ds(b * T + c * 512, 512)]
                            dve.scalar_tensor_tensor(x, oo[:, m, :], MOD[:, 1, bass.ds(b, 1), 4 + m], x, ALU.mult,
                                                     ALU.add).then_inc(s_x, 1)


def mlp_stage(nc, g, d, tag, layer):
    with ExitStack() as ctx:
        s = Scope(nc, ctx, tag)
        w1 = s.sb("w1", [P, DK, 2, FM * P])
        w2 = s.sb("w2", [P, FM, D])
        vec = s.sb("vec", [P, 2 * FM + 3 * DK])
        xc, sq, hn = (s.sb(n, [P, DK, NB]) for n in ("xc", "sq", "hn"))
        lv, rs = s.sb("lv", [P, NB]), s.sb("rs", [P, NB])
        ge = s.sb("ge", [P, 2, NB])
        hh = s.sb("hh", [P, FM, NB])
        p_mean, p_var = s.ps("p_mean"), s.ps("p_var")
        p_a, p_g = ([s.ps(f"{n}{k}") for k in range(2)] for n in ("p_a", "p_g"))
        p_w = [s.ps(f"p_w{k}") for k in range(DK)]
        names = "load mean xc sq var rs a v hn a_ ge hh w y".split()
        s_load, s_mean, s_xc, s_sq, s_var, s_rs, s_l, s_v, s_hn, s_a, s_ge, s_hh, s_w, s_y = (s.sem("s" + x) for x in names)
        Y, Z = g["Y"], g["Z"]
        V_B2, V_G, V_B = 2 * FM, 2 * FM + DK, 2 * FM + 2 * DK

        def blocks(eng, body):
            with eng.Fori(0, B) as b:
                body((b, 0), b * NBLK, (b, 1))
                body((b, 1), b * NBLK + 1, (b + 1, 0))

        with nc.Block() as block:
            @block.sync
            def _(sp):
                src = d["mlp"][layer]
                sp.dma_start(w1[:, :, :, :], src["w1"].rearrange("(k p) a n -> p k a n", p=P)).then_inc(s_load, 16)
                sp.dma_start(w2[:, :, :], src["w2"].rearrange("(k p) n -> p k n", p=P)).then_inc(s_load, 16)
                sp.dma_start(vec[:, :], src["vec"]).then_inc(s_load, 16)

            @block.tensor
            def _(pe):
                def mean(w, i):
                    pe.wait_ge(s_xc, ONE + 2 * i)
                    for k in range(DK):
                        ins = pe.matmul(p_mean[:, :], g["ones"][:, :], Z[:, k, col(w[0], w[1] * NB - k, NB)],
                                        start=(k == 0), stop=(k == DK - 1))
                    ins.then_inc(s_mean, 1)

                def variance(i):
                    pe.wait_ge(s_sq, ONE + i + 1)
                    pe.wait_ge(s_l, ONE + i)
                    for k in range(DK):
                        ins = pe.matmul(p_var[:, :], g["ones"][:, :], sq[:, k, :], start=(k == 0), stop=(k == DK - 1))
                    ins.then_inc(s_var, 1)

                def body(w, i, nxt):
                    pe.wait_ge(s_hn, ONE + i + 1)
                    for m in range(FM):
                        if m == 0:
                            mean(nxt, i + 1)
                        if m == FM - 2:
                            variance(i + 1)
                        for x, pp in enumerate((p_a, p_g)):
                            pe.wait_ge((s_hh, s_ge)[x], ONE + upto(i, FM, max(0, m - 1)))
                            for k in range(DK):
                                ins = pe.matmul(pp[m % 2][:, :], w1[:, k, x, m * P:(m + 1) * P], hn[:, k, :], start=(k == 0), stop=(k == DK - 1))
                            ins.then_inc(s_a, 1)
                    pe.wait_ge(s_y, ONE + upto(i, DK, 0))
                    for part in (range(FM - 1), range(FM - 1, FM)):
                        pe.wait_ge(s_hh, ONE + upto(i, FM, part[-1] + 1))
                        for n in range(DK):
                            for k in part:
                                ins = pe.matmul(p_w[n][:, :], w2[:, k, n * P:(n + 1) * P], hh[:, k, :], start=(k == 0), stop=(k == FM - 1))
                            if k == FM - 1:
                                ins.then_inc(s_w, 1)

                mean((0, 0), 0)
                variance(0)
                pe.wait_ge(s_load, ONE + 48)
                blocks(pe, body)

            @block.scalar
            def _(act):
                def square(i):
                    act.wait_ge(s_xc, ONE + 2 * i + 2)
                    act.wait_ge(s_var, ONE + i)
                    act.activation(sq[:, :, :], xc[:, :, :], ACT.Square).then_inc(s_sq, 1)

                def root(i):
                    act.wait_ge(s_var, ONE + i + 1)
                    act.wait_ge(s_v, ONE + 2 * i)
                    act.activation(lv[:, :], p_var[:, :], ACT.Ln, bias=g["bias"][:, 0:1]).then_inc(s_l, 1)
                    act.wait_ge(s_l, ONE + i + 1)
                    act.activation(rs[:, :], lv[:, :], ACT.Exp, scale=-0.5).then_inc(s_rs, 1)

                def body(w, i, nxt):
                    for m in range(FM):
                        if m == 2:
                            square(i + 1)
                        act.wait_ge(s_a, ONE + upto(i, 2 * FM, 2 * m + 2))
                        act.wait_ge(s_hh, ONE + upto(i, FM, max(0, m - 1)))
                        act.activation(ge[:, m % 2, :], p_g[m % 2][:, :], ACT.Gelu, bias=vec[:, FM + m:FM + m + 1]).then_inc(s_ge, 1)
                    root(i + 1)

                square(0)
                root(0)
                act.wait_ge(s_load, ONE + 48)
                blocks(act, body)

            @block.vector
            def _(dve):
                def centre(w, i):
                    dve.wait_ge(s_hn, ONE + i)
                    dve.wait_ge(s_mean, ONE + i + 1)
                    for k in range(DK):
                        dve.tensor_tensor(xc[:, k, :], Z[:, k, col(w[0], w[1] * NB - k, NB)], p_mean[:, :], ALU.subtract).then_inc(s_xc, 1)

                def norm(i):
                    link = Chain(dve, s_v, i, 2)
                    dve.wait_ge(s_rs, ONE + i + 1)
                    for k in range(DK):
                        link(dve.tensor_tensor(xc[:, k, :], xc[:, k, :], rs[:, :], ALU.mult))
                    dve.wait_ge(s_a, ONE + 2 * FM * i)
                    for k in range(DK):
                        ins = dve.tensor_scalar(hn[:, k, :], xc[:, k, :], vec[:, V_G + k:V_G + k + 1], vec[:, V_B + k:V_B + k + 1],
                                                ALU.mult, ALU.add)
                    ins.then_inc(s_hn, 1)

                def body(w, i, nxt):
                    for m in range(FM):
                        if m == 1:
                            centre(nxt, i + 1)
                        dve.wait_ge(s_w, ONE + DK * i)
                        dve.wait_ge(s_ge, ONE + upto(i, FM, m + 1))
                        dve.scalar_tensor_tensor(hh[:, m, :], p_a[m % 2][:, :], vec[:, m:m + 1], ge[:, m % 2, :], ALU.add,
                                                 ALU.mult).then_inc(s_hh, 1)
                    norm(i + 1)
                    for n in range(DK):
                        dve.wait_ge(s_w, ONE + upto(i, DK, n + 1))
                        dve.scalar_tensor_tensor(Y[:, n, col(w[0], w[1] * NB, NB)], p_w[n][:, :], vec[:, V_B2 + n:V_B2 + n + 1],
                                                 Z[:, n, col(w[0], w[1] * NB, NB)], ALU.add, ALU.add).then_inc(s_y, 1)

                dve.wait_ge(s_load, ONE + 48)
                centre((0, 0), 0)
                norm(0)
                blocks(dve, body)


def output_stage(nc, g, d, out, last=True):
    with ExitStack() as ctx:
        s = Scope(nc, ctx, "out")
        s_x, s_out = s.sem("x"), s.sem("o")
        X, Y, MOD = g["X"], g["Y"], g["MOD"]
        with nc.Block() as block:
            @block.vector
            def _(dve):
                with dve.Fori(0, B) as b:
                    for k in range(DK):
                        x = X[:, k, bass.ds(b * T, T)]
                        if last:
                            ins = dve.scalar_tensor_tensor(x, Y[:, k, col(b, 0, T)], MOD[:, 1, bass.ds(b, 1), 10 + k], x, ALU.mult, ALU.add)
                        else:
                            ins = dve.tensor_copy(x, x)
                        ins.then_inc(s_x, 1)

            @block.sync
            def _(sp):
                with sp.Fori(0, B) as b:
                    for k in range(DK):
                        sp.wait_ge(s_x, ONE + upto(b, DK, k + 1))
                        sp.dma_start(out[k * P:(k + 1) * P, bass.ds(b * T, T)], X[:, k, bass.ds(b * T, T)]).then_inc(s_out, 16)
                sp.wait_ge(s_out, ONE + 16 * B * DK)


def build(nc, d, out, stages=99, dump=None):
    with ExitStack() as ctx:
        g = {}

        def keep(name, shape, dt=F32):
            g[name] = ctx.enter_context(nc.sbuf_tensor(f"g_{name}", shape, dt))

        keep("X", [P, DK, B * T])
        keep("MOD", [P, 2, B, 12])
        keep("SLOT", [P, 64])
        keep("FAC", [P, 64])
        keep("bias", [P, 4])
        for name in ("ones", "ident", "blk64", "rot64"):
            keep(name, [P, P])
        for name in ("s_dram", "slot_dram", "f_dram"):
            g[name] = nc.dram_tensor(name, [2 * B, T], F32, kind="Internal").ap()
        g["part_dram"] = nc.dram_tensor("part_dram", [3, 2, B * A_G, 64, T], BF16, kind="Internal").ap()
        g["v_dram"] = nc.dram_tensor("v_dram", [B * A_G, T // P, P, P], F32, kind="Internal").ap()
        modulation_stage(nc, g, d)
        if stages >= 1:
            with ExitStack() as c1:
                g["OA"] = c1.enter_context(nc.sbuf_tensor("g_OA", [P, A_G * B, T], F32))
                split_stage(nc, g, d)
                causal_stage(nc, g, d)
        keep("Y", [P, DK, B * TP + WIN + 1])
        zero_columns(nc, g, "Y")
        if stages >= 2:
            norm_stage(nc, g, d, "n1", 0, 1, route=True)
            routing_stage(nc, g, d)
            window_stage(nc, g, d, "li", False)
        if stages >= 3:
            routed_stage(nc, g, d)
        if stages >= 4:
            norm_stage(nc, g, d, "n2", 1, 0)
            mixing_stage(nc, g, d)
        if stages >= 5:
            g["Z"] = ctx.enter_context(nc.sbuf_tensor("g_Z", [P, DK, B * TP + NB + 1], F32))
            zero_columns(nc, g, "Z")
            norm_stage(nc, g, d, "n3", 1, 1)
            for layer in range(2):
                window_stage(nc, g, d, f"lo{layer}", True, layer)
                mlp_stage(nc, g, d, f"ml{layer}", layer)
        output_stage(nc, g, d, out, last=stages >= 5)


def zero_columns(nc, g, name):
    with ExitStack() as ctx:
        s_zero = Scope(nc, ctx, "zc" + name).sem("zero")
        with nc.Block() as block:
            @block.gpsimd
            def _(pool):
                for b in range(B):
                    pool.memset(g[name][:, :, b * TP:b * TP + 1], 0.0).then_inc(s_zero, 1)
                pool.memset(g[name][:, :, B * TP:], 0.0).then_inc(s_zero, 1)
                pool.wait_ge(s_zero, ONE + B + 1)


def constants():
    def bf(v):
        return (np.ascontiguousarray(v, np.float32).view(np.uint32) >> 16).astype(np.uint16)

    i = np.arange(P)
    c = {"ones": np.full((P, P), 1.0 / D, np.float32), "ident": np.eye(P, dtype=np.float32)}
    c["blk64"] = (i[:, None] // 64 == i[None, :] // 64).astype(np.float32)
    rot = np.zeros((P, P), np.float32)
    for p in range(P):
        rot[p + 32 if p % 64 < 32 else p - 32, p] = -1.0 if p % 64 < 32 else 1.0
    c["rot64"] = rot
    c["idb"] = bf(np.eye(P))
    c["mqk"] = bf(np.where(i[None, :] > i[:, None], NEG, 0.0))
    c["mkq"] = bf(np.where(i[None, :] > i[:, None], NEG, 0.0).T)
    den = np.zeros((P, P), np.float32)
    den[(i // 32) * 32 + 16, i] = 1.0
    c["den"] = den
    c["blk16"] = (i[:, None] // 16 == i[None, :] // 16).astype(np.float32)
    c["low16"] = ((i[:, None] // 16 == i[None, :] // 16) & (i[:, None] < i[None, :])).astype(np.float32)
    rc = np.zeros((P, 4), np.float32)
    for p in range(P):
        num = (NQ, NKV)[(p // 16) % 2]
        k = min(num * FETCH, T)
        rc[p, :3] = np.log(T / k), np.log(k), num
    c["rc"] = rc
    c["bits"] = np.tile(np.array([1 << max(29 - n, 0) for n in range(32)], np.int32), (P, 1))
    cur = np.where(i[None, :] > i[:, None], NEG, 0.0)
    prev = np.where(i[None, :] < i[:, None], NEG, 0.0)
    none = np.full((P, P), NEG)
    m = [np.concatenate([cur, none], 1)] + [np.concatenate([cur, prev], 1)] * 3 + [np.concatenate([prev, cur], 1)]
    c["mask"] = bf(np.stack(m, 1))
    half = np.arange(0, DH, 2, dtype=np.float32)
    inv = (1.0 / 10000.0 ** (half / DH)).astype(np.float32)
    t = np.arange(T, dtype=np.float32)
    fr = (t[:, None] * inv[None, :]).astype(np.float32)
    fr = np.concatenate([fr, fr], -1)
    base = ((half + np.float32(0.4 * DH)) / np.float32(1.4 * DH)).astype(np.float32)
    power = ((t - T // 2) / np.float32(WIN // 2)).astype(np.float32)
    sc = (base[None, :] ** power[:, None]).astype(np.float32)
    sc = np.concatenate([sc, sc], -1)
    cos, sin = np.cos(fr), np.sin(fr)
    tabs = [cos * sc, sin * sc, cos / sc, sin / sc]
    c["tab"] = np.ascontiguousarray(np.stack([np.concatenate([x.T, x.T], 0) for x in tabs], 1)).astype(np.float32)
    c["iota"] = np.tile(np.arange(NKV, dtype=np.float32), (P, 1))
    c["iop"] = np.stack([i, i + P], 1).astype(np.float32)
    return c


STAGES = 99


def kernel(**a):
    import concourse.bacc as _bacc
    from concourse.bass_utils import run_bass_kernel_spmd as _run

    a = {k: np.asarray(v) for k, v in a.items()}
    f32 = np.float32

    def cols(v):
        return np.ascontiguousarray(v.reshape(-1, P).T)

    def head_rows(w):
        out = np.zeros((A_H, 32) + w.shape[1:], f32)
        out[:, :A_HD] = w.reshape((A_H, A_HD) + w.shape[1:])
        return out.reshape((A_H * 32,) + w.shape[1:])

    h = {"xT": a["L0_attn_x"].reshape(B * T, D).T}
    for l in range(2):
        h[f"cT{l}"] = a[f"L{l}_c"].T
        h[f"wmod{l}"] = a[f"L{l}_wmod"]
    h["wqk"] = np.concatenate([a["L0_attn_Wq"].T, a["L0_attn_Wk"].T], 1).reshape(D, 4, P)
    h["bqk"] = np.concatenate([cols(a["L0_attn_bq"]), cols(a["L0_attn_bk"])], 1)
    h["wv"], h["bv"] = a["L0_attn_Wv"].T, a["L0_attn_bv"].reshape(1, D)
    h["wo16"] = head_rows(a["L0_attn_Wo"].T)
    h["bo"] = cols(a["L0_attn_bo"])
    h["rtok"] = np.stack([a["L0_ffn_q_routing_token"], a["L0_ffn_kv_routing_token"]], 1)
    wkv = a["L0_ffn_wkv_light"]
    h["light_wq"], h["light_wk"], h["light_wv"] = a["L0_ffn_wq_light"], wkv[:, :HID], wkv[:, HID:]
    h["light_wo"], h["light_gam"] = a["L0_ffn_wo_light"], cols(a["L0_ffn_gamma_light"])
    kv = a["L0_ffn_wkv_heavy"].reshape(HEADS, 2, DH, D)
    h["heavy_wq"], h["heavy_wo"] = a["L0_ffn_wq_heavy"], a["L0_ffn_wo_heavy"]
    h["heavy_wk"], h["heavy_wv"] = kv[:, 0].reshape(HID, D).T, kv[:, 1].reshape(HID, D).T
    h["heavy_gam"] = cols(a["L0_ffn_gamma_heavy"])
    for n in ("Wv", "Wr", "Wo"):
        h["mix_" + n + "T"] = a["L1_attn_" + n].T
    h["mix_vec"] = np.stack([cols(a["L1_attn_" + n]) for n in ("time_decay", "time_mix_v", "time_mix_r")], 1)
    for l in range(2):
        w = a["L1_ffn_wqkv"][l]
        for n, x in enumerate("qkv"):
            h[f"local{l}_w{x}"] = w[:, n * HID:(n + 1) * HID]
        h[f"local{l}_wo"] = a["L1_ffn_wo"][l]
        h[f"local{l}_gam"] = np.stack([np.concatenate([a[f"L1_ffn_{x}_scale"][l]] * 2) for x in "qk"], 1)
        w1 = np.zeros((D, 2, FM * P), f32)
        w1[:, :, :FFN] = a["L1_ffn_w1"][l].reshape(D, 2, FFN)
        b1 = np.zeros((2, FM * P), f32)
        b1[:, :FFN] = a["L1_ffn_b1"][l].reshape(2, FFN)
        w2 = np.zeros((FM * P, D), f32)
        w2[:FFN] = a["L1_ffn_w2"][l]
        h[f"mlp{l}_w1"], h[f"mlp{l}_w2"] = w1, w2
        h[f"mlp{l}_vec"] = np.concatenate([cols(b1[0]), cols(b1[1]), cols(a["L1_ffn_b2"][l]), cols(a["L1_ffn_ln_g"][l]),
                                           cols(a["L1_ffn_ln_b"][l])], 1)
    h.update(constants())

    nc = _bacc.Bacc("TRN2", target_bir_lowering=False, num_devices=1)
    arrays, t = {}, {}
    for name, v in h.items():
        v = np.ascontiguousarray(v)
        arrays[f"in_{name}_dram"] = v
        t[name] = nc.dram_tensor(f"in_{name}_dram", v.shape, mybir.dt.from_np(v.dtype), kind="ExternalInput").ap()
    d = dict(t)
    for name in ("idb", "mqk", "mkq", "mask"):
        d[name] = t[name].bitcast(BF16)
    d["cT"], d["wmod"] = [t["cT0"], t["cT1"]], [t["wmod0"], t["wmod1"]]
    for grp_ in ("light", "heavy", "mix"):
        d[grp_] = {k[len(grp_) + 1:]: v for k, v in t.items() if k.startswith(grp_ + "_")}
    for grp_ in ("local", "mlp"):
        d[grp_] = [{k[len(grp_) + 2:]: v for k, v in t.items() if k.startswith(f"{grp_}{l}_")} for l in range(2)]
    out = nc.dram_tensor("out_0_dram", (D, B * T), F32, kind="ExternalOutput").ap()
    build(nc, d, out, STAGES)
    r = _run(nc, [arrays], core_ids=[0])
    return np.ascontiguousarray(r.results[0]["out_0_dram"].T).reshape(B, T, D)
```
